# Optimizing a Trainium2 kernel written in Bass

```python
import numpy as np
import jax
import jax.numpy as jnp

def _softmax(x, axis=-1):
    return jax.nn.softmax(x, axis=axis)

def _gelu(x):
    return jax.nn.gelu(x, approximate=True)

def _silu(x):
    return jax.nn.silu(x)

def _sigmoid(x):
    return jax.nn.sigmoid(x)

def _layernorm(x, axis=-1, eps=1e-05):
    m = jnp.mean(x, axis=axis, keepdims=True)
    v = jnp.var(x, axis=axis, keepdims=True)
    return (x - m) / jnp.sqrt(v + eps)

def _scatter_add(tgt, idx, src, axis=0):
    return tgt.at[idx].add(src)

def _segment_sum(src, seg, n):
    return jax.ops.segment_sum(src, seg, n)
kernel_name = 'mk_decoder_postln_d1_seqx_r8_43f6bc'

def setup_inputs(seed: int=0):
    np.random.seed(seed)
    _w = jnp.asarray

    def _rec_inputs():
        import jax
        import jax.numpy as jnp
        _rk = jax.random.key(seed)
        x = -0.0003929 + 0.9999 * jax.random.normal(jax.random.fold_in(_rk, 1), (8, 56, 256), jnp.float32)
        _lenS = 56 - jax.random.randint(jax.random.fold_in(_rk, 7), (8,), 0, max(1, 56 // 4) + 1, jnp.int32)
        _lenS2 = 1500 - jax.random.randint(jax.random.fold_in(_rk, 8), (8,), 0, max(1, 1500 // 4) + 1, jnp.int32)
        _ctx_2048P = jax.random.normal(jax.random.fold_in(_rk, 11), (8, 16, 256), jnp.float32)
        _ctx_2048c = jax.random.dirichlet(jax.random.fold_in(_rk, 511), 0.3 * jnp.ones((16,), jnp.float32), (8, 1500))
        _ctx_2048t = jnp.einsum('bsk,bkd->bsd', _ctx_2048c, _ctx_2048P)
        _ctx_2048t = _ctx_2048t * jax.lax.rsqrt(jnp.mean(jnp.square(_ctx_2048t)) + 1e-12) * 0.953939
        ctx_2048 = -1.39393e-06 + 0.999914 * (_ctx_2048t + 0.3 * jax.random.normal(jax.random.fold_in(_rk, 611), (8, 1500, 256), jnp.float32))
        itok_BxS_0_1023 = jax.random.randint(jax.random.fold_in(_rk, 12), (8, 56), 0, 128, jnp.int32)
        return (x, ctx_2048, itok_BxS_0_1023)
    x, ctx_2048, itok_BxS_0_1023 = _rec_inputs()

    def _L0_attn_setup():
        import jax, jax.numpy as jnp
        import numpy as np
        N_HEAD = 16
        N_EMBD = 256
        HEAD_DIM = N_EMBD // N_HEAD
        key = jax.random.key(seed)
        kx, kqkv, kp = jax.random.split(key, 3)
        B, S = (2, 256)
        x = jax.random.normal(kx, (B, S, N_EMBD), dtype=jnp.float32)
        scale = 1.0 / np.sqrt(N_EMBD)
        Wqkv = jax.random.uniform(kqkv, (3 * N_EMBD, N_EMBD), dtype=jnp.float32, minval=-scale, maxval=scale)
        Wproj = jax.random.uniform(kp, (N_EMBD, N_EMBD), dtype=jnp.float32, minval=-scale, maxval=scale)
        return {'x': x, 'Wqkv': Wqkv, 'Wproj': Wproj}
    _L0_attn_all = _L0_attn_setup()
    _L0_attn_in = {k: v for k, v in _L0_attn_all.items() if k in ('Wqkv', 'Wproj')}
    del _L0_attn_all

    def _L0_xattn_setup():
        import jax, jax.numpy as jnp
        import numpy as np
        B, Lq, Lk = (2, 512, 128)
        Q_DIM, KV_DIM = (256, 256)
        H, HD = (16, 128)
        KVC, QC, R = (64, 96, 64)
        LOOKBACK = 8
        NEG = -1e+30

        def _rope(x, L):
            half = x.shape[-1] // 2
            inv_freq = 1.0 / 10000.0 ** (jnp.arange(half, dtype=jnp.float32) / half)
            ang = jnp.arange(L, dtype=jnp.float32)[:, None] * inv_freq
            cos, sin = (jnp.cos(ang), jnp.sin(ang))
            x1, x2 = (x[..., :half], x[..., half:])
            return jnp.concatenate([x1 * cos - x2 * sin, x1 * sin + x2 * cos], axis=-1)
        key = jax.random.key(seed)
        ks = jax.random.split(key, 11)

        def w(k, shape, fan_in):
            return jax.random.normal(k, shape, jnp.float32) / np.sqrt(fan_in).astype(np.float32)
        return {'q': jax.random.normal(ks[0], (B, Lq, Q_DIM), jnp.float32), 'kv': jax.random.normal(ks[1], (B, Lk, KV_DIM), jnp.float32), 'seg_id': jnp.sort(jax.random.randint(ks[2], (B, Lq), 0, Lk), axis=-1), 'W_kvc': w(ks[3], (KV_DIM, KVC), KV_DIM), 'W_dq': w(ks[4], (Q_DIM, QC), Q_DIM), 'W_uq': w(ks[5], (QC, H * HD), QC), 'W_qr': w(ks[6], (QC, H * R), QC), 'W_uk': w(ks[7], (KVC, H * HD), KVC), 'W_kr': w(ks[8], (KVC, R), KVC), 'W_uv': w(ks[9], (KVC, H * HD), KVC), 'W_o': w(ks[10], (H * HD, Q_DIM), H * HD)}
    _L0_xattn_all = _L0_xattn_setup()
    _L0_xattn_in = {k: v for k, v in _L0_xattn_all.items() if k in ('W_kvc', 'W_dq', 'W_uq', 'W_qr', 'W_uk', 'W_kr', 'W_uv', 'W_o')}
    del _L0_xattn_all

    def _L0_ffn_setup():
        import jax, jax.numpy as jnp
        import numpy as np
        EPS = 1e-08

        def _rmsnorm(x, g):
            return g * (x * jax.lax.rsqrt(jnp.mean(x * x, axis=-1, keepdims=True) + EPS))

        def _act_quant(x):
            scale = 127.0 / jnp.clip(jnp.max(jnp.abs(x), axis=-1, keepdims=True), 0.0001, None)
            y = jnp.clip(jnp.round(x * scale), -128, 127) / scale
            return x + jax.lax.stop_gradient(y - x)

        def _ternary_quant(w):
            s = jnp.mean(jnp.abs(w))
            wq = jnp.round(jnp.tanh(w / (s + EPS))) * jnp.arctanh(s)
            return w + jax.lax.stop_gradient(wq - w)

        def _linear_bit(x, w, g):
            xq = _act_quant(_rmsnorm(x, g))
            wq = _ternary_quant(w)
            return jnp.einsum('bsd,od->bso', xq, wq)
        key = jax.random.key(seed)
        k = jax.random.split(key, 4)
        B, S, D, H = (4, 256, 256, 1024)
        std_up = float(np.sqrt(2.0 / (D + H)))
        std_dn = float(np.sqrt(2.0 / (H + D)))
        return {'x': jax.random.normal(k[0], (B, S, D), dtype=jnp.float32), 'w1': jax.random.normal(k[1], (H, D), dtype=jnp.float32) * std_up, 'g1': jnp.ones((D,), dtype=jnp.float32), 'w2': jax.random.normal(k[2], (H, D), dtype=jnp.float32) * std_up, 'g2': jnp.ones((D,), dtype=jnp.float32), 'w3': jax.random.normal(k[3], (D, H), dtype=jnp.float32) * std_dn, 'g3': jnp.ones((H,), dtype=jnp.float32)}
    _L0_ffn_all = _L0_ffn_setup()
    _L0_ffn_in = {k: v for k, v in _L0_ffn_all.items() if k in ('w1', 'g1', 'w2', 'g2', 'w3', 'g3')}
    del _L0_ffn_all
    return {'x': x, 'ctx_2048': ctx_2048, 'itok_BxS_0_1023': itok_BxS_0_1023, 'L0_attn_Wqkv': _L0_attn_in['Wqkv'], 'L0_attn_Wproj': _L0_attn_in['Wproj'], 'L0_xattn_W_kvc': _L0_xattn_in['W_kvc'], 'L0_xattn_W_dq': _L0_xattn_in['W_dq'], 'L0_xattn_W_uq': _L0_xattn_in['W_uq'], 'L0_xattn_W_qr': _L0_xattn_in['W_qr'], 'L0_xattn_W_uk': _L0_xattn_in['W_uk'], 'L0_xattn_W_kr': _L0_xattn_in['W_kr'], 'L0_xattn_W_uv': _L0_xattn_in['W_uv'], 'L0_xattn_W_o': _L0_xattn_in['W_o'], 'L0_ffn_w1': _L0_ffn_in['w1'], 'L0_ffn_g1': _L0_ffn_in['g1'], 'L0_ffn_w2': _L0_ffn_in['w2'], 'L0_ffn_g2': _L0_ffn_in['g2'], 'L0_ffn_w3': _L0_ffn_in['w3'], 'L0_ffn_g3': _L0_ffn_in['g3']}

def reference(x, ctx_2048, itok_BxS_0_1023, L0_attn_Wqkv, L0_attn_Wproj, L0_xattn_W_kvc, L0_xattn_W_dq, L0_xattn_W_uq, L0_xattn_W_qr, L0_xattn_W_uk, L0_xattn_W_kr, L0_xattn_W_uv, L0_xattn_W_o, L0_ffn_w1, L0_ffn_g1, L0_ffn_w2, L0_ffn_g2, L0_ffn_w3, L0_ffn_g3):
    import jax
    import jax.numpy as jnp

    def _L0_attn_ref(x, Wqkv, Wproj):
        import jax, jax.numpy as jnp
        import numpy as np
        N_HEAD = 16
        N_EMBD = 256
        HEAD_DIM = N_EMBD // N_HEAD
        B, S, E = x.shape
        qkv = x @ Wqkv.T
        q, k, v = jnp.split(qkv, 3, axis=2)
        q = q.reshape(B, S, N_HEAD, HEAD_DIM).transpose(0, 2, 1, 3)
        k = k.reshape(B, S, N_HEAD, HEAD_DIM).transpose(0, 2, 1, 3)
        v = v.reshape(B, S, N_HEAD, HEAD_DIM).transpose(0, 2, 1, 3)
        scores = jnp.einsum('bhqd,bhkd->bhqk', q, k) / jnp.sqrt(jnp.float32(HEAD_DIM))
        causal = jnp.tril(jnp.ones((S, S), dtype=bool))
        scores = jnp.where(causal[None, None, :, :], scores, -jnp.inf)
        weights = jax.nn.softmax(scores, axis=-1)
        out = jnp.einsum('bhqk,bhkd->bhqd', weights, v)
        out = out.transpose(0, 2, 1, 3).reshape(B, S, E)
        return out @ Wproj.T

    def _L0_xattn_ref(q, kv, seg_id, W_kvc, W_dq, W_uq, W_qr, W_uk, W_kr, W_uv, W_o):
        import jax, jax.numpy as jnp
        import numpy as np
        B, Lq, Lk = (2, 512, 128)
        Q_DIM, KV_DIM = (256, 256)
        H, HD = (16, 128)
        KVC, QC, R = (64, 96, 64)
        LOOKBACK = 8
        NEG = -1e+30

        def _rope(x, L):
            half = x.shape[-1] // 2
            inv_freq = 1.0 / 10000.0 ** (jnp.arange(half, dtype=jnp.float32) / half)
            ang = jnp.arange(L, dtype=jnp.float32)[:, None] * inv_freq
            cos, sin = (jnp.cos(ang), jnp.sin(ang))
            x1, x2 = (x[..., :half], x[..., half:])
            return jnp.concatenate([x1 * cos - x2 * sin, x1 * sin + x2 * cos], axis=-1)
        b, lq, _ = q.shape
        lk = kv.shape[1]
        kv_c = kv @ W_kvc
        q_c = q @ W_dq
        q_nope = (q_c @ W_uq).reshape(b, lq, H, HD).transpose(0, 2, 1, 3)
        q_rope = (q_c @ W_qr).reshape(b, lq, H, R).transpose(0, 2, 1, 3)
        k_nope = (kv_c @ W_uk).reshape(b, lk, H, HD)
        v = (kv_c @ W_uv).reshape(b, lk, H, HD)
        k_rope = kv_c @ W_kr
        q_rope = _rope(q_rope, lq)
        k_rope = _rope(k_rope, lk)
        scale = 1.0 / np.sqrt(HD + R).astype(np.float32)
        scores = (jnp.einsum('bhqd,bkhd->bhqk', q_nope, k_nope) + jnp.einsum('bhqr,bkr->bhqk', q_rope, k_rope)) * scale
        k_ids = jnp.arange(lk)[None, None, :]
        qs = seg_id[:, :, None]
        good = (k_ids <= qs) & (k_ids >= qs - LOOKBACK)
        scores = jnp.where(good[:, None, :, :], scores, NEG)
        attn = jax.nn.softmax(scores, axis=-1)
        out = jnp.einsum('bhqk,bkhd->bqhd', attn, v).reshape(b, lq, H * HD)
        return out @ W_o

    def _L0_ffn_ref(x, w1, g1, w2, g2, w3, g3):
        import jax, jax.numpy as jnp
        import numpy as np
        EPS = 1e-08

        def _rmsnorm(x, g):
            return g * (x * jax.lax.rsqrt(jnp.mean(x * x, axis=-1, keepdims=True) + EPS))

        def _act_quant(x):
            scale = 127.0 / jnp.clip(jnp.max(jnp.abs(x), axis=-1, keepdims=True), 0.0001, None)
            y = jnp.clip(jnp.round(x * scale), -128, 127) / scale
            return x + jax.lax.stop_gradient(y - x)

        def _ternary_quant(w):
            s = jnp.mean(jnp.abs(w))
            wq = jnp.round(jnp.tanh(w / (s + EPS))) * jnp.arctanh(s)
            return w + jax.lax.stop_gradient(wq - w)

        def _linear_bit(x, w, g):
            xq = _act_quant(_rmsnorm(x, g))
            wq = _ternary_quant(w)
            return jnp.einsum('bsd,od->bso', xq, wq)
        swish = jax.nn.silu(_linear_bit(x, w1, g1))
        x_v = _linear_bit(x, w2, g2)
        h = swish * x_v
        return _linear_bit(h, w3, g3)
    x = _layernorm(x + _L0_attn_ref(x, L0_attn_Wqkv, L0_attn_Wproj), axis=-1)
    x = _layernorm(x + _L0_xattn_ref(x, ctx_2048, itok_BxS_0_1023, L0_xattn_W_kvc, L0_xattn_W_dq, L0_xattn_W_uq, L0_xattn_W_qr, L0_xattn_W_uk, L0_xattn_W_kr, L0_xattn_W_uv, L0_xattn_W_o), axis=-1)
    x = _layernorm(x + _L0_ffn_ref(x, L0_ffn_w1, L0_ffn_g1, L0_ffn_w2, L0_ffn_g2, L0_ffn_w3, L0_ffn_g3), axis=-1)
    return x

_drawn_inputs = setup_inputs


def setup_inputs(seed=0):
    import zlib

    import numpy as np

    out = dict(_drawn_inputs(seed))
    spreads = {'L0_ffn_g1': (1.0, 0.2), 'L0_ffn_g2': (1.0, 0.2), 'L0_ffn_g3': (1.0, 0.2)}
    factors = {}
    for name, (base, spread) in spreads.items():
        noise = np.random.default_rng([zlib.crc32(name.encode()), seed]).standard_normal(out[name].shape)
        drawn = base * np.exp(spread * noise) if base else spread * noise
        out[name] = jnp.asarray(drawn.astype(out[name].dtype))
    for name, factor in factors.items():
        out[name] = (out[name] * factor).astype(out[name].dtype)
    return out
```

```python
from contextlib import ExitStack

import numpy as np

import concourse.bass as bass
from concourse import mybir

ALU = mybir.AluOpType
ACT = mybir.ActivationFunctionType
AXX = mybir.AxisListType.X
F32 = mybir.dt.float32
BF16 = mybir.dt.bfloat16
I32 = mybir.dt.int32

P = 128
B, S, E = 8, 56, 256
N = B * S
EC = E // P
SP = 64
RT, R = 4, 2 * S
NH, HD = 16, 16
HH = NH // 2
NG = RT * 2
VW = 2 * HD + 2
XH, XD, XC, XQ, XR = 16, 128, 64, 96, 64
XP = XH // 2
LK, LOOKBACK = 1500, 8
WIN = 128
KT, NKT = 125, 12
F = 1024
NEG = -1e30
MAGIC = 12582912.0
LN_EPS, RMS_EPS = 1e-5, 1e-8

C_ID, C_QC, C_QS, C_KC, C_KS, C_IO, C_CB = 0, 128, 184, 240, 368, 496, 624
C_END = C_CB + S
HMASK = C_END
C_ALL = HMASK + HH


def constants():
    half = XR // 2
    inv = (1.0 / np.float32(10000.0) ** (np.arange(half, dtype=np.float32) / np.float32(half))).astype(np.float32)
    ang = np.arange(LK, dtype=np.float32)[:, None] * inv
    cos, sin = np.cos(ang).T, np.sin(ang).T
    kc = np.concatenate([np.ones((XC, LK)), cos, cos]).astype(np.float32)
    ks = np.concatenate([np.zeros((XC, LK)), -sin, sin]).astype(np.float32)
    scale = np.float32(1.0 / np.sqrt(XD + XR))
    c = np.zeros((P, C_ALL), np.float32)
    c[:, C_ID:C_ID + P] = np.eye(P)
    c[:, C_QC:C_QC + S] = kc[:, :S] * scale
    c[:, C_QS:C_QS + S] = np.concatenate([ks[XC:, :S], ks[XC:, :S]]) * scale
    c[:, C_KC:C_KC + WIN] = kc[:, :WIN]
    c[:, C_KS:C_KS + WIN] = ks[:, :WIN]
    c[:, C_IO:C_IO + WIN] = np.arange(WIN) + LOOKBACK / 2
    c[:S, C_CB:C_CB + S] = np.triu(np.full((S, S), NEG), 1)
    c[:, HMASK:HMASK + HH] = np.arange(P)[:, None] // HD == np.arange(HH)[None, :]
    io = np.broadcast_to(np.arange(LK, dtype=np.float32) + LOOKBACK / 2, (R, LK)).copy()
    return c, kc, ks, io


def decoder(nc, x, ctx_kv, seg, wqkv, wproj, w_kvc, w_dq, w_uq, w_qr, w_uk, w_kr, w_uv, w_o,
            w1, g1, w2, g2, w3, g3, const, kcos, ksin, kiota, out):
    with ExitStack() as stack:
        def sb(name, shape, dt=F32):
            return stack.enter_context(nc.sbuf_tensor(name, shape, dt))

        def sem(name):
            return stack.enter_context(nc.semaphore(name))

        bank = [stack.enter_context(nc.psum_tensor(f"bank{i}", [P, 512], F32)) for i in range(8)]

        cst = sb("cst", [P, C_ALL])
        ident = cst[:, C_ID:C_ID + P]
        identb = sb("identb", [P, P], BF16)
        identd = sb("identd", [S, R], BF16)
        causal = sb("causal", [SP, S], BF16)
        ones = sb("ones", [P, P])
        xn = sb("xn", [R, RT, E])
        def carve(block, sizes):
            at, pieces = 0, {}
            for name, cols in sizes:
                pieces[name] = block[:, at:at + cols]
                at += cols
            return pieces

        lower = sb("lower", [P, 13696])
        A = carve(lower, [("wqkv_n", 6 * E), ("wproj_n", EC * E), ("xt", EC * B * SP), ("wqkv_t", EC * 3 * E), ("wproj_t", EC * E),
                          ("qt", EC * B * SP), ("kt", EC * B * SP), ("vblk", B * HH * VW), ("srel", 2 * HH * S), ("prob", 2 * HH * SP),
                          ("probt", HH * P), ("attn", 2 * E), ("attnt", EC * N)])
        wqkv_n = A["wqkv_n"].rearrange("p (o e) -> p o e", e=E)
        wproj_n = A["wproj_n"].rearrange("p (o e) -> p o e", e=E)
        xt = A["xt"].rearrange("p (c b s) -> p c b s", c=EC, b=B)
        wqkv_t = A["wqkv_t"].rearrange("p (c o) -> p c o", c=EC)
        wproj_t = A["wproj_t"].rearrange("p (c o) -> p c o", c=EC)
        qt = A["qt"].rearrange("p (c b s) -> p c b s", c=EC, b=B)
        kt = A["kt"].rearrange("p (c b s) -> p c b s", c=EC, b=B)
        vblk = A["vblk"].rearrange("p (b h w) -> p b h w", b=B, h=HH)
        srel = A["srel"].rearrange("p (a h s) -> p a h s", a=2, h=HH)
        prob = A["prob"].rearrange("p (a h s) -> p a h s", a=2, h=HH)
        probt = A["probt"].rearrange("p (a h s) -> p a h s", a=2, h=HH // 2)
        attn = A["attn"].rearrange("p (a h d) -> p a h d", a=2, h=NH)
        attnt = A["attnt"].rearrange("p (c n) -> p c n", c=EC)
        C = carve(lower, [("wt", 8 * E), ("x1t", EC * N), ("qct", N), ("t2", 4 * N), ("xprob", 3 * 4 * WIN), ("xpt", 2 * 4 * R), ("ctxt", XP * N)])
        x1t = C["x1t"].rearrange("p (c n) -> p c n", c=EC)
        qct = C["qct"][0:XQ, :]
        t2 = C["t2"].rearrange("p (a b q s) -> p a b q s", a=2, b=B, q=2)
        xprob = C["xprob"][0:R, :].rearrange("p (a h k) -> p a h k", a=3, h=4)
        xpt = C["xpt"].rearrange("p (a h s) -> p a h s", a=2, h=4)
        ctxt = C["ctxt"].rearrange("p (h n) -> p h n", h=XP)
        big = sb("big", [P, 2 * B * HH * S])
        kblk = big[:, :].rearrange("p (c b h s) -> p c b h s", c=2, b=B, h=HH)
        qf = big[:, :].rearrange("p (h b q s) -> p h b q s", h=XP, b=B, q=2)
        smax = sb("smax", [P, 2, HH])
        orec = sb("orec", [P, HH, 2])
        res = sb("res", [R, 2, E])
        stats = sb("stats", [R, 6])
        mv = sb("mv", [R, 3, RT, 2])
        veps = sb("veps", [R, 3, RT])
        rstd = sb("rstd", [R, 3, RT])
        mhalf = sb("mhalf", [R, 1])
        x1 = sb("x1", [R, RT, E])
        x2 = xn
        stage = sb("stage", [P, XP * LK])
        wo_n = stage[:, 0:4096].rearrange("p (h e) -> p h e", h=XH)
        ukuv_n = stage[:, 4096:6144]
        uq_n = stage[0:XQ, 6144:8192]
        ukuv_t = stage[:, 8192:10240].rearrange("p (h k) -> p h k", h=XH)
        uq_t = stage[:, 10240:11776].rearrange("p (h k) -> p h k", h=XH)
        kv_n = sb("kv_n", [P, B, E])
        wn = [ukuv_n.rearrange("p (o e) -> p o e", e=E), stage[:, 6144:8192].rearrange("p (o e) -> p o e", e=E),
              kv_n[:, :, :].rearrange("p b e -> p (b e)").rearrange("p (o e) -> p o e", o=2)]
        wdq_n = sb("wdq_n", [P, EC, XQ])
        wqa = sb("wqa", [XQ, XH, P])
        wqs = sb("wqs", [XQ, XH, XR])
        wk1 = sb("wk1", [P, EC, P])
        wk2 = sb("wk2", [P, EC, P])
        wkr = sb("wkr", [XC, 2, XR])
        wkvct = sb("wkvct", [XC, E])
        wvo_b = sb("wvo", [P, XP * E])
        wvo = wvo_b[:, :].rearrange("p (h e) -> p h e", h=XP)
        segr = wvo_b[0:1, 0:N].bitcast(I32)
        segc = wvo_b[0:1, N:2 * N]
        kv_t = sb("kv_t", [P, EC, B, WIN])
        ka = sb("ka", [P, B, WIN])
        kb_b = sb("kb", [P, B * WIN])
        kb = kb_b[:, :].rearrange("p (b k) -> p b k", b=B)
        wqr_n = kb_b[0:XQ, :].rearrange("p (h r) -> p h r", h=XH)
        wtanh = kb_b[:, :].rearrange("p (a n) -> p a n", a=2)
        vx = sb("vx", [P, B, XC])
        segi = sb("segi", [R, B], I32)
        segf = sb("segf", [R, B])
        segm = sb("segm", [1, 1])
        flag = sb("flag", [1, 1], I32)
        g3_b = sb("g3_b", [R, F])
        g3b = g3_b[:, :]
        dist = g3_b[0:S, :].rearrange("p (b k) -> p b k", b=B)
        xmask = sb("xmask", [S, B, WIN], BF16)
        xmax = sb("xmax", [R, 3, 4])
        xsum = sb("xsum", [R, 3, 4])
        xrec = sb("xrec", [R, 3, 4])
        wt_b = C["wt"].bitcast(BF16)
        wt3 = sb("w3_t", [P, 8, E], BF16)
        wt = [wt_b[:, 0:2 * F].rearrange("p (c f) -> p c f", c=EC), wt_b[:, 2 * F:4 * F].rearrange("p (c f) -> p c f", c=EC), wt3[:, :, :]]
        wsum = sb("wsum", [P, 3])
        wtot = sb("wtot", [P, 3])
        wmean = sb("wmean", [P, 3])
        weps = sb("weps", [P, 3])
        winv = sb("winv", [P, 3])
        wone = sb("wone", [P, 2, 3])
        watan = sb("watan", [P, 3])
        wrnd = sb("wrnd", [P, 512])
        junk_w = wt3[:, :, :].rearrange("p k e -> p (k e)")
        g12 = sb("g12", [R, 2, E])
        FB = big[0:R, :]
        junk = FB[:, 0:1024]
        th = FB[:, 1024:2048].rearrange("p (a n) -> p a n", a=2)
        hg = FB[:, 2048:4096].rearrange("p (a n) -> p a n", a=2)
        hraw = FB[:, 4096:6144].rearrange("p (a n) -> p a n", a=2)
        D = carve(stage, [("xg", 2 * E), ("xq", 2 * E), ("xqt", 4 * R), ("hq", F), ("hqt", 4 * R), ("yout", 2 * E)])
        xg = D["xg"][0:R, :].rearrange("p (g e) -> p g e", g=2)
        xq = D["xq"][0:R, :].bitcast(BF16).rearrange("p (a g e) -> p a g e", a=2, g=2)
        xqt = D["xqt"].bitcast(BF16).rearrange("p (a g c s) -> p a g c s", a=2, g=2, c=EC)
        hq = D["hq"][0:R, :].bitcast(BF16).rearrange("p (a f) -> p a f", a=2)
        hqt = D["hqt"].bitcast(BF16).rearrange("p (k s) -> p k s", k=8)
        yout = D["yout"][0:R, :].rearrange("p (a e) -> p a e", a=2)
        fs = sb("fs", [R, RT, 28])

        s_cst, s_x, s_wqkv, s_wproj = sem("s_cst"), sem("s_x"), sem("s_wqkv"), sem("s_wproj")
        s_uq, s_ukuv, s_wqr, s_wo, s_wdq, s_wkv = (sem(n) for n in ("s_uq", "s_ukuv", "s_wqr", "s_wo", "s_wdq", "s_wkv"))
        s_kv, s_seg, s_w, s_g = sem("s_kv"), sem("s_seg"), [sem(f"s_w{i}") for i in range(3)], sem("s_g")
        s_idb, s_zero, s_ones, s_segf, s_mask, s_qr = (sem(n) for n in ("s_idb", "s_zero", "s_ones", "s_segf", "s_mask", "s_qr"))
        s_xtp, s_xt, s_wtp, s_wt, s_qkp, s_qk, s_kblk = (sem(n) for n in ("s_xtp", "s_xt", "s_wtp", "s_wt", "s_qkp", "s_qk", "s_kblk"))
        s_vp, s_v, s_sc, s_sub, s_exp, s_ptp, s_pt = (sem(n) for n in ("s_vp", "s_v", "s_sc", "s_sub", "s_exp", "s_ptp", "s_pt"))
        s_av, s_attn, s_atp, s_at, s_y, s_res, s_var, s_rstd, s_ln = (sem(n) for n in ("s_av", "s_attn", "s_atp", "s_at", "s_y", "s_res", "s_var", "s_rstd", "s_ln"))
        s_up, s_ue = sem("s_up"), sem("s_ue")
        s_wabs, s_winv, s_wrnd, s_watan, s_wln = (sem(n) for n in ("s_wabs", "s_winv", "s_wrnd", "s_watan", "s_wln"))
        s_krope = sem("s_krope")
        s_x1tp, s_x1t, s_qcp, s_qc = (sem(n) for n in ("s_x1tp", "s_x1t", "s_qcp", "s_qc"))
        s_bp, s_ap, s_bt, s_at2, s_qf = (sem(n) for n in ("s_bp", "s_ap", "s_bt", "s_at2", "s_qf"))
        s_flag = sem("s_flag")
        s_xs, s_xmax, s_xexp, s_xrec, s_xnorm, s_xptp, s_xpt, s_xop, s_xo = (sem(n) for n in ("s_xs", "s_xmax", "s_xexp", "s_xrec", "s_xnorm", "s_xptp", "s_xpt", "s_xop", "s_xo"))
        s_xy, s_xres = sem("s_xy"), sem("s_xres")
        s_sq, s_rr, s_xg, s_xq, s_xqp, s_xqt = (sem(n) for n in ("s_sq", "s_rr", "s_xg", "s_xq", "s_xqp", "s_xqt"))
        s_f, s_uv, s_th, s_h, s_hg, s_hsq, s_ms, s_rr3, s_hq, s_hqp, s_hqt, s_y3, s_r3, s_yo = (sem(n) for n in (
            "s_f", "s_uv", "s_th", "s_h", "s_hg", "s_hsq", "s_ms", "s_rr3", "s_hq", "s_hqp", "s_hqt", "s_y3", "s_r3", "s_yo"))
        s_out = [sem(f"s_out{i}") for i in range(2)]
        s_dve, s_pool, s_act = sem("s_dve"), sem("s_pool"), sem("s_act")
        g_q, g_kv, g_tab, g_ktp, g_kt, g_kp, g_k1, g_k2, g_k, g_sp, g_s, g_max, g_exp, g_rec, g_norm, g_pk, g_ptp, g_pt, g_op, g_acc, g_io, g_mask, g_out = (
            sem("g_" + n) for n in ("q", "kv", "tab", "ktp", "kt", "kp", "k1", "k2", "k", "sp", "s", "max", "exp", "rec",
                                    "norm", "pk", "ptp", "pt", "op", "acc", "io", "mask", "out"))

        g_sc = stage[0:R, 0:XP * LK].rearrange("p (h k) -> p h k", h=XP)
        g_qb = kv_t[:, 0, :, :].rearrange("p b k -> p (b k)")[:, 0:XH * S].rearrange("p (h r) -> p h r", h=XP)
        g_iota = C["t2"][0:R, 0:LK]
        g_msk = C["xprob"][0:R, 0:LK]
        g_kvn = kv_n[0:KT, 0, :]
        g_kvt = kv_n[:, 1, :].rearrange("p (c k) -> p c k", c=EC)[:, :, 0:KT]
        g_cos, g_sin = kv_n[:, 2, 0:KT], kv_n[:, 2, 128:128 + KT]
        g_key, g_key2 = kv_n[:, 3, 0:KT], kv_n[:, 3, 128:128 + KT]
        g_v = kv_n[0:KT, 4:7, :].rearrange("p a e -> p (a e)").rearrange("p (t c) -> p t c", c=XC)
        g_vk = kv_n[0:KT, 7, 0:XC]
        g_pk_b = kv_t[0:R, 1, :, :].rearrange("p b k -> p (b k)")[:, 0:XP * KT].rearrange("p (h k) -> p h k", h=XP)
        g_ptb = ka[0:KT, :, :].rearrange("p b k -> p (b k)")[:, 0:XP * R].rearrange("p (h k) -> p h k", h=XP)
        g_acc_b = kb[:, :, :].rearrange("p b k -> p (b k)")[:, 0:XP * S].rearrange("p (h k) -> p h k", h=XP)
        g_mx, g_sm, g_rc = fs[:, 0, 0:XP], fs[:, 1, 0:XP], fs[:, 2, 0:XP]

        block = stack.enter_context(nc.Block())

        @block.sync
        def _(sp):
            def load(dst, src, s, **kw):
                sp.dma_start(dst, src, **kw).then_inc(s, 16)

            load(xn[:, :, :], x.rearrange("(t p) e -> p t e", p=R), s_x)
            load(cst[:, :], const, s_cst)
            load(wqkv_n[:, :, :], wqkv.rearrange("(o p) e -> p o e", p=P), s_wqkv)
            load(wproj_n[:, :, :], wproj.rearrange("(o p) e -> p o e", p=P), s_wproj)
            load(uq_n, w_uq, s_uq)
            load(ukuv_n[0:XC, :], w_uk, s_ukuv)
            load(ukuv_n[XC:P, :], w_uv, s_ukuv)
            load(wqr_n[:, :, :], w_qr.rearrange("q (h r) -> q h r", h=XH), s_wqr)
            load(wk1[:, :, 0:XC], w_kvc.rearrange("(c p) k -> p c k", p=P), s_wkv)
            load(wkr[:, 0, :], w_kr, s_wkv)
            load(wkr[:, 1, 0:XR // 2], w_kr[:, XR // 2:XR], s_wkv)
            load(wkr[:, 1, XR // 2:XR], w_kr[:, 0:XR // 2], s_wkv)
            load(wdq_n[:, :, :], w_dq.rearrange("(c p) k -> p c k", p=P), s_wdq)
            load(segr[:, :], seg.rearrange("(o b) s -> o (b s)", o=1), s_seg)
            load(segi[0:S, :], seg.rearrange("b s -> s b"), s_seg, allow_slow_non_contiguous=True)
            load(segi[S:R, :], seg.rearrange("b s -> s b"), s_seg, allow_slow_non_contiguous=True)
            load(kv_n[:, :, :], ctx_kv[:, 0:WIN, :].rearrange("b k e -> k b e"), s_kv)
            load(wo_n, w_o.rearrange("(h d) e -> d h e", d=XD), s_wo)
            sp.wait_ge(s_ue, 8)
            load(wn[0][:, :, :], w1.rearrange("(o p) e -> p o e", p=P), s_w[0])
            load(wn[1][:, :, :], w2.rearrange("(o p) e -> p o e", p=P), s_w[1])
            sp.wait_ge(s_ue, 16)
            load(wn[2][:, :, :], w3.rearrange("(o p) e -> p o e", p=P), s_w[2])
            load(g12[:, 0, :], g1.rearrange("(o e) -> o e", o=1).broadcast_to([R, E]), s_g)
            load(g12[:, 1, :], g2.rearrange("(o e) -> o e", o=1).broadcast_to([R, E]), s_g)
            sp.wait_ge(s_mask, 1)
            load(g3b[:, :], g3.rearrange("(o e) -> o e", o=1).broadcast_to([R, F]), s_g)

            sp.wait_ge(s_flag, 1)
            outside = sp.value_load(flag[0:1, 0:1])
            with sp.If(outside > 0):
                sp.wait_ge(s_ue, UNITS)
                sp.wait_ge(s_qf, XP)
                sp.wait_ge(s_krope, 1)
                sp.dma_start(g_iota, kiota).then_inc(g_io, 16)
                with sp.Fori(0, B) as b:
                    with sp.Fori(0, NKT) as t:
                        it = b * NKT + t
                        sp.wait_ge(g_sp, it + 1)
                        sp.dma_start(g_kvn, ctx_kv[bass.ds(b, 1), bass.ds(t * KT, KT), :].rearrange("b k e -> (b k) e")).then_inc(g_kv, 16)
                        sp.dma_start(g_cos, kcos[:, bass.ds(t * KT, KT)]).then_inc(g_tab, 16)
                        sp.dma_start(g_sin, ksin[:, bass.ds(t * KT, KT)]).then_inc(g_tab, 16)
            for t in range(RT):
                sp.wait_ge(s_yo, t + 1)
                sp.dma_start(out[t * R:(t + 1) * R, :], yout[:, t % 2, :]).then_inc(s_out[t % 2], 16)
            for s in s_out:
                sp.wait_ge(s, 16 * RT // 2)

        @block.tensor
        def _(pe):
            mm = nc.tensor.matmul

            def turn(dst, src, eye):
                return nc.tensor.transpose(dst, src, eye)

            def turn4(dst, blocks, eye):
                for i, src in enumerate(blocks):
                    n = src.shape[0]
                    last = turn(dst[0:src.shape[1], i * n:(i + 1) * n], src, eye[0:n, 0:n])
                return last

            def unit(u):
                o = bank[4 + u % 2]
                if u < 2:
                    pe.wait_ge(s_v, 8)
                else:
                    pe.wait_ge(s_ue, u - 1)
                if u < 4:
                    if u == 0:
                        pe.wait_ge(s_uq, 16)
                    last = turn4(o, [uq_n[:, (4 * u + i) * XD:(4 * u + i + 1) * XD] for i in range(4)], ident)
                elif u < 8:
                    if u == 4:
                        pe.wait_ge(s_ukuv, 32)
                    last = turn4(o, [ukuv_n[:, (4 * (u - 4) + i) * XD:(4 * (u - 4) + i + 1) * XD] for i in range(4)], ident)
                elif u < 10:
                    if u == 8:
                        pe.wait_ge(s_ue, 8)
                    for i in range(8):
                        h = 8 * (u - 8) + i
                        last = mm(o[0:XQ, i * XC:(i + 1) * XC], uq_t[:, h, :], ukuv_t[:, h, 0:XC], start=True, stop=True)
                elif u == 10:
                    pe.wait_ge(s_wkv, 64)
                    for c in range(EC):
                        last = turn(o[0:XC, c * P:(c + 1) * P], wk1[:, c, 0:XC], ident)
                elif u == 11:
                    pe.wait_ge(s_ue, 11)
                    for c in range(EC):
                        last = mm(o[:, c * P:(c + 1) * P], wkvct[:, c * P:(c + 1) * P],
                                  wkr[:, :, :].rearrange("k a r -> k (a r)"), start=True, stop=True)
                elif u < 16:
                    if u == 12:
                        pe.wait_ge(s_kv, 16)
                    last = turn4(o, [kv_n[:, i % B, (i // B) * P:(i // B + 1) * P] for i in range(4 * (u - 12), 4 * (u - 12) + 4)], ident)
                elif u < 20:
                    if u == 16:
                        pe.wait_ge(s_ue, 16)
                        pe.wait_ge(s_zero, 1)
                    w, h = (wk1, wk2)[(u - 16) // 2], (u - 16) % 2
                    for c in range(EC):
                        last = mm(o[:, :], w[:, c, :], kv_t[:, c, 4 * h:4 * h + 4, :].rearrange("p b k -> p (b k)"), start=(c == 0), stop=(c == EC - 1))
                elif u == 20:
                    for b in range(B):
                        for c in range(EC):
                            last = mm(o[:, b * XC:(b + 1) * XC], kv_t[:, c, b, :], wk1[:, c, 0:XC], start=(c == 0), stop=(c == EC - 1))
                elif u < 25:
                    if u == 21:
                        pe.wait_ge(s_wo, 16)
                    for i in range(4):
                        h = 4 * (u - 21) + i
                        q, k = i % 2, i // 2
                        last = mm(o[q * XC:(q + 1) * XC, k * E:(k + 1) * E], ukuv_t[:, h, XC:P], wo_n[:, h, :], start=True, stop=True)
                elif u == 25:
                    pe.wait_ge(s_wabs, 3)
                    pe.wait_ge(s_ones, 1)
                    last = mm(o[:, 0:3], ones[:, :], wsum[:, :], start=True, stop=True)
                else:
                    j, k = (u - 26) // 4, (u - 26) % 4
                    if k == 0:
                        pe.wait_ge(s_w[j], 16)
                    if j < 2:
                        blocks = [wn[j][:, i % 8, (i // 8) * P:(i // 8 + 1) * P] for i in range(4 * k, 4 * k + 4)]
                    else:
                        blocks = [wn[j][:, i % 2, (i // 2) * P:(i // 2 + 1) * P] for i in range(4 * k, 4 * k + 4)]
                    last = turn4(o, blocks, ident)
                last.then_inc(s_up, 1)

            pe.wait_ge(s_cst, 16)
            pe.wait_ge(s_x, 16)
            for c in range(EC):
                for t in range(RT):
                    last = turn(bank[c][:, t * R:(t + 1) * R], xn[:, t, c * P:(c + 1) * P], ident[0:R, 0:R])
                last.then_inc(s_xtp, 1)
            pe.wait_ge(s_wqkv, 16)
            for k in range(3):
                turn4(bank[2 + k], [wqkv_n[:, i % 6, (i // 6) * P:(i // 6 + 1) * P] for i in range(4 * k, 4 * k + 4)], ident).then_inc(s_wtp, 1)
            pe.wait_ge(s_wproj, 16)
            turn4(bank[5], [wproj_n[:, i % 2, (i // 2) * P:(i // 2 + 1) * P] for i in range(4)], ident).then_inc(s_wtp, 1)
            pe.wait_ge(s_xt, 2)
            pe.wait_ge(s_wt, 3)
            for m in range(4):
                for c in range(EC):
                    last = mm(bank[(6, 7, 0, 1)[m]][:, :], wqkv_t[:, c, m * P:(m + 1) * P], xt[:, c, :, :].rearrange("p b s -> p (b s)"),
                              start=(c == 0), stop=(c == EC - 1))
                last.then_inc(s_qkp, 1)
            pe.wait_ge(s_wt, 4)
            for t in range(RT):
                for a in range(2):
                    for q in range(2):
                        for c in range(EC):
                            last = mm(bank[2 + t][q * SP:(q + 1) * SP, a * P:(a + 1) * P], xt[:, c, 2 * t + a, :],
                                      wqkv_t[:, c, 2 * E:3 * E].rearrange("p (h q d) -> p h q d", h=HH, q=2)[:, :, q, :], start=(c == 0), stop=(c == EC - 1))
                last.then_inc(s_vp, 1)

            def scores(g):
                t, hf = g // 2, g % 2
                o = bank[6 + g % 2]
                if g == 0:
                    pe.wait_ge(s_qk, 4)
                    pe.wait_ge(s_idb, 2)
                if g < 2:
                    pe.wait_ge(s_kblk, g + 1)
                else:
                    pe.wait_ge(s_sub, g - 1)
                for a in range(2):
                    rows = o[a * SP:(a + 1) * SP, 0:HH * S]
                    mm(rows, identb[0:SP, 0:SP], causal[:, :].unsqueeze(1).broadcast_to([SP, HH, S]), start=True, stop=False)
                    last = mm(rows, qt[:, hf, 2 * t + a, :], kblk[:, hf, 2 * t + a, :, :].rearrange("p h s -> p (h s)"), start=False, stop=True)
                last.then_inc(s_sc, 1)

            def prob_turn(g):
                pe.wait_ge(s_exp, g + 1)
                if g >= 2:
                    pe.wait_ge(s_pt, g - 1)
                turn4(bank[g % 2], [prob[:, g % 2, 2 * i:2 * i + 2, :].rearrange("p h s -> p (h s)") for i in range(4)], ident).then_inc(s_ptp, 1)

            def values(g):
                t, hf = g // 2, g % 2
                pe.wait_ge(s_pt, g + 1)
                if g == 0:
                    pe.wait_ge(s_v, 8)
                if hf == 0 and t >= 1:
                    pe.wait_ge(s_attn, t)
                for i in range(4):
                    for a in range(2):
                        last = mm(bank[2][a * SP:(a + 1) * SP, (4 * hf + i) * VW:(4 * hf + i + 1) * VW], probt[:, g % 2, i, a * SP:(a + 1) * SP],
                                  vblk[:, 2 * t + a, 4 * hf + i, :], start=True, stop=True)
                last.then_inc(s_av, 1)

            def attn_turn(t):
                pe.wait_ge(s_attn, t + 1)
                for c in range(EC):
                    last = turn(bank[3][:, c * P:(c + 1) * P], attn[:, t % 2, c * HH:(c + 1) * HH, :].rearrange("p h d -> p (h d)"), ident)
                last.then_inc(s_atp, 1)

            def project(t):
                pe.wait_ge(s_at, t + 1)
                if t >= 1:
                    pe.wait_ge(s_res, t)
                for c in range(EC):
                    last = mm(bank[3][0:R, E:2 * E], attnt[:, c, t * R:(t + 1) * R], wproj_t[:, c, :], start=(c == 0), stop=(c == EC - 1))
                last.then_inc(s_y, 1)

            scores(0)
            for g in range(NG):
                if g + 1 < NG:
                    scores(g + 1)
                for u in range(SPREAD[g], SPREAD[g + 1]):
                    unit(u)
                prob_turn(g)
                if g >= 3 and g % 2 == 1:
                    project((g - 3) // 2)
                values(g)
                if g >= 2 and g % 2 == 0:
                    attn_turn(g // 2 - 1)
            attn_turn(RT - 1)
            project(RT - 1)
            for u in range(SPREAD[NG], UNITS):
                unit(u)

            for t in range(RT):
                pe.wait_ge(s_ln, t + 1)
                for c in range(EC):
                    last = turn(bank[c][:, t * R:(t + 1) * R], x1[:, t, c * P:(c + 1) * P], ident[0:R, 0:R])
            last.then_inc(s_x1tp, 1)
            pe.wait_ge(s_x1t, 2)
            pe.wait_ge(s_wdq, 16)
            for c in range(EC):
                last = mm(bank[2][0:XQ, 0:N], wdq_n[:, c, :], x1t[:, c, :], start=(c == 0), stop=(c == EC - 1))
            last.then_inc(s_qcp, 1)
            pe.wait_ge(s_qc, 1)
            pe.wait_ge(s_qr, 2)
            for p in range(XP):
                if p >= 2:
                    pe.wait_ge(s_bt, p - 1)
                mm(bank[p % 2][:, 0:N], wqs[:, 2 * p:2 * p + 2, :].rearrange("q h r -> q (h r)"), qct[:, :], start=True, stop=True).then_inc(s_bp, 1)
                for h in (2 * p, 2 * p + 1):
                    if h >= 4:
                        pe.wait_ge(s_at2, h - 3)
                    mm(bank[(2, 3, 6, 7)[h % 4]][:, 0:N], wqa[:, h, :], qct[:, :], start=True, stop=True).then_inc(s_ap, 1)

            def context_out(t):
                pe.wait_ge(s_xo, 2 * t + 2)
                if t >= 1:
                    pe.wait_ge(s_xres, t)
                for p in range(XP):
                    last = mm(bank[7][0:R, 0:E], ctxt[:, p, t * R:(t + 1) * R], wvo[:, p, :], start=(p == 0), stop=(p == XP - 1))
                last.then_inc(s_xy, 1)

            pe.wait_ge(s_flag, 1)
            outside = pe.value_load(flag[0:1, 0:1])
            with pe.If(outside > 0):
                pe.wait_ge(s_at2, XH)
                pe.wait_ge(s_bt, XP)
                pe.wait_ge(s_ue, UNITS)
                with pe.Fori(0, B) as b:
                    with pe.Fori(0, NKT) as t:
                        it = b * NKT + t
                        pe.wait_ge(g_kv, 16 * it + 16)
                        for c in range(EC):
                            last = turn(bank[0][:, c * P:c * P + KT], g_kvn[:, c * P:(c + 1) * P], ident[0:KT, 0:KT])
                        last.then_inc(g_ktp, 1)
                        pe.wait_ge(g_kt, it + 1)
                        for k, w in enumerate((wk1, wk2)):
                            for c in range(EC):
                                mm(bank[1][:, k * P:k * P + KT], w[:, c, :], g_kvt[:, c, :], start=(c == 0), stop=(c == EC - 1))
                        for c in range(EC):
                            last = mm(bank[1][0:KT, 2 * P:2 * P + XC], g_kvt[:, c, :], wk1[:, c, 0:XC], start=(c == 0), stop=(c == EC - 1))
                        last.then_inc(g_kp, 1)
                        pe.wait_ge(g_k, it + 1)
                        pe.wait_ge(g_q, b + 1)
                        for p in range(XP):
                            last = mm(bank[2 + p // 4][0:R, (p % 4) * KT:(p % 4 + 1) * KT], g_qb[:, p, :],
                                      g_key, start=True, stop=True)
                        last.then_inc(g_s, 1)
                    with pe.Fori(0, NKT) as t:
                        it = b * NKT + t
                        pe.wait_ge(g_pk, it + 1)
                        for p in range(XP):
                            last = turn(bank[4 + p // 4][0:KT, (p % 4) * R:(p % 4 + 1) * R], g_pk_b[:, p, :], ident[0:R, 0:R])
                        last.then_inc(g_ptp, 1)
                        pe.wait_ge(g_pt, it + 1)
                        for a in range(2):
                            last = mm(bank[6][a * XC:(a + 1) * XC, 0:XP * S], g_vk, g_ptb[:, :, a * S:(a + 1) * S], start=True, stop=True)
                        last.then_inc(g_op, 1)
                for t in range(RT):
                    context_out(t)
            with pe.Else():
                def xscores(k):
                    b, hf = k // 2, k % 2
                    o = bank[4 + k % 3]
                    if k == 0:
                        pe.wait_ge(s_mask, 1)
                        pe.wait_ge(s_idb, 4)
                        pe.wait_ge(s_krope, 1)
                        pe.wait_ge(s_qf, XP)
                        pe.wait_ge(s_at2, XH)
                        pe.wait_ge(s_ue, UNITS)
                    if k >= 3:
                        pe.wait_ge(s_xexp, k - 2)
                    mm(o[0:R, :], identd[:, :], xmask[:, b, :].unsqueeze(1).broadcast_to([S, 4, WIN]), start=True, stop=False)
                    for i in range(4):
                        last = mm(o[0:R, i * WIN:(i + 1) * WIN], qf[:, 4 * hf + i, b, :, :].rearrange("p q s -> p (q s)"), ka[:, b, :], start=False, stop=(i == 3))
                    last.then_inc(s_xs, 1)

                def xturn(k):
                    pe.wait_ge(s_xnorm, k + 1)
                    if k >= 2:
                        pe.wait_ge(s_xpt, k - 1)
                    for i in range(4):
                        last = turn(bank[k % 2][:, i * R:(i + 1) * R], xprob[:, k % 3, i, :], ident[0:R, 0:R])
                    last.then_inc(s_xptp, 1)

                def xvalues(k):
                    b, hf = k // 2, k % 2
                    pe.wait_ge(s_xpt, k + 1)
                    if hf == 0 and b >= 2:
                        pe.wait_ge(s_xo, b - 1)
                    for a in range(2):
                        last = mm(bank[2 + b % 2][a * XC:(a + 1) * XC, hf * 4 * S:(hf + 1) * 4 * S], vx[:, b, :], xpt[:, k % 2, :, a * S:(a + 1) * S], start=True, stop=True)
                    last.then_inc(s_xop, 1)

                KS = 2 * B
                for k in range(KS + 3):
                    if k < KS:
                        xscores(k)
                    if 2 <= k < KS + 2:
                        xturn(k - 2)
                    if k >= 3:
                        xvalues(k - 3)
                    if k >= 7 and (k - 7) % 4 == 0:
                        context_out((k - 7) // 4)
                context_out(RT - 1)

            def turn_x(t):
                pe.wait_ge(s_xq, t + 1)
                if t == 0:
                    pe.wait_ge(s_wrnd, 24)
                else:
                    pe.wait_ge(s_xqt, t)
                ob = bank[0][:, :].bitcast(BF16)
                for g in range(2):
                    for c in range(EC):
                        i = g * EC + c
                        last = turn(ob[:, i * R:(i + 1) * R], xq[:, t % 2, g, c * P:(c + 1) * P], identb[0:R, 0:R])
                last.then_inc(s_xqp, 1)

            def up(t, hf):
                k = 2 * t + hf
                if hf == 0:
                    pe.wait_ge(s_xqt, t + 1)
                if k >= 2:
                    pe.wait_ge(s_h, k - 1)
                for g in range(2):
                    for c in range(EC):
                        last = mm(bank[1 + 2 * g + k % 2][0:R, :], xqt[:, t % 2, g, c, :], wt[g][:, c, hf * 512:(hf + 1) * 512], start=(c == 0), stop=(c == EC - 1))
                last.then_inc(s_uv, 1)

            def turn_h(t):
                pe.wait_ge(s_hq, t + 1)
                if t >= 1:
                    pe.wait_ge(s_hqt, t)
                ob = bank[5][:, :].bitcast(BF16)
                for k in range(8):
                    last = turn(ob[:, k * R:(k + 1) * R], hq[:, t % 2, k * P:(k + 1) * P], identb[0:R, 0:R])
                last.then_inc(s_hqp, 1)

            def down(t):
                pe.wait_ge(s_hqt, t + 1)
                if t >= 2:
                    pe.wait_ge(s_r3, t - 1)
                for k in range(8):
                    last = mm(bank[6 + t % 2][0:R, 0:E], hqt[:, k, :], wt[2][:, k, :], start=(k == 0), stop=(k == 7))
                last.then_inc(s_y3, 1)

            for t in range(RT + 1):
                if t < RT:
                    turn_x(t)
                    up(t, 0)
                    up(t, 1)
                if t >= 1:
                    turn_h(t - 1)
                    down(t - 1)

        @block.scalar
        def _(act):
            def copy(dst, src, scale=1.0):
                return nc.scalar.activation(dst, src, ACT.Copy, scale=scale)

            def unit(u):
                o = bank[4 + u % 2]
                if u == 25:
                    for j in range(3):
                        act.wait_ge(s_w[j], 16)
                        if j:
                            act.wait_ge(s_wabs, j)
                        nc.scalar.activation(junk_w, wn[j][:, :, :].rearrange("p a b -> p (a b)"), ACT.Abs, accum_out=wsum[:, j:j + 1]).then_inc(s_wabs, 1)
                act.wait_ge(s_up, u + 1)
                if u < 4:
                    last = copy(uq_t[:, 4 * u:4 * u + 4, :].rearrange("p h k -> p (h k)"), o[:, 0:4 * XQ])
                elif u < 8:
                    last = copy(ukuv_t[:, 4 * (u - 4):4 * (u - 4) + 4, :].rearrange("p h k -> p (h k)"), o[:, :])
                elif u < 10:
                    last = copy(wqa[:, 8 * (u - 8):8 * (u - 8) + 8, 0:XC], o[0:XQ, :].rearrange("p (h k) -> p h k", h=8))
                elif u == 10:
                    last = copy(wkvct[:, :], o[0:XC, 0:E])
                elif u == 11:
                    ob = o[:, 0:E].rearrange("p (c k) -> p c k", c=EC)
                    copy(wk1[:, :, XC:P], ob[:, :, 0:XR])
                    last = copy(wk2[:, :, XC:P], ob[:, :, XR:2 * XR])
                elif u < 16:
                    last = copy(kv_t[:, :, :, :].rearrange("p c b k -> p (c b k)")[:, 512 * (u - 12):512 * (u - 11)], o[:, :])
                elif u < 20:
                    if u == 18:
                        act.wait_ge(s_qr, 2)
                    d, h = (ka, kb)[(u - 16) // 2], (u - 16) % 2
                    last = copy(d[:, 4 * h:4 * h + 4, :].rearrange("p b k -> p (b k)"), o[:, :])
                elif u == 20:
                    last = copy(vx[:, :, :].rearrange("p b k -> p (b k)"), o[:, :])
                elif u < 25:
                    act.wait_ge(s_flag, 1)
                    last = copy(wvo[:, 2 * (u - 21):2 * (u - 21) + 2, :].rearrange("p h e -> p (h e)"), o[:, :])
                elif u == 25:
                    last = copy(wtot[:, :], o[:, 0:3])
                else:
                    v = u - 26
                    if v == 0:
                        act.wait_ge(s_krope, 1)
                        act.wait_ge(s_winv, 1)
                    if v >= 2:
                        act.wait_ge(s_wrnd, 2 * v - 2)
                    last = nc.scalar.activation(wtanh[:, v % 2, :], o[:, :], ACT.Tanh, scale=winv[:, v // 4:v // 4 + 1])
                last.then_inc(s_ue, 1)

            for k in range(3):
                act.wait_ge(s_wtp, k + 1)
                copy(wqkv_t[:, :, :].rearrange("p c o -> p (c o)")[:, 512 * k:512 * (k + 1)], bank[2 + k][:, :]).then_inc(s_wt, 1)
            act.wait_ge(s_wtp, 4)
            copy(wproj_t[:, :, :].rearrange("p c o -> p (c o)"), bank[5][:, :]).then_inc(s_wt, 1)
            for m in range(4):
                act.wait_ge(s_qkp, m + 1)
                d = (qt, kt)[m // 2][:, m % 2, :, :].rearrange("p b s -> p (b s)")
                copy(d, bank[(6, 7, 0, 1)[m]][:, :], HD ** -0.5 if m < 2 else 1.0).then_inc(s_qk, 1)
            act.wait_ge(s_zero, 2)
            for t in range(RT):
                act.wait_ge(s_vp, t + 1)
                for q in range(2):
                    src = bank[2 + t][q * SP:q * SP + S, 0:2 * P].rearrange("p (b h d) -> p b h d", b=2, h=HH)
                    copy(vblk[q * SP:q * SP + S, 2 * t:2 * t + 2, :, q * HD:(q + 1) * HD], src).then_inc(s_v, 1)

            for g in range(NG):
                act.wait_ge(s_sub, g + 1)
                if g >= 2:
                    act.wait_ge(s_ptp, g - 1)
                nc.scalar.activation(prob[:, g % 2, :, 0:S], srel[:, g % 2, :, :], ACT.Exp).then_inc(s_exp, 1)
                for u in range(SPREAD[g], SPREAD[g + 1]):
                    unit(u)
            for u in range(SPREAD[NG], UNITS):
                unit(u)
            act.wait_ge(s_wln, 1)
            nc.scalar.activation(wone[:, 0, :], wone[:, 1, :], ACT.Ln).then_inc(s_watan, 1)

            act.wait_ge(s_x1tp, 1)
            copy(x1t[:, 0, :], bank[0][:, 0:N]).then_inc(s_x1t, 1)
            act.wait_ge(s_qcp, 1)
            copy(qct[:, :], bank[2][0:XQ, 0:N]).then_inc(s_qc, 1)

            act.wait_ge(s_flag, 1)
            outside = act.value_load(flag[0:1, 0:1])
            with act.If(outside > 0):
                with act.Fori(0, B) as b:
                    with act.Fori(0, NKT) as t:
                        it = b * NKT + t
                        act.wait_ge(g_ktp, it + 1)
                        copy(g_kvt, bank[0][:, 0:E].rearrange("p (c k) -> p c k", c=EC)[:, :, 0:KT]).then_inc(g_kt, 1)
                    act.wait_ge(g_max, b + 1)
                    for p in range(XP):
                        last = nc.scalar.activation(g_sc[:, p, :], g_sc[:, p, :], ACT.Exp, bias=g_mx[:, p:p + 1], accum_out=g_sm[:, p:p + 1])
                    last.then_inc(g_exp, 1)
                    with act.Fori(0, NKT) as t:
                        it = b * NKT + t
                        act.wait_ge(g_ptp, it + 1)
                        for q in range(2):
                            last = copy(g_ptb[:, 4 * q:4 * q + 4, :].rearrange("p h k -> p (h k)"), bank[4 + q][0:KT, 0:4 * R])
                        last.then_inc(g_pt, 1)
            with act.Else():
                for k in range(2 * B + 4):
                    if k < 2 * B:
                        act.wait_ge(s_xmax, k + 1)
                        if k >= 3:
                            act.wait_ge(s_xptp, k - 2)
                        for i in range(4):
                            last = nc.scalar.activation(xprob[:, k % 3, i, :], bank[4 + k % 3][0:R, i * WIN:(i + 1) * WIN], ACT.Exp,
                                                        bias=xmax[:, k % 3, i:i + 1], accum_out=xsum[:, k % 3, i:i + 1])
                        last.then_inc(s_xexp, 1)
                    if k >= 5 and k % 2 == 1:
                        b = (k - 5) // 2
                        act.wait_ge(s_xop, 2 * b + 2)
                        copy(ctxt[:, :, b * S:(b + 1) * S], bank[2 + b % 2][:, 0:N].rearrange("p (h s) -> p h s", h=XP)).then_inc(s_xo, 1)

            def square_x(t):
                act.wait_ge(s_ln, RT + t + 1)
                if t >= 1:
                    act.wait_ge(s_sq, t)
                nc.scalar.activation(junk[:, 0:E], x2[:, t, :], ACT.Square, accum_out=fs[:, t, 0:1]).then_inc(s_sq, 1)

            def gate(k):
                act.wait_ge(s_uv, k + 1)
                act.wait_ge(s_f, k // 2 + 1)
                if k >= 2:
                    act.wait_ge(s_h, k - 1)
                nc.scalar.activation(th[:, k % 2, :], bank[1 + k % 2][0:R, :], ACT.Tanh, scale=fs[:, k // 2, 14:15]).then_inc(s_th, 1)

            def square_h(k):
                t, hf = k // 2, k % 2
                act.wait_ge(s_h, k + 1)
                if k:
                    act.wait_ge(s_hsq, k)
                nc.scalar.activation(junk[:, 512:1024], hraw[:, t % 2, hf * 512:(hf + 1) * 512], ACT.Square, accum_out=fs[:, t, 16 + hf:17 + hf]).then_inc(s_hsq, 1)

            def take_h(t):
                act.wait_ge(s_hqp, t + 1)
                if t >= 1:
                    act.wait_ge(s_y3, t)
                copy(hqt[:, :, :].rearrange("p k s -> p (k s)"), bank[5][:, :].bitcast(BF16)[:, 0:8 * R]).then_inc(s_hqt, 1)

            square_x(0)
            for t in range(RT + 1):
                if t + 1 < RT:
                    square_x(t + 1)
                if t < RT:
                    act.wait_ge(s_xqp, t + 1)
                    if t >= 2:
                        act.wait_ge(s_uv, 2 * (t - 1))
                    copy(xqt[:, t % 2, :, :, :].rearrange("p g c s -> p (g c s)"), bank[0][:, :].bitcast(BF16)[:, 0:4 * R]).then_inc(s_xqt, 1)
                    gate(2 * t)
                    gate(2 * t + 1)
                    square_h(2 * t)
                    square_h(2 * t + 1)
                if t >= 1:
                    take_h(t - 1)

        @block.vector
        def _(v):
            steps = [0]

            def link(ins):
                steps[0] += 1
                ins.then_inc(s_dve, 1)
                v.wait_ge(s_dve, steps[0])

            def turned_prob(g):
                v.wait_ge(s_ptp, g + 1)
                if g >= 2:
                    v.wait_ge(s_av, g - 1)
                nc.vector.tensor_copy(probt[:, g % 2, :, :].rearrange("p h k -> p (h k)"), bank[g % 2][:, :]).then_inc(s_pt, 1)

            def layernorm(n, t, r, dst, done):
                link(nc.vector.bn_stats(stats[:, :], r))
                link(nc.vector.bn_aggr(mv[:, n, t, :], stats[:, :]))
                nc.vector.tensor_scalar(veps[:, n, t:t + 1], mv[:, n, t, 1:2], LN_EPS, None, ALU.add).then_inc(s_var, 1)
                v.wait_ge(s_rstd, RT * n + t + 1)
                nc.vector.tensor_scalar(dst, r, mv[:, n, t, 0:1], rstd[:, n, t:t + 1], ALU.subtract, ALU.mult).then_inc(done, 1)

            v.wait_ge(s_zero, 3)
            for c in range(EC):
                v.wait_ge(s_xtp, c + 1)
                nc.vector.tensor_copy(xt[:, c, :, 0:S], bank[c][:, 0:N].rearrange("p (b s) -> p b s", b=B)).then_inc(s_xt, 1)
            for c in range(2):
                v.wait_ge(s_qk, 3 + c)
                for h in range(HH):
                    last = nc.vector.tensor_scalar(kblk[:, c, :, h, :], kt[:, c, :, 0:S], cst[:, HMASK + h:HMASK + h + 1], None, ALU.mult)
                last.then_inc(s_kblk, 1)

            def soft(g):
                v.wait_ge(s_sc, g + 1)
                s = bank[6 + g % 2][:, 0:HH * S].rearrange("p (h s) -> p h s", h=HH)
                link(nc.vector.tensor_reduce(smax[:, g % 2, :], s, AXX, ALU.max))
                if g >= 2:
                    v.wait_ge(s_exp, g - 1)
                nc.vector.tensor_tensor(srel[:, g % 2, :, :], s, smax[:, g % 2, :].unsqueeze(2).broadcast_to([P, HH, S]), ALU.subtract).then_inc(s_sub, 1)

            def normalise(t):
                v.wait_ge(s_av, 2 * t + 2)
                o = bank[2][:, 0:HH * VW].rearrange("p (h w) -> p h w", h=HH)
                link(nc.vector.reciprocal(orec[:, :, :], o[:, :, 2 * HD:VW]))
                if t >= 2:
                    v.wait_ge(s_atp, t - 1)
                nc.vector.tensor_tensor(attn[:, t % 2, :, :].rearrange("p (h q) d -> p h q d", q=2), o[:, :, 0:2 * HD].rearrange("p h (q d) -> p h q d", q=2),
                                        orec[:, :, :].unsqueeze(3).broadcast_to([P, HH, 2, HD]), ALU.mult).then_inc(s_attn, 1)

            def attn_turned(t):
                v.wait_ge(s_atp, t + 1)
                nc.vector.tensor_copy(attnt[:, :, t * R:(t + 1) * R].rearrange("p c (a s) -> p c a s", a=2),
                                      bank[3][:, 0:E].rearrange("p (c a s) -> p c a s", c=EC, a=2)[:, :, :, 0:S]).then_inc(s_at, 1)

            def add_norm1(t):
                v.wait_ge(s_y, t + 1)
                nc.vector.tensor_tensor(res[:, t % 2, :], bank[3][0:R, E:2 * E], xn[:, t, :], ALU.add).then_inc(s_res, 1)
                v.wait_ge(s_res, t + 1)
                layernorm(0, t, res[:, t % 2, :], x1[:, t, :], s_ln)

            soft(0)
            for g in range(NG):
                if g + 1 < NG:
                    soft(g + 1)
                turned_prob(g)
                if g >= 2 and g % 2 == 0:
                    normalise(g // 2 - 1)
                    attn_turned(g // 2 - 1)
                if g >= 3 and g % 2 == 1:
                    add_norm1((g - 3) // 2)
                if g == 2:
                    v.wait_ge(s_seg, 48)
                    link(nc.vector.tensor_scalar(segc[:, :], segr[:, :], -(WIN - 1) / 2.0, None, ALU.add))
                    link(nc.vector.tensor_tensor(segc[:, :], segc[:, :], segc[:, :], ALU.mult))
                    link(nc.vector.tensor_reduce(segm[:, :], segc[:, :], AXX, ALU.max))
                    nc.vector.tensor_scalar(flag[:, :], segm[:, :], (WIN / 2.0) ** 2 - WIN / 4.0, None, ALU.is_gt).then_inc(s_flag, 1)
            normalise(RT - 1)
            attn_turned(RT - 1)
            add_norm1(RT - 1)

            v.wait_ge(s_ue, 26)
            link(nc.vector.tensor_scalar(wmean[:, :], wtot[:, :], 1.0 / (F * E), None, ALU.mult))
            link(nc.vector.tensor_scalar(weps[:, :], wmean[:, :], RMS_EPS, None, ALU.add))
            nc.vector.reciprocal(winv[:, :], weps[:, :]).then_inc(s_winv, 1)
            link(nc.vector.tensor_scalar(wone[:, 0, :], wmean[:, :], -1.0, 1.0, ALU.mult, ALU.add))
            link(nc.vector.reciprocal(wone[:, 0, :], wone[:, 0, :]))
            link(nc.vector.tensor_scalar(wone[:, 1, :], wmean[:, :], 1.0, None, ALU.add))
            nc.vector.tensor_tensor(wone[:, 1, :], wone[:, 1, :], wone[:, 0, :], ALU.mult).then_inc(s_wln, 1)

            v.wait_ge(s_x1tp, 1)
            nc.vector.tensor_copy(x1t[:, 1, :], bank[1][:, 0:N]).then_inc(s_x1t, 1)

            qcos = cst[:, C_QC:C_QC + S].unsqueeze(1).broadcast_to([P, B, S])
            qsin = cst[:, C_QS:C_QS + S].unsqueeze(1).broadcast_to([P, B, S])
            for p in range(XP):
                v.wait_ge(s_bp, p + 1)
                if p >= 2:
                    v.wait_ge(s_qf, p - 1)
                for q in range(2):
                    rows = slice(q * XR, (q + 1) * XR)
                    last = nc.vector.tensor_tensor(t2[XR:P, p % 2, :, q, :],
                                                   bank[p % 2][rows, 0:N].rearrange("p (b s) -> p b s", b=B), qsin[rows, :, :], ALU.mult)
                last.then_inc(s_bt, 1)
                for h in (2 * p, 2 * p + 1):
                    v.wait_ge(s_ap, h + 1)
                    nc.vector.tensor_tensor(qf[:, p, :, h % 2, :],
                                            bank[(2, 3, 6, 7)[h % 4]][:, 0:N].rearrange("p (b s) -> p b s", b=B), qcos, ALU.mult).then_inc(s_at2, 1)

            def add_norm2(t):
                v.wait_ge(s_xy, t + 1)
                nc.vector.tensor_tensor(res[:, t % 2, :], bank[7][0:R, 0:E], x1[:, t, :], ALU.add).then_inc(s_xres, 1)
                v.wait_ge(s_xres, t + 1)
                layernorm(1, t, res[:, t % 2, :], x2[:, t, :], s_ln)

            outside_before = steps[0]
            outside = v.value_load(flag[0:1, 0:1])
            with v.If(outside > 0):
                v.wait_ge(g_io, 16)
                v.wait_ge(s_qf, XP)
                v.wait_ge(s_segf, 1)
                v.wait_ge(s_krope, 1)
                v.wait_ge(s_ue, UNITS)
                nc.vector.memset(g_acc_b, 0.0).then_inc(g_sp, 1)
                with v.Fori(0, B) as b:
                    nc.vector.tensor_copy(g_qb, big[:, :].rearrange("p (h n) -> p h n", h=XP)[:, :, bass.ds(b * R, R)]).then_inc(g_q, 1)
                    nc.vector.tensor_scalar(g_msk, g_iota, segf[:, bass.ds(b, 1)], None, ALU.subtract).then_inc(g_mask, 1)
                    v.wait_ge(g_mask, 3 * b + 1)
                    nc.vector.tensor_tensor(g_msk, g_msk, g_msk, ALU.mult).then_inc(g_mask, 1)
                    v.wait_ge(g_mask, 3 * b + 2)
                    nc.vector.tensor_scalar(g_msk, g_msk, LOOKBACK ** 2 / 4.0, NEG, ALU.is_gt, ALU.mult).then_inc(g_mask, 1)
                    with v.Fori(0, NKT) as t:
                        it = b * NKT + t
                        v.wait_ge(g_kp, it + 1)
                        v.wait_ge(g_tab, 32 * it + 32)
                        nc.vector.tensor_tensor(g_key, bank[1][:, 0:KT], g_cos, ALU.mult).then_inc(g_k1, 1)
                        nc.vector.tensor_tensor(g_key2, bank[1][:, P:P + KT], g_sin, ALU.mult).then_inc(g_k2, 1)
                        nc.vector.tensor_copy(g_v[:, bass.ds(t, 1), :], bank[1][0:KT, 2 * P:2 * P + XC].unsqueeze(1))
                        v.wait_ge(g_k1, it + 1)
                        v.wait_ge(g_k2, it + 1)
                        nc.vector.tensor_tensor(g_key, g_key, g_key2, ALU.add).then_inc(g_k, 1)
                        v.wait_ge(g_s, it + 1)
                        v.wait_ge(g_mask, 3 * b + 3)
                        for q in range(2):
                            last = nc.vector.tensor_tensor(g_sc[:, 4 * q:4 * q + 4, bass.ds(t * KT, KT)], bank[2 + q][0:R, 0:4 * KT].rearrange("p (h k) -> p h k", h=4),
                                                    g_msk[:, bass.ds(t * KT, KT)].unsqueeze(1).broadcast_to([R, 4, KT]), ALU.add)
                        last.then_inc(g_sp, 1)
                    v.wait_ge(g_sp, NKT * b + NKT + 1)
                    nc.vector.tensor_reduce(g_mx, g_sc, AXX, ALU.max, negate=True).then_inc(g_max, 1)
                    v.wait_ge(g_exp, b + 1)
                    nc.vector.reciprocal(g_rc, g_sm).then_inc(g_rec, 1)
                    v.wait_ge(g_rec, b + 1)
                    nc.vector.tensor_tensor(g_sc, g_sc, g_rc.unsqueeze(2).broadcast_to([R, XP, LK]), ALU.mult).then_inc(g_norm, 1)
                    v.wait_ge(g_norm, b + 1)
                    nc.vector.memset(g_acc_b, 0.0).then_inc(g_acc, 1)
                    with v.Fori(0, NKT) as t:
                        it = b * NKT + t
                        nc.vector.tensor_copy(g_vk, g_v[:, bass.ds(t, 1), :].rearrange("p a c -> p (a c)"))
                        nc.vector.tensor_copy(g_pk_b, g_sc[:, :, bass.ds(t * KT, KT)]).then_inc(g_pk, 1)
                        v.wait_ge(g_op, it + 1)
                        v.wait_ge(g_acc, it + b + 1)
                        nc.vector.tensor_tensor(g_acc_b, g_acc_b, bank[6][:, 0:N].rearrange("p (h s) -> p h s", h=XP), ALU.add).then_inc(g_acc, 1)
                    v.wait_ge(g_acc, (NKT + 1) * b + NKT + 1)
                    nc.vector.tensor_copy(ctxt[:, :, bass.ds(b * S, S)], g_acc_b).then_inc(s_xo, 1)
                for t in range(RT):
                    add_norm2(t)
            steps[0] = outside_before
            with v.Else():
                KS = 2 * B

                def xmaxima(k):
                    v.wait_ge(s_xs, k + 1)
                    if k >= 3:
                        v.wait_ge(s_xexp, k - 2)
                    nc.vector.tensor_reduce(xmax[:, k % 3, :], bank[4 + k % 3][0:R, :].rearrange("p (h k) -> p h k", h=4), AXX, ALU.max, negate=True).then_inc(s_xmax, 1)

                def xrecip(k):
                    v.wait_ge(s_xexp, k + 1)
                    if k >= 3:
                        v.wait_ge(s_xnorm, k - 2)
                    nc.vector.reciprocal(xrec[:, k % 3, :], xsum[:, k % 3, :]).then_inc(s_xrec, 1)

                def xturned(k):
                    v.wait_ge(s_xptp, k + 1)
                    if k >= 2:
                        v.wait_ge(s_xop, k - 1)
                    nc.vector.tensor_copy(xpt[:, k % 2, :, :].rearrange("p h k -> p (h k)"), bank[k % 2][:, 0:4 * R]).then_inc(s_xpt, 1)

                for k in range(KS + 3):
                    if k < KS:
                        xmaxima(k)
                    if 1 <= k < KS + 1:
                        xrecip(k - 1)
                    if 2 <= k < KS + 2:
                        xturned(k - 2)
                    if k >= 7 and (k - 7) % 4 == 0 and (k - 7) // 4 < RT - 1:
                        add_norm2((k - 7) // 4)
                add_norm2(RT - 1)

            v.wait_ge(s_watan, 1)
            link(nc.vector.tensor_scalar(watan[:, :], wone[:, 0, :], 0.5, None, ALU.mult))
            v.wait_ge(s_g, 48)

            def quant_x(t):
                f = fs[:, t, :]
                v.wait_ge(s_ln, RT + t + 1)
                if t >= 2:
                    v.wait_ge(s_xqp, t - 1)
                link(nc.vector.tensor_tensor(xg[:, :, :], x2[:, t, :].unsqueeze(1).broadcast_to([R, 2, E]), g12[:, :, :], ALU.mult))
                nc.vector.tensor_reduce(f[:, 2:4], xg[:, :, :], AXX, ALU.max, apply_absolute_value=True).then_inc(s_xg, 1)
                v.wait_ge(s_xg, t + 1)
                v.wait_ge(s_rr, t + 1)
                link(nc.vector.tensor_scalar(f[:, 4:6], f[:, 2:4], f[:, 1:2], 1e-4, ALU.mult, ALU.max))
                link(nc.vector.reciprocal(f[:, 6:8], f[:, 4:6]))
                link(nc.vector.tensor_scalar(f[:, 8:10], f[:, 6:8], f[:, 1:2], 127.0, ALU.mult, ALU.mult))
                for g in range(2):
                    last = nc.vector.tensor_scalar(xg[:, g, :], xg[:, g, :], f[:, 8 + g:9 + g], MAGIC, ALU.mult, ALU.add)
                link(last)
                nc.vector.tensor_scalar(xq[:, t % 2, :, :], xg[:, :, :], MAGIC, None, ALU.subtract).then_inc(s_xq, 1)
                v.wait_ge(s_xq, t + 1)
                link(nc.vector.scalar_tensor_tensor(f[:, 10:12], f[:, 4:6], 1.0 / 127.0, watan[0:R, 0:2], ALU.mult, ALU.mult))
                nc.vector.tensor_scalar(f[:, 14:15], f[:, 10:11], 0.5, None, ALU.mult).then_inc(s_f, 1)
                link(nc.vector.scalar_tensor_tensor(f[:, 15:16], f[:, 10:11], 0.5, f[:, 11:12], ALU.mult, ALU.mult))

            def hidden(k):
                t, hf = k // 2, k % 2
                v.wait_ge(s_th, k + 1)
                if t >= 2:
                    v.wait_ge(s_hg, 2 * (t - 1))
                    v.wait_ge(s_hsq, 2 * (t - 1))
                link(nc.vector.scalar_tensor_tensor(th[:, k % 2, :], th[:, k % 2, :], 1.0, bank[1 + k % 2][0:R, :], ALU.add, ALU.mult))
                nc.vector.tensor_tensor(hraw[:, t % 2, hf * 512:(hf + 1) * 512], th[:, k % 2, :], bank[3 + k % 2][0:R, :], ALU.mult).then_inc(s_h, 1)

            def quant_h(t):
                f = fs[:, t, :]
                v.wait_ge(s_hg, 2 * t + 2)
                link(nc.vector.tensor_reduce(f[:, 18:19], hg[:, t % 2, :], AXX, ALU.max, apply_absolute_value=True))
                v.wait_ge(s_hsq, 2 * t + 2)
                link(nc.vector.tensor_tensor(f[:, 19:20], f[:, 16:17], f[:, 17:18], ALU.add))
                link(nc.vector.tensor_tensor(f[:, 20:21], f[:, 15:16], f[:, 15:16], ALU.mult))
                link(nc.vector.scalar_tensor_tensor(f[:, 19:20], f[:, 19:20], 1.0 / F, f[:, 20:21], ALU.mult, ALU.mult))
                nc.vector.tensor_scalar(f[:, 21:22], f[:, 19:20], RMS_EPS, None, ALU.add).then_inc(s_ms, 1)
                v.wait_ge(s_rr3, t + 1)
                link(nc.vector.tensor_tensor(f[:, 23:24], f[:, 22:23], f[:, 15:16], ALU.mult))
                link(nc.vector.tensor_scalar(f[:, 24:25], f[:, 18:19], f[:, 23:24], 1e-4, ALU.mult, ALU.max))
                link(nc.vector.reciprocal(f[:, 25:26], f[:, 24:25]))
                link(nc.vector.tensor_scalar(f[:, 26:27], f[:, 25:26], f[:, 23:24], 127.0, ALU.mult, ALU.mult))
                link(nc.vector.scalar_tensor_tensor(f[:, 27:28], f[:, 24:25], 1.0 / 127.0, watan[0:R, 2:3], ALU.mult, ALU.mult))
                link(nc.vector.tensor_scalar(hg[:, t % 2, :], hg[:, t % 2, :], f[:, 26:27], MAGIC, ALU.mult, ALU.add))
                if t >= 2:
                    v.wait_ge(s_hqp, t - 1)
                nc.vector.tensor_scalar(hq[:, t % 2, :], hg[:, t % 2, :], MAGIC, None, ALU.subtract).then_inc(s_hq, 1)

            def add_norm3(t):
                v.wait_ge(s_y3, t + 1)
                nc.vector.scalar_tensor_tensor(res[:, t % 2, :], bank[6 + t % 2][0:R, 0:E], fs[:, t, 27:28], x2[:, t, :], ALU.mult, ALU.add).then_inc(s_r3, 1)
                v.wait_ge(s_r3, t + 1)
                if t >= 2:
                    v.wait_ge(s_out[t % 2], 16 * (t // 2))
                layernorm(2, t, res[:, t % 2, :], yout[:, t % 2, :], s_yo)

            quant_x(0)
            for t in range(RT):
                if t + 1 < RT:
                    quant_x(t + 1)
                hidden(2 * t)
                hidden(2 * t + 1)
                quant_h(t)
                if t >= 1:
                    add_norm3(t - 1)
            add_norm3(RT - 1)

        @block.gpsimd
        def _(g):
            g.memset(wk2[:, :, 0:XC], 0.0).then_inc(s_zero, 1)
            g.memset(vblk[:, :, :, :], 0.0).then_inc(s_pool, 1)
            g.wait_ge(s_pool, 1)
            g.memset(vblk[0:SP, :, :, 2 * HD:2 * HD + 1], 1.0).then_inc(s_pool, 1)
            g.memset(vblk[SP:P, :, :, 2 * HD + 1:VW], 1.0).then_inc(s_pool, 1)
            g.wait_ge(s_pool, 3)
            g.memset(prob[:, :, :, S:SP], 0.0).then_inc(s_zero, 1)
            g.memset(xt[:, :, :, :], 0.0).then_inc(s_zero, 1)
            g.memset(mhalf[:, :], -0.5).then_inc(s_pool, 1)
            g.memset(ones[:, :], 1.0).then_inc(s_ones, 1)
            g.wait_ge(s_cst, 16)
            g.tensor_copy(identb[:, :], ident).then_inc(s_idb, 1)
            g.tensor_copy(causal[:, :], cst[0:SP, C_CB:C_CB + S]).then_inc(s_idb, 1)
            g.tensor_copy(identd[:, 0:S], cst[0:S, 0:S]).then_inc(s_idb, 1)
            g.tensor_copy(identd[:, S:R], cst[0:S, 0:S]).then_inc(s_idb, 1)
            g.wait_ge(s_wqr, 16)
            g.tensor_copy(wqa[:, :, XC:P], wqr_n[:, :, :]).then_inc(s_qr, 1)
            g.tensor_copy(wqs[:, :, 0:XR // 2], wqr_n[:, :, XR // 2:XR])
            g.tensor_copy(wqs[:, :, XR // 2:XR], wqr_n[:, :, 0:XR // 2]).then_inc(s_qr, 1)
            g.wait_ge(s_seg, 48)
            g.tensor_copy(segf[:, :], segi[:, :]).then_inc(s_segf, 1)
            g.wait_ge(s_segf, 1)
            g.tensor_tensor(dist[:, :, :], cst[0:S, C_IO:C_IO + WIN].unsqueeze(1).broadcast_to([S, B, WIN]),
                            segf[0:S, :].unsqueeze(2).broadcast_to([S, B, WIN]), ALU.subtract).then_inc(s_pool, 1)
            g.wait_ge(s_pool, 5)
            g.tensor_tensor(dist[:, :, :], dist[:, :, :], dist[:, :, :], ALU.mult).then_inc(s_pool, 1)
            g.wait_ge(s_pool, 6)
            g.tensor_scalar(xmask[:, :, :], dist[:, :, :], LOOKBACK ** 2 / 4.0, NEG, ALU.is_gt, ALU.mult).then_inc(s_mask, 1)

            def root(n, t):
                g.wait_ge(s_var, RT * n + t + 1)
                g.tensor_tensor(rstd[:, n, t:t + 1], veps[:, n, t:t + 1], mhalf[:, :], ALU.pow).then_inc(s_rstd, 1)

            def round_w(v):
                g.wait_ge(s_ue, 27 + v)
                if v >= 1:
                    g.wait_ge(s_wrnd, 2 * v)
                g.tensor_scalar(wrnd[:, :], wtanh[:, v % 2, :], MAGIC, None, ALU.add).then_inc(s_wrnd, 1)
                g.wait_ge(s_wrnd, 2 * v + 1)
                j, k = v // 4, v % 4
                g.tensor_scalar(wt[j][:, :, :].rearrange("p a b -> p (a b)")[:, k * 512:(k + 1) * 512], wrnd[:, :], MAGIC, None, ALU.subtract).then_inc(s_wrnd, 1)

            g.wait_ge(s_ue, 20)
            kc = cst[:, C_KC:C_KC + WIN].unsqueeze(1).broadcast_to([P, B, WIN])
            ks = cst[:, C_KS:C_KS + WIN].unsqueeze(1).broadcast_to([P, B, WIN])
            g.tensor_tensor(ka[:, :, :], ka[:, :, :], kc, ALU.mult).then_inc(s_pool, 1)
            g.tensor_tensor(kb[:, :, :], kb[:, :, :], ks, ALU.mult).then_inc(s_pool, 1)
            g.wait_ge(s_pool, 8)
            g.tensor_tensor(ka[:, :, :], ka[:, :, :], kb[:, :, :], ALU.add).then_inc(s_krope, 1)
            for t in range(RT):
                root(0, t)
            for v in range(12):
                round_w(v)
            g.wait_ge(s_wrnd, 24)
            for p in range(XP):
                g.wait_ge(s_bt, p + 1)
                g.wait_ge(s_at2, 2 * p + 2)
                both = qf[XR:P, p, :, :, :].rearrange("p b q s -> p (b q s)")
                g.tensor_tensor(both, both, t2[XR:P, p % 2, :, :, :].rearrange("p b q s -> p (b q s)"), ALU.add).then_inc(s_qf, 1)

            g.wait_ge(s_qf, XP)
            g.wait_ge(s_flag, 1)
            outside = g.value_load(flag[0:1, 0:1])
            with g.If(outside > 0):
                for t in range(RT):
                    root(1, t)
            with g.Else():
                for k in range(2 * B):
                    g.wait_ge(s_xrec, k + 1)
                    g.tensor_tensor(xprob[:, k % 3, :, :], xprob[:, k % 3, :, :], xrec[:, k % 3, :].unsqueeze(2).broadcast_to([R, 4, WIN]), ALU.mult).then_inc(s_xnorm, 1)
                    if k >= 6 and (k - 6) % 4 == 0 and k < 2 * B:
                        root(1, (k - 6) // 4)
                root(1, RT - 1)

            def rms_x(t):
                f = fs[:, t, :]
                g.wait_ge(s_sq, t + 1)
                g.tensor_scalar(f[:, 12:13], f[:, 0:1], 1.0 / E, RMS_EPS, ALU.mult, ALU.add).then_inc(s_pool, 1)
                g.wait_ge(s_pool, 9 + t)
                g.tensor_tensor(f[:, 1:2], f[:, 12:13], mhalf[:, :], ALU.pow).then_inc(s_rr, 1)

            g.wait_ge(s_g, 48)
            rms_x(0)
            for t in range(RT):
                if t + 1 < RT:
                    rms_x(t + 1)
                for k in (2 * t, 2 * t + 1):
                    g.wait_ge(s_h, k + 1)
                    if t >= 2:
                        g.wait_ge(s_hq, t - 1)
                    cols = slice((k % 2) * 512, (k % 2 + 1) * 512)
                    g.tensor_tensor(hg[:, t % 2, cols], hraw[:, t % 2, cols], g3b[:, cols], ALU.mult).then_inc(s_hg, 1)
                g.wait_ge(s_ms, t + 1)
                g.tensor_tensor(fs[:, t, 22:23], fs[:, t, 21:22], mhalf[:, :], ALU.pow).then_inc(s_rr3, 1)
                if t >= 1:
                    root(2, t - 1)
            root(2, RT - 1)


UNITS = 38
SPREAD = [0, 5, 10, 15, 20, 24, 25, 25, 25]


def kernel(x, ctx_2048, itok_BxS_0_1023, L0_attn_Wqkv, L0_attn_Wproj, L0_xattn_W_kvc, L0_xattn_W_dq, L0_xattn_W_uq,
           L0_xattn_W_qr, L0_xattn_W_uk, L0_xattn_W_kr, L0_xattn_W_uv, L0_xattn_W_o, L0_ffn_w1, L0_ffn_g1, L0_ffn_w2,
           L0_ffn_g2, L0_ffn_w3, L0_ffn_g3):
    import concourse.bacc as bacc
    from concourse.bass_utils import run_bass_kernel_spmd

    nc = bacc.Bacc("TRN2", target_bir_lowering=False, num_devices=1)
    c, kc, ks, io = constants()
    named = {
        "x": np.ascontiguousarray(x).reshape(N, E), "ctx_kv": ctx_2048, "seg": itok_BxS_0_1023, "wqkv": L0_attn_Wqkv,
        "wproj": L0_attn_Wproj, "w_kvc": L0_xattn_W_kvc, "w_dq": L0_xattn_W_dq, "w_uq": L0_xattn_W_uq,
        "w_qr": L0_xattn_W_qr, "w_uk": L0_xattn_W_uk, "w_kr": L0_xattn_W_kr, "w_uv": L0_xattn_W_uv, "w_o": L0_xattn_W_o,
        "w1": L0_ffn_w1, "g1": L0_ffn_g1, "w2": L0_ffn_w2, "g2": L0_ffn_g2, "w3": L0_ffn_w3, "g3": L0_ffn_g3,
        "const": c, "kcos": kc, "ksin": ks, "kiota": io,
    }
    arrays, args = {}, []
    for name, a in named.items():
        a = np.ascontiguousarray(a)
        arrays[f"in_{name}"] = a
        args.append(nc.dram_tensor(f"in_{name}", a.shape, mybir.dt.from_np(a.dtype), kind="ExternalInput").ap())
    args.append(nc.dram_tensor("out_y", (N, E), F32, kind="ExternalOutput").ap())
    decoder(nc, *args)
    r = run_bass_kernel_spmd(nc, [arrays], core_ids=[0])
    return r.results[0]["out_y"].reshape(B, S, E)
```

```python
from contextlib import ExitStack

import numpy as np

import concourse.bass as bass
from concourse import mybir

ALU = mybir.AluOpType
ACT = mybir.ActivationFunctionType
AXX = mybir.AxisListType.X
F32 = mybir.dt.float32
BF16 = mybir.dt.bfloat16
I32 = mybir.dt.int32

P = 128
B, S, E = 8, 56, 256
N = B * S
EC = E // P
SP = 64
RT, R = 4, 2 * S
NH, HD = 16, 16
HH = NH // 2
NG = RT * 2
VW = 2 * HD + 2
XH, XD, XC, XQ, XR = 16, 128, 64, 96, 64
XP = XH // 2
LK, LOOKBACK = 1500, 8
WIN = 128
KT, NKT = 125, 12
F = 1024
NEG = -1e30
MAGIC = 12582912.0
LN_EPS, RMS_EPS = 1e-5, 1e-8

C_ID, C_QC, C_QS, C_KC, C_KS, C_IO, C_CB = 0, 128, 184, 240, 368, 496, 624
C_END = C_CB + S
HMASK = C_END
C_ALL = HMASK + HH


def constants():
    half = XR // 2
    inv = (1.0 / np.float32(10000.0) ** (np.arange(half, dtype=np.float32) / np.float32(half))).astype(np.float32)
    ang = np.arange(LK, dtype=np.float32)[:, None] * inv
    cos, sin = np.cos(ang).T, np.sin(ang).T
    kc = np.concatenate([np.ones((XC, LK)), cos, cos]).astype(np.float32)
    ks = np.concatenate([np.zeros((XC, LK)), -sin, sin]).astype(np.float32)
    scale = np.float32(1.0 / np.sqrt(XD + XR))
    c = np.zeros((P, C_ALL), np.float32)
    c[:, C_ID:C_ID + P] = np.eye(P)
    c[:, C_QC:C_QC + S] = kc[:, :S] * scale
    c[:, C_QS:C_QS + S] = np.concatenate([ks[XC:, :S], ks[XC:, :S]]) * scale
    c[:, C_KC:C_KC + WIN] = kc[:, :WIN]
    c[:, C_KS:C_KS + WIN] = ks[:, :WIN]
    c[:, C_IO:C_IO + WIN] = np.arange(WIN) + LOOKBACK / 2
    c[:S, C_CB:C_CB + S] = np.triu(np.full((S, S), NEG), 1)
    c[:, HMASK:HMASK + HH] = np.arange(P)[:, None] // HD == np.arange(HH)[None, :]
    io = np.broadcast_to(np.arange(LK, dtype=np.float32) + LOOKBACK / 2, (R, LK)).copy()
    return c, kc, ks, io


def decoder(nc, x, ctx_kv, seg, wqkv, wproj, w_kvc, w_dq, w_uq, w_qr, w_uk, w_kr, w_uv, w_o,
            w1, g1, w2, g2, w3, g3, const, kcos, ksin, kiota, out):
    with ExitStack() as stack:
        def sb(name, shape, dt=F32):
            return stack.enter_context(nc.sbuf_tensor(name, shape, dt))

        def sem(name):
            return stack.enter_context(nc.semaphore(name))

        bank = [stack.enter_context(nc.psum_tensor(f"bank{i}", [P, 512], F32)) for i in range(8)]

        cst = sb("cst", [P, C_ALL])
        ident = cst[:, C_ID:C_ID + P]
        identb = sb("identb", [P, P], BF16)
        identd = sb("identd", [S, R], BF16)
        causal = sb("causal", [SP, S], BF16)
        ones = sb("ones", [P, P])
        xn = sb("xn", [R, RT, E])
        def carve(block, sizes):
            at, pieces = 0, {}
            for name, cols in sizes:
                pieces[name] = block[:, at:at + cols]
                at += cols
            return pieces

        lower = sb("lower", [P, 13696])
        A = carve(lower, [("wqkv_n", 6 * E), ("wproj_n", EC * E), ("xt", EC * B * SP), ("wqkv_t", EC * 3 * E), ("wproj_t", EC * E),
                          ("qt", EC * B * SP), ("kt", EC * B * SP), ("vblk", B * HH * VW), ("srel", 2 * HH * S), ("prob", 2 * HH * SP),
                          ("probt", HH * P), ("attn", 2 * E), ("attnt", EC * N)])
        wqkv_n = A["wqkv_n"].rearrange("p (o e) -> p o e", e=E)
        wproj_n = A["wproj_n"].rearrange("p (o e) -> p o e", e=E)
        xt = A["xt"].rearrange("p (c b s) -> p c b s", c=EC, b=B)
        wqkv_t = A["wqkv_t"].rearrange("p (c o) -> p c o", c=EC)
        wproj_t = A["wproj_t"].rearrange("p (c o) -> p c o", c=EC)
        qt = A["qt"].rearrange("p (c b s) -> p c b s", c=EC, b=B)
        kt = A["kt"].rearrange("p (c b s) -> p c b s", c=EC, b=B)
        vblk = A["vblk"].rearrange("p (b h w) -> p b h w", b=B, h=HH)
        srel = A["srel"].rearrange("p (a h s) -> p a h s", a=2, h=HH)
        prob = A["prob"].rearrange("p (a h s) -> p a h s", a=2, h=HH)
        probt = A["probt"].rearrange("p (a h s) -> p a h s", a=2, h=HH // 2)
        attn = A["attn"].rearrange("p (a h d) -> p a h d", a=2, h=NH)
        attnt = A["attnt"].rearrange("p (c n) -> p c n", c=EC)
        C = carve(lower, [("wt", 8 * E), ("x1t", EC * N), ("qct", N), ("t2", 4 * N), ("xprob", 3 * 4 * WIN), ("xpt", 2 * 4 * R), ("ctxt", XP * N)])
        x1t = C["x1t"].rearrange("p (c n) -> p c n", c=EC)
        qct = C["qct"][0:XQ, :]
        t2 = C["t2"].rearrange("p (a b q s) -> p a b q s", a=2, b=B, q=2)
        xprob = C["xprob"][0:R, :].rearrange("p (a h k) -> p a h k", a=3, h=4)
        xpt = C["xpt"].rearrange("p (a h s) -> p a h s", a=2, h=4)
        ctxt = C["ctxt"].rearrange("p (h n) -> p h n", h=XP)
        big = sb("big", [P, 2 * B * HH * S])
        kblk = big[:, :].rearrange("p (c b h s) -> p c b h s", c=2, b=B, h=HH)
        qf = big[:, :].rearrange("p (h b q s) -> p h b q s", h=XP, b=B, q=2)
        smax = sb("smax", [P, 2, HH])
        orec = sb("orec", [P, HH, 2])
        res = sb("res", [R, 2, E])
        r3 = sb("r3", [R, 2, E])
        stats = sb("stats", [R, 6])
        mv = sb("mv", [R, 3, RT, 2])
        veps = sb("veps", [R, 3, RT])
        rstd = sb("rstd", [R, 3, RT])
        mhalf = sb("mhalf", [R, 1])
        x1 = sb("x1", [R, RT, E])
        x2 = xn
        stage = sb("stage", [P, XP * LK])
        wo_n = stage[:, 0:4096].rearrange("p (h e) -> p h e", h=XH)
        ukuv_n = stage[:, 4096:6144]
        uq_n = stage[0:XQ, 6144:8192]
        ukuv_t = stage[:, 8192:10240].rearrange("p (h k) -> p h k", h=XH)
        uq_t = stage[:, 10240:11776].rearrange("p (h k) -> p h k", h=XH)
        kv_n = sb("kv_n", [P, B, E])
        wn = [ukuv_n.rearrange("p (o e) -> p o e", e=E), stage[:, 6144:8192].rearrange("p (o e) -> p o e", e=E),
              kv_n[:, :, :].rearrange("p b e -> p (b e)").rearrange("p (o e) -> p o e", o=2)]
        wdq_n = sb("wdq_n", [P, EC, XQ])
        wqa = sb("wqa", [XQ, XH, P])
        wqs = sb("wqs", [XQ, XH, XR])
        wk1 = sb("wk1", [P, EC, P])
        wk2 = sb("wk2", [P, EC, P])
        wkr = sb("wkr", [XC, 2, XR])
        wkvct = sb("wkvct", [XC, E])
        wvo_b = sb("wvo", [P, XP * E])
        wvo = wvo_b[:, :].rearrange("p (h e) -> p h e", h=XP)
        segr = wvo_b[0:1, 0:N].bitcast(I32)
        segc = wvo_b[0:1, N:2 * N]
        kv_t = sb("kv_t", [P, EC, B, WIN])
        ka = sb("ka", [P, B, WIN])
        kb_b = sb("kb", [P, B * WIN])
        kb = kb_b[:, :].rearrange("p (b k) -> p b k", b=B)
        wqr_n = kb_b[0:XQ, :].rearrange("p (h r) -> p h r", h=XH)
        wtanh = kb_b[:, :].rearrange("p (a n) -> p a n", a=2)
        vx = sb("vx", [P, B, XC])
        segi = sb("segi", [R, B], I32)
        segf = sb("segf", [R, B])
        segm = sb("segm", [1, 1])
        flag = sb("flag", [1, 1], I32)
        g3_b = sb("g3_b", [R, F])
        g3b = g3_b[:, :]
        dist = g3_b[0:S, :].rearrange("p (b k) -> p b k", b=B)
        xmask = sb("xmask", [S, B, WIN], BF16)
        xmax = sb("xmax", [R, 3, 4])
        xsum = sb("xsum", [R, 3, 4])
        xrec = sb("xrec", [R, 3, 4])
        wt_b = C["wt"].bitcast(BF16)
        wt3 = sb("w3_t", [P, 8, E], BF16)
        wt = [wt_b[:, 0:2 * F].rearrange("p (c f) -> p c f", c=EC), wt_b[:, 2 * F:4 * F].rearrange("p (c f) -> p c f", c=EC), wt3[:, :, :]]
        wsum = sb("wsum", [P, 3])
        wtot = sb("wtot", [P, 3])
        wmean = sb("wmean", [P, 3])
        weps = sb("weps", [P, 3])
        winv = sb("winv", [P, 3])
        wone = sb("wone", [P, 2, 3])
        watan = sb("watan", [P, 3])
        junk_w = wt3[:, :, :].rearrange("p k e -> p (k e)")
        g12 = sb("g12", [R, 2, E])
        D = carve(stage, [("junk", F), ("th", F), ("hg", 2 * F), ("hraw", 2 * F),
                          ("xg", 2 * E), ("xq", 2 * E), ("xqt", 4 * R), ("hq", F), ("hqt", 4 * R), ("yout", 2 * E)])
        junk = D["junk"][0:R, :]
        th = D["th"][0:R, :].rearrange("p (a n) -> p a n", a=2)
        hg = D["hg"][0:R, :].rearrange("p (a n) -> p a n", a=2)
        hraw = D["hraw"][0:R, :].rearrange("p (a n) -> p a n", a=2)
        xg = D["xg"][0:R, :].rearrange("p (g e) -> p g e", g=2)
        xq = D["xq"][0:R, :].bitcast(BF16).rearrange("p (a g e) -> p a g e", a=2, g=2)
        xqt = D["xqt"].bitcast(BF16).rearrange("p (a g c s) -> p a g c s", a=2, g=2, c=EC)
        hq = D["hq"][0:R, :].bitcast(BF16).rearrange("p (a f) -> p a f", a=2)
        hqt = D["hqt"].bitcast(BF16).rearrange("p (k s) -> p k s", k=8)
        yout = D["yout"][0:R, :].rearrange("p (a e) -> p a e", a=2)
        fs = sb("fs", [R, RT, 28])

        s_cst, s_x, s_wqkv, s_wproj = sem("s_cst"), sem("s_x"), sem("s_wqkv"), sem("s_wproj")
        s_uq, s_ukuv, s_wqr, s_wo, s_wdq, s_wkv = (sem(n) for n in ("s_uq", "s_ukuv", "s_wqr", "s_wo", "s_wdq", "s_wkv"))
        s_kv, s_seg, s_w, s_g = sem("s_kv"), sem("s_seg"), [sem(f"s_w{i}") for i in range(3)], sem("s_g")
        s_idb, s_zero, s_ones, s_segf, s_mask, s_qr = (sem(n) for n in ("s_idb", "s_zero", "s_ones", "s_segf", "s_mask", "s_qr"))
        s_xtp, s_xt, s_wtp, s_wt, s_qkp, s_qk, s_kblk = (sem(n) for n in ("s_xtp", "s_xt", "s_wtp", "s_wt", "s_qkp", "s_qk", "s_kblk"))
        s_vp, s_v, s_sc, s_sub, s_exp, s_ptp, s_pt = (sem(n) for n in ("s_vp", "s_v", "s_sc", "s_sub", "s_exp", "s_ptp", "s_pt"))
        s_av, s_attn, s_atp, s_at, s_y, s_res, s_ln = (sem(n) for n in ("s_av", "s_attn", "s_atp", "s_at", "s_y", "s_res", "s_ln"))
        s_var, s_rstd = ([sem(f"{n}{i}") for i in range(3)] for n in ("s_var", "s_rstd"))
        s_up, s_ue = sem("s_up"), sem("s_ue")
        s_wabs, s_winv, s_wrnd, s_watan, s_wln = (sem(n) for n in ("s_wabs", "s_winv", "s_wrnd", "s_watan", "s_wln"))
        s_krope = sem("s_krope")
        s_x1tp, s_x1t, s_qcp, s_qc = (sem(n) for n in ("s_x1tp", "s_x1t", "s_qcp", "s_qc"))
        s_bp, s_ap, s_bt, s_at2, s_qf = (sem(n) for n in ("s_bp", "s_ap", "s_bt", "s_at2", "s_qf"))
        s_flag = sem("s_flag")
        s_xs, s_xmax, s_xexp, s_xrec, s_xnorm, s_xptp, s_xpt, s_xop, s_xo = (sem(n) for n in ("s_xs", "s_xmax", "s_xexp", "s_xrec", "s_xnorm", "s_xptp", "s_xpt", "s_xop", "s_xo"))
        s_xy, s_xres = sem("s_xy"), sem("s_xres")
        s_sq, s_rr, s_xg, s_xq, s_xqp, s_xqt = (sem(n) for n in ("s_sq", "s_rr", "s_xg", "s_xq", "s_xqp", "s_xqt"))
        s_f, s_uv, s_th, s_h, s_hg, s_hsq, s_ms, s_rr3, s_hq, s_hqp, s_hqt, s_y3, s_r3, s_yo = (sem(n) for n in (
            "s_f", "s_uv", "s_th", "s_h", "s_hg", "s_hsq", "s_ms", "s_rr3", "s_hq", "s_hqp", "s_hqt", "s_y3", "s_r3", "s_yo"))
        s_out = [sem(f"s_out{i}") for i in range(2)]
        s_dve, s_pool, s_act = sem("s_dve"), sem("s_pool"), sem("s_act")
        g_q, g_kv, g_tab, g_ktp, g_kt, g_kp, g_k1, g_k2, g_k, g_sp, g_s, g_max, g_exp, g_rec, g_norm, g_pk, g_ptp, g_pt, g_op, g_acc, g_io, g_mask, g_out = (
            sem("g_" + n) for n in ("q", "kv", "tab", "ktp", "kt", "kp", "k1", "k2", "k", "sp", "s", "max", "exp", "rec",
                                    "norm", "pk", "ptp", "pt", "op", "acc", "io", "mask", "out"))

        g_sc = stage[0:R, 0:XP * LK].rearrange("p (h k) -> p h k", h=XP)
        g_qb = kv_t[:, 0, :, :].rearrange("p b k -> p (b k)")[:, 0:XH * S].rearrange("p (h r) -> p h r", h=XP)
        g_iota = C["t2"][0:R, 0:LK]
        g_msk = C["xprob"][0:R, 0:LK]
        g_kvn = kv_n[0:KT, 0, :]
        g_kvt = kv_n[:, 1, :].rearrange("p (c k) -> p c k", c=EC)[:, :, 0:KT]
        g_cos, g_sin = kv_n[:, 2, 0:KT], kv_n[:, 2, 128:128 + KT]
        g_key, g_key2 = kv_n[:, 3, 0:KT], kv_n[:, 3, 128:128 + KT]
        g_v = kv_n[0:KT, 4:7, :].rearrange("p a e -> p (a e)").rearrange("p (t c) -> p t c", c=XC)
        g_vk = kv_n[0:KT, 7, 0:XC]
        g_pk_b = kv_t[0:R, 1, :, :].rearrange("p b k -> p (b k)")[:, 0:XP * KT].rearrange("p (h k) -> p h k", h=XP)
        g_ptb = ka[0:KT, :, :].rearrange("p b k -> p (b k)")[:, 0:XP * R].rearrange("p (h k) -> p h k", h=XP)
        g_acc_b = kb[:, :, :].rearrange("p b k -> p (b k)")[:, 0:XP * S].rearrange("p (h k) -> p h k", h=XP)
        g_mx, g_sm, g_rc = fs[:, 0, 0:XP], fs[:, 1, 0:XP], fs[:, 2, 0:XP]

        block = stack.enter_context(nc.Block())

        @block.sync
        def _(sp):
            def load(dst, src, s, **kw):
                sp.dma_start(dst, src, **kw).then_inc(s, 16)

            load(xn[:, :, :], x.rearrange("(t p) e -> p t e", p=R), s_x)
            load(cst[:, :], const, s_cst)
            load(wqkv_n[:, :, :], wqkv.rearrange("(o p) e -> p o e", p=P), s_wqkv)
            load(wproj_n[:, :, :], wproj.rearrange("(o p) e -> p o e", p=P), s_wproj)
            load(uq_n, w_uq, s_uq)
            load(ukuv_n[0:XC, :], w_uk, s_ukuv)
            load(ukuv_n[XC:P, :], w_uv, s_ukuv)
            load(wqr_n[:, :, :], w_qr.rearrange("q (h r) -> q h r", h=XH), s_wqr)
            load(wk1[:, :, 0:XC], w_kvc.rearrange("(c p) k -> p c k", p=P), s_wkv)
            load(wkr[:, 0, :], w_kr, s_wkv)
            load(wkr[:, 1, 0:XR // 2], w_kr[:, XR // 2:XR], s_wkv)
            load(wkr[:, 1, XR // 2:XR], w_kr[:, 0:XR // 2], s_wkv)
            load(wdq_n[:, :, :], w_dq.rearrange("(c p) k -> p c k", p=P), s_wdq)
            load(segr[:, :], seg.rearrange("(o b) s -> o (b s)", o=1), s_seg)
            load(segi[0:S, :], seg.rearrange("b s -> s b"), s_seg, allow_slow_non_contiguous=True)
            load(segi[S:R, :], seg.rearrange("b s -> s b"), s_seg, allow_slow_non_contiguous=True)
            load(kv_n[:, :, :], ctx_kv[:, 0:WIN, :].rearrange("b k e -> k b e"), s_kv)
            load(wo_n, w_o.rearrange("(h d) e -> d h e", d=XD), s_wo)
            sp.wait_ge(s_ue, 8)
            load(wn[0][:, :, :], w1.rearrange("(o p) e -> p o e", p=P), s_w[0])
            load(wn[1][:, :, :], w2.rearrange("(o p) e -> p o e", p=P), s_w[1])
            sp.wait_ge(s_ue, 16)
            load(wn[2][:, :, :], w3.rearrange("(o p) e -> p o e", p=P), s_w[2])
            load(g12[:, 0, :], g1.rearrange("(o e) -> o e", o=1).broadcast_to([R, E]), s_g)
            load(g12[:, 1, :], g2.rearrange("(o e) -> o e", o=1).broadcast_to([R, E]), s_g)
            sp.wait_ge(s_mask, 1)
            load(g3b[:, :], g3.rearrange("(o e) -> o e", o=1).broadcast_to([R, F]), s_g)

            sp.wait_ge(s_flag, 1)
            outside = sp.value_load(flag[0:1, 0:1])
            with sp.If(outside > 0):
                sp.wait_ge(s_ue, UNITS)
                sp.wait_ge(s_qf, XP)
                sp.wait_ge(s_krope, 1)
                sp.dma_start(g_iota, kiota).then_inc(g_io, 16)
                with sp.Fori(0, B) as b:
                    with sp.Fori(0, NKT) as t:
                        it = b * NKT + t
                        sp.wait_ge(g_sp, it + 1)
                        sp.dma_start(g_kvn, ctx_kv[bass.ds(b, 1), bass.ds(t * KT, KT), :].rearrange("b k e -> (b k) e")).then_inc(g_kv, 16)
                        sp.dma_start(g_cos, kcos[:, bass.ds(t * KT, KT)]).then_inc(g_tab, 16)
                        sp.dma_start(g_sin, ksin[:, bass.ds(t * KT, KT)]).then_inc(g_tab, 16)
            for t in range(RT):
                sp.wait_ge(s_yo, t + 1)
                sp.dma_start(out[t * R:(t + 1) * R, :], yout[:, t % 2, :]).then_inc(s_out[t % 2], 16)
            for s in s_out:
                sp.wait_ge(s, 16 * RT // 2)

        @block.tensor
        def _(pe):
            mm = nc.tensor.matmul

            def turn(dst, src, eye):
                return nc.tensor.transpose(dst, src, eye)

            def turn4(dst, blocks, eye):
                for i, src in enumerate(blocks):
                    n = src.shape[0]
                    last = turn(dst[0:src.shape[1], i * n:(i + 1) * n], src, eye[0:n, 0:n])
                return last

            def unit(u):
                o = bank[4 + u % 2]
                if u < 2:
                    pe.wait_ge(s_v, 8)
                else:
                    pe.wait_ge(s_ue, u - 1)
                if u < 4:
                    if u == 0:
                        pe.wait_ge(s_uq, 16)
                    last = turn4(o, [uq_n[:, (4 * u + i) * XD:(4 * u + i + 1) * XD] for i in range(4)], ident)
                elif u < 8:
                    if u == 4:
                        pe.wait_ge(s_ukuv, 32)
                    last = turn4(o, [ukuv_n[:, (4 * (u - 4) + i) * XD:(4 * (u - 4) + i + 1) * XD] for i in range(4)], ident)
                elif u < 10:
                    if u == 8:
                        pe.wait_ge(s_ue, 8)
                    for i in range(8):
                        h = 8 * (u - 8) + i
                        last = mm(o[0:XQ, i * XC:(i + 1) * XC], uq_t[:, h, :], ukuv_t[:, h, 0:XC], start=True, stop=True)
                elif u == 10:
                    pe.wait_ge(s_wkv, 64)
                    for c in range(EC):
                        last = turn(o[0:XC, c * P:(c + 1) * P], wk1[:, c, 0:XC], ident)
                elif u == 11:
                    pe.wait_ge(s_ue, 11)
                    for c in range(EC):
                        last = mm(o[:, c * P:(c + 1) * P], wkvct[:, c * P:(c + 1) * P],
                                  wkr[:, :, :].rearrange("k a r -> k (a r)"), start=True, stop=True)
                elif u < 16:
                    if u == 12:
                        pe.wait_ge(s_kv, 16)
                    last = turn4(o, [kv_n[:, i % B, (i // B) * P:(i // B + 1) * P] for i in range(4 * (u - 12), 4 * (u - 12) + 4)], ident)
                elif u < 20:
                    if u == 16:
                        pe.wait_ge(s_ue, 16)
                        pe.wait_ge(s_zero, 1)
                    w, h = (wk1, wk2)[(u - 16) // 2], (u - 16) % 2
                    for c in range(EC):
                        last = mm(o[:, :], w[:, c, :], kv_t[:, c, 4 * h:4 * h + 4, :].rearrange("p b k -> p (b k)"), start=(c == 0), stop=(c == EC - 1))
                elif u == 20:
                    for b in range(B):
                        for c in range(EC):
                            last = mm(o[:, b * XC:(b + 1) * XC], kv_t[:, c, b, :], wk1[:, c, 0:XC], start=(c == 0), stop=(c == EC - 1))
                elif u < 25:
                    if u == 21:
                        pe.wait_ge(s_wo, 16)
                    for i in range(4):
                        h = 4 * (u - 21) + i
                        q, k = i % 2, i // 2
                        last = mm(o[q * XC:(q + 1) * XC, k * E:(k + 1) * E], ukuv_t[:, h, XC:P], wo_n[:, h, :], start=True, stop=True)
                elif u == 25:
                    pe.wait_ge(s_wabs, 3)
                    pe.wait_ge(s_ones, 1)
                    last = mm(o[:, 0:3], ones[:, :], wsum[:, :], start=True, stop=True)
                else:
                    j, k = (u - 26) // 4, (u - 26) % 4
                    if k == 0:
                        pe.wait_ge(s_w[j], 16)
                    if j < 2:
                        blocks = [wn[j][:, i % 8, (i // 8) * P:(i // 8 + 1) * P] for i in range(4 * k, 4 * k + 4)]
                    else:
                        blocks = [wn[j][:, i % 2, (i // 2) * P:(i // 2 + 1) * P] for i in range(4 * k, 4 * k + 4)]
                    last = turn4(o, blocks, ident)
                last.then_inc(s_up, 1)

            pe.wait_ge(s_cst, 16)
            pe.wait_ge(s_x, 16)
            for c in range(EC):
                for t in range(RT):
                    last = turn(bank[c][:, t * R:(t + 1) * R], xn[:, t, c * P:(c + 1) * P], ident[0:R, 0:R])
                last.then_inc(s_xtp, 1)
            pe.wait_ge(s_wqkv, 16)
            for k in range(3):
                turn4(bank[2 + k], [wqkv_n[:, i % 6, (i // 6) * P:(i // 6 + 1) * P] for i in range(4 * k, 4 * k + 4)], ident).then_inc(s_wtp, 1)
            pe.wait_ge(s_wproj, 16)
            turn4(bank[5], [wproj_n[:, i % 2, (i // 2) * P:(i // 2 + 1) * P] for i in range(4)], ident).then_inc(s_wtp, 1)
            pe.wait_ge(s_xt, 2)
            pe.wait_ge(s_wt, 3)
            for m in range(4):
                for c in range(EC):
                    last = mm(bank[(6, 7, 0, 1)[m]][:, :], wqkv_t[:, c, m * P:(m + 1) * P], xt[:, c, :, :].rearrange("p b s -> p (b s)"),
                              start=(c == 0), stop=(c == EC - 1))
                last.then_inc(s_qkp, 1)
            pe.wait_ge(s_wt, 4)
            for t in range(RT):
                for a in range(2):
                    for q in range(2):
                        for c in range(EC):
                            last = mm(bank[2 + t][q * SP:(q + 1) * SP, a * P:(a + 1) * P], xt[:, c, 2 * t + a, :],
                                      wqkv_t[:, c, 2 * E:3 * E].rearrange("p (h q d) -> p h q d", h=HH, q=2)[:, :, q, :], start=(c == 0), stop=(c == EC - 1))
                last.then_inc(s_vp, 1)

            def scores(g):
                t, hf = g // 2, g % 2
                o = bank[6 + g % 2]
                if g == 0:
                    pe.wait_ge(s_qk, 4)
                    pe.wait_ge(s_idb, 2)
                if g < 2:
                    pe.wait_ge(s_kblk, g + 1)
                else:
                    pe.wait_ge(s_sub, g - 1)
                for a in range(2):
                    rows = o[a * SP:(a + 1) * SP, 0:HH * S]
                    mm(rows, identb[0:SP, 0:SP], causal[:, :].unsqueeze(1).broadcast_to([SP, HH, S]), start=True, stop=False)
                    last = mm(rows, qt[:, hf, 2 * t + a, :], kblk[:, hf, 2 * t + a, :, :].rearrange("p h s -> p (h s)"), start=False, stop=True)
                last.then_inc(s_sc, 1)

            def prob_turn(g):
                pe.wait_ge(s_exp, g + 1)
                if g >= 2:
                    pe.wait_ge(s_pt, g - 1)
                turn4(bank[g % 2], [prob[:, g % 2, 2 * i:2 * i + 2, :].rearrange("p h s -> p (h s)") for i in range(4)], ident).then_inc(s_ptp, 1)

            def values(g):
                t, hf = g // 2, g % 2
                pe.wait_ge(s_pt, g + 1)
                if g == 0:
                    pe.wait_ge(s_v, 8)
                if hf == 0 and t >= 1:
                    pe.wait_ge(s_attn, t)
                for i in range(4):
                    for a in range(2):
                        last = mm(bank[2][a * SP:(a + 1) * SP, (4 * hf + i) * VW:(4 * hf + i + 1) * VW], probt[:, g % 2, i, a * SP:(a + 1) * SP],
                                  vblk[:, 2 * t + a, 4 * hf + i, :], start=True, stop=True)
                last.then_inc(s_av, 1)

            def attn_turn(t):
                pe.wait_ge(s_attn, t + 1)
                for c in range(EC):
                    last = turn(bank[3][:, c * P:(c + 1) * P], attn[:, t % 2, c * HH:(c + 1) * HH, :].rearrange("p h d -> p (h d)"), ident)
                last.then_inc(s_atp, 1)

            def project(t):
                pe.wait_ge(s_at, t + 1)
                if t >= 1:
                    pe.wait_ge(s_res, t)
                for c in range(EC):
                    last = mm(bank[3][0:R, E:2 * E], attnt[:, c, t * R:(t + 1) * R], wproj_t[:, c, :], start=(c == 0), stop=(c == EC - 1))
                last.then_inc(s_y, 1)

            scores(0)
            for g in range(NG):
                if g + 1 < NG:
                    scores(g + 1)
                for u in range(SPREAD[g], SPREAD[g + 1]):
                    unit(u)
                prob_turn(g)
                if g >= 3 and g % 2 == 1:
                    project((g - 3) // 2)
                values(g)
                if g >= 2 and g % 2 == 0:
                    attn_turn(g // 2 - 1)
            attn_turn(RT - 1)
            project(RT - 1)
            unit(25)

            for t in range(RT):
                pe.wait_ge(s_ln, t + 1)
                for c in range(EC):
                    last = turn(bank[c][:, t * R:(t + 1) * R], x1[:, t, c * P:(c + 1) * P], ident[0:R, 0:R])
            last.then_inc(s_x1tp, 1)
            pe.wait_ge(s_x1t, 2)
            pe.wait_ge(s_wdq, 16)
            for c in range(EC):
                last = mm(bank[2][0:XQ, 0:N], wdq_n[:, c, :], x1t[:, c, :], start=(c == 0), stop=(c == EC - 1))
            last.then_inc(s_qcp, 1)
            pe.wait_ge(s_qc, 1)
            pe.wait_ge(s_qr, 2)
            for p in range(XP):
                if p >= 2:
                    pe.wait_ge(s_bt, p - 1)
                mm(bank[p % 2][:, 0:N], wqs[:, 2 * p:2 * p + 2, :].rearrange("q h r -> q (h r)"), qct[:, :], start=True, stop=True).then_inc(s_bp, 1)
                for h in (2 * p, 2 * p + 1):
                    if h >= 4:
                        pe.wait_ge(s_at2, h - 3)
                    mm(bank[(2, 3, 6, 7)[h % 4]][:, 0:N], wqa[:, h, :], qct[:, :], start=True, stop=True).then_inc(s_ap, 1)
                for u in FFN_UNITS[p]:
                    unit(u)

            def context_out(t, downs):
                pe.wait_ge(s_xo, 2 * t + 2)
                if downs:
                    pe.wait_ge(s_r3, downs)
                if t >= 1:
                    pe.wait_ge(s_xres, t)
                for p in range(XP):
                    last = mm(bank[7][0:R, 0:E], ctxt[:, p, t * R:(t + 1) * R], wvo[:, p, :], start=(p == 0), stop=(p == XP - 1))
                last.then_inc(s_xy, 1)

            def turn_x(t, turned):
                if turned:
                    pe.wait_ge(s_hqt, 2 * turned)
                pe.wait_ge(s_xq, t + 1)
                if t == 0:
                    pe.wait_ge(s_wrnd, 12)
                else:
                    pe.wait_ge(s_xqt, t)
                ob = bank[6][:, :].bitcast(BF16)
                for g in range(2):
                    for c in range(EC):
                        i = g * EC + c
                        last = turn(ob[:, i * R:(i + 1) * R], xq[:, t % 2, g, c * P:(c + 1) * P], identb[0:R, 0:R])
                last.then_inc(s_xqp, 1)

            def up(t, hf):
                k = 2 * t + hf
                if hf == 0:
                    pe.wait_ge(s_xqt, t + 1)
                if k >= 1:
                    pe.wait_ge(s_h, k)
                for g in range(2):
                    for c in range(EC):
                        last = mm(bank[1 + 2 * g][0:R, :], xqt[:, t % 2, g, c, :], wt[g][:, c, hf * 512:(hf + 1) * 512], start=(c == 0), stop=(c == EC - 1))
                last.then_inc(s_uv, 1)

            def turn_h(t, turned):
                pe.wait_ge(s_xqt, turned)
                pe.wait_ge(s_hq, t + 1)
                ob = bank[6][:, :].bitcast(BF16)
                for a in range(2):
                    if 2 * t + a >= 1:
                        pe.wait_ge(s_hqt, 2 * t + a)
                    for k in range(4):
                        last = turn(ob[:, (4 + k) * R:(5 + k) * R], hq[:, t % 2, (4 * a + k) * P:(4 * a + k + 1) * P], identb[0:R, 0:R])
                    last.then_inc(s_hqp, 1)

            def down(t, outs):
                pe.wait_ge(s_xres, outs)
                pe.wait_ge(s_hqt, 2 * t + 2)
                if t >= 1:
                    pe.wait_ge(s_r3, t)
                for k in range(8):
                    last = mm(bank[7][0:R, E:2 * E], hqt[:, k, :], wt[2][:, k, :], start=(k == 0), stop=(k == 7))
                last.then_inc(s_y3, 1)

            pe.wait_ge(s_flag, 1)
            outside = pe.value_load(flag[0:1, 0:1])
            with pe.If(outside > 0):
                pe.wait_ge(s_at2, XH)
                pe.wait_ge(s_bt, XP)
                pe.wait_ge(s_ue, UNITS)
                with pe.Fori(0, B) as b:
                    with pe.Fori(0, NKT) as t:
                        it = b * NKT + t
                        pe.wait_ge(g_kv, 16 * it + 16)
                        for c in range(EC):
                            last = turn(bank[0][:, c * P:c * P + KT], g_kvn[:, c * P:(c + 1) * P], ident[0:KT, 0:KT])
                        last.then_inc(g_ktp, 1)
                        pe.wait_ge(g_kt, it + 1)
                        for k, w in enumerate((wk1, wk2)):
                            for c in range(EC):
                                mm(bank[1][:, k * P:k * P + KT], w[:, c, :], g_kvt[:, c, :], start=(c == 0), stop=(c == EC - 1))
                        for c in range(EC):
                            last = mm(bank[1][0:KT, 2 * P:2 * P + XC], g_kvt[:, c, :], wk1[:, c, 0:XC], start=(c == 0), stop=(c == EC - 1))
                        last.then_inc(g_kp, 1)
                        pe.wait_ge(g_k, it + 1)
                        pe.wait_ge(g_q, b + 1)
                        for p in range(XP):
                            last = mm(bank[2 + p // 4][0:R, (p % 4) * KT:(p % 4 + 1) * KT], g_qb[:, p, :],
                                      g_key, start=True, stop=True)
                        last.then_inc(g_s, 1)
                    with pe.Fori(0, NKT) as t:
                        it = b * NKT + t
                        pe.wait_ge(g_pk, it + 1)
                        for p in range(XP):
                            last = turn(bank[4 + p // 4][0:KT, (p % 4) * R:(p % 4 + 1) * R], g_pk_b[:, p, :], ident[0:R, 0:R])
                        last.then_inc(g_ptp, 1)
                        pe.wait_ge(g_pt, it + 1)
                        for a in range(2):
                            last = mm(bank[6][a * XC:(a + 1) * XC, 0:XP * S], g_vk, g_ptb[:, :, a * S:(a + 1) * S], start=True, stop=True)
                        last.then_inc(g_op, 1)
                for t in range(RT):
                    context_out(t, t)
                    turn_x(t, t)
                    up(t, 0)
                    up(t, 1)
                    turn_h(t, t + 1)
                    down(t, t + 1)
            with pe.Else():
                def xscores(k):
                    b, hf = k // 2, k % 2
                    o = bank[4 + k % 2]
                    if k == 0:
                        pe.wait_ge(s_mask, 1)
                        pe.wait_ge(s_idb, 4)
                        pe.wait_ge(s_krope, 1)
                        pe.wait_ge(s_qf, XP)
                        pe.wait_ge(s_at2, XH)
                        pe.wait_ge(s_ue, UNITS)
                    if k >= 2:
                        pe.wait_ge(s_xexp, k - 1)
                    mm(o[0:R, :], identd[:, :], xmask[:, b, :].unsqueeze(1).broadcast_to([S, 4, WIN]), start=True, stop=False)
                    for i in range(4):
                        last = mm(o[0:R, i * WIN:(i + 1) * WIN], qf[:, 4 * hf + i, b, :, :].rearrange("p q s -> p (q s)"), ka[:, b, :], start=False, stop=(i == 3))
                    last.then_inc(s_xs, 1)

                def xturn(k):
                    pe.wait_ge(s_xnorm, k + 1)
                    if k >= 1:
                        pe.wait_ge(s_xpt, k)
                    for i in range(4):
                        last = turn(bank[0][:, i * R:(i + 1) * R], xprob[:, k % 3, i, :], ident[0:R, 0:R])
                    last.then_inc(s_xptp, 1)

                def xvalues(k):
                    b, hf = k // 2, k % 2
                    pe.wait_ge(s_xpt, k + 1)
                    if hf == 0 and b >= 1:
                        pe.wait_ge(s_xo, b)
                    for a in range(2):
                        last = mm(bank[2][a * XC:(a + 1) * XC, hf * 4 * S:(hf + 1) * 4 * S], vx[:, b, :], xpt[:, k % 2, :, a * S:(a + 1) * S], start=True, stop=True)
                    last.then_inc(s_xop, 1)

                for k in range(STEPS):
                    if k < KS:
                        xscores(k)
                    if 0 <= k - 2 < KS:
                        xturn(k - 2)
                    for t in tile(k, PE_DOWN):
                        down(t, started(k, PE_OUT))
                    for t in tile(k, PE_TURN_H):
                        turn_h(t, started(k, PE_TURN_X))
                    if 0 <= k - 3 < KS:
                        xvalues(k - 3)
                    for t in tile(k, PE_OUT):
                        context_out(t, started(k + 1, PE_DOWN))
                    for t in tile(k, PE_TURN_X):
                        turn_x(t, started(k + 1, PE_TURN_H))
                    for t in tile(k, PE_UP0):
                        up(t, 0)
                    for t in tile(k, PE_UP1):
                        up(t, 1)

        @block.scalar
        def _(act):
            def copy(dst, src, scale=1.0):
                return nc.scalar.activation(dst, src, ACT.Copy, scale=scale)

            def unit(u):
                o = bank[4 + u % 2]
                if u == 25:
                    for j in range(3):
                        act.wait_ge(s_w[j], 16)
                        if j:
                            act.wait_ge(s_wabs, j)
                        nc.scalar.activation(junk_w, wn[j][:, :, :].rearrange("p a b -> p (a b)"), ACT.Abs, accum_out=wsum[:, j:j + 1]).then_inc(s_wabs, 1)
                act.wait_ge(s_up, u + 1)
                if u < 4:
                    last = copy(uq_t[:, 4 * u:4 * u + 4, :].rearrange("p h k -> p (h k)"), o[:, 0:4 * XQ])
                elif u < 8:
                    last = copy(ukuv_t[:, 4 * (u - 4):4 * (u - 4) + 4, :].rearrange("p h k -> p (h k)"), o[:, :])
                elif u < 10:
                    last = copy(wqa[:, 8 * (u - 8):8 * (u - 8) + 8, 0:XC], o[0:XQ, :].rearrange("p (h k) -> p h k", h=8))
                elif u == 10:
                    last = copy(wkvct[:, :], o[0:XC, 0:E])
                elif u == 11:
                    ob = o[:, 0:E].rearrange("p (c k) -> p c k", c=EC)
                    copy(wk1[:, :, XC:P], ob[:, :, 0:XR])
                    last = copy(wk2[:, :, XC:P], ob[:, :, XR:2 * XR])
                elif u < 16:
                    last = copy(kv_t[:, :, :, :].rearrange("p c b k -> p (c b k)")[:, 512 * (u - 12):512 * (u - 11)], o[:, :])
                elif u < 20:
                    if u == 18:
                        act.wait_ge(s_qr, 2)
                    d, h = (ka, kb)[(u - 16) // 2], (u - 16) % 2
                    last = copy(d[:, 4 * h:4 * h + 4, :].rearrange("p b k -> p (b k)"), o[:, :])
                elif u == 20:
                    last = copy(vx[:, :, :].rearrange("p b k -> p (b k)"), o[:, :])
                elif u < 25:
                    act.wait_ge(s_flag, 1)
                    last = copy(wvo[:, 2 * (u - 21):2 * (u - 21) + 2, :].rearrange("p h e -> p (h e)"), o[:, :])
                elif u == 25:
                    last = copy(wtot[:, :], o[:, 0:3])
                else:
                    v = u - 26
                    if v == 0:
                        act.wait_ge(s_krope, 1)
                        act.wait_ge(s_winv, 1)
                    if v >= 2:
                        act.wait_ge(s_wrnd, v - 1)
                    last = nc.scalar.activation(wtanh[:, v % 2, :], o[:, :], ACT.Tanh, scale=winv[:, v // 4:v // 4 + 1])
                last.then_inc(s_ue, 1)

            for k in range(3):
                act.wait_ge(s_wtp, k + 1)
                copy(wqkv_t[:, :, :].rearrange("p c o -> p (c o)")[:, 512 * k:512 * (k + 1)], bank[2 + k][:, :]).then_inc(s_wt, 1)
            act.wait_ge(s_wtp, 4)
            copy(wproj_t[:, :, :].rearrange("p c o -> p (c o)"), bank[5][:, :]).then_inc(s_wt, 1)
            for m in range(4):
                act.wait_ge(s_qkp, m + 1)
                d = (qt, kt)[m // 2][:, m % 2, :, :].rearrange("p b s -> p (b s)")
                copy(d, bank[(6, 7, 0, 1)[m]][:, :], HD ** -0.5 if m < 2 else 1.0).then_inc(s_qk, 1)
            act.wait_ge(s_zero, 2)
            for t in range(RT):
                act.wait_ge(s_vp, t + 1)
                for q in range(2):
                    src = bank[2 + t][q * SP:q * SP + S, 0:2 * P].rearrange("p (b h d) -> p b h d", b=2, h=HH)
                    copy(vblk[q * SP:q * SP + S, 2 * t:2 * t + 2, :, q * HD:(q + 1) * HD], src).then_inc(s_v, 1)

            for g in range(NG):
                act.wait_ge(s_sub, g + 1)
                if g >= 2:
                    act.wait_ge(s_ptp, g - 1)
                nc.scalar.activation(prob[:, g % 2, :, 0:S], srel[:, g % 2, :, :], ACT.Exp).then_inc(s_exp, 1)
                for u in range(SPREAD[g], SPREAD[g + 1]):
                    unit(u)
            unit(25)

            act.wait_ge(s_x1tp, 1)
            copy(x1t[:, 0, :], bank[0][:, 0:N]).then_inc(s_x1t, 1)
            act.wait_ge(s_qcp, 1)
            copy(qct[:, :], bank[2][0:XQ, 0:N]).then_inc(s_qc, 1)

            for p in range(XP):
                for u in FFN_UNITS[p]:
                    unit(u)
            act.wait_ge(s_wln, 1)
            nc.scalar.activation(wone[:, 0, :], wone[:, 1, :], ACT.Ln).then_inc(s_watan, 1)

            def square_x(t):
                act.wait_ge(s_ln, RT + t + 1)
                if t >= 1:
                    act.wait_ge(s_sq, t)
                nc.scalar.activation(junk[:, 0:E], x2[:, t, :], ACT.Square, accum_out=fs[:, t, 0:1]).then_inc(s_sq, 1)

            def take_x(t):
                act.wait_ge(s_xqp, t + 1)
                if t >= 2:
                    act.wait_ge(s_uv, 2 * (t - 1))
                copy(xqt[:, t % 2, :, :, :].rearrange("p g c s -> p (g c s)"), bank[6][:, :].bitcast(BF16)[:, 0:4 * R]).then_inc(s_xqt, 1)

            def gate(k):
                act.wait_ge(s_uv, k + 1)
                act.wait_ge(s_f, k // 2 + 1)
                if k >= 2:
                    act.wait_ge(s_h, k - 1)
                nc.scalar.activation(th[:, k % 2, :], bank[1][0:R, :], ACT.Tanh, scale=fs[:, k // 2, 14:15]).then_inc(s_th, 1)

            def square_h(k):
                t, hf = k // 2, k % 2
                act.wait_ge(s_h, k + 1)
                if k:
                    act.wait_ge(s_hsq, k)
                nc.scalar.activation(junk[:, 512:1024], hraw[:, t % 2, hf * 512:(hf + 1) * 512], ACT.Square, accum_out=fs[:, t, 16 + hf:17 + hf]).then_inc(s_hsq, 1)

            def take_h(t):
                for a in range(2):
                    act.wait_ge(s_hqp, 2 * t + a + 1)
                    if t >= 1 and a == 0:
                        act.wait_ge(s_y3, t)
                    copy(hqt[:, 4 * a:4 * a + 4, :].rearrange("p k s -> p (k s)"), bank[6][:, :].bitcast(BF16)[:, 4 * R:8 * R]).then_inc(s_hqt, 1)

            act.wait_ge(s_flag, 1)
            outside = act.value_load(flag[0:1, 0:1])
            with act.If(outside > 0):
                with act.Fori(0, B) as b:
                    with act.Fori(0, NKT) as t:
                        it = b * NKT + t
                        act.wait_ge(g_ktp, it + 1)
                        copy(g_kvt, bank[0][:, 0:E].rearrange("p (c k) -> p c k", c=EC)[:, :, 0:KT]).then_inc(g_kt, 1)
                    act.wait_ge(g_max, b + 1)
                    for p in range(XP):
                        last = nc.scalar.activation(g_sc[:, p, :], g_sc[:, p, :], ACT.Exp, bias=g_mx[:, p:p + 1], accum_out=g_sm[:, p:p + 1])
                    last.then_inc(g_exp, 1)
                    with act.Fori(0, NKT) as t:
                        it = b * NKT + t
                        act.wait_ge(g_ptp, it + 1)
                        for q in range(2):
                            last = copy(g_ptb[:, 4 * q:4 * q + 4, :].rearrange("p h k -> p (h k)"), bank[4 + q][0:KT, 0:4 * R])
                        last.then_inc(g_pt, 1)
                for t in range(RT):
                    square_x(t)
                    take_x(t)
                    for k in (2 * t, 2 * t + 1):
                        gate(k)
                        square_h(k)
                    take_h(t)
            with act.Else():
                for k in range(STEPS):
                    if k < KS:
                        act.wait_ge(s_xmax, k + 1)
                        if k >= 3:
                            act.wait_ge(s_xptp, k - 2)
                        for i in range(4):
                            last = nc.scalar.activation(xprob[:, k % 3, i, :], bank[4 + k % 2][0:R, i * WIN:(i + 1) * WIN], ACT.Exp,
                                                        bias=xmax[:, k % 3, i:i + 1], accum_out=xsum[:, k % 3, i:i + 1])
                        last.then_inc(s_xexp, 1)
                    if k % 2 == 0 and 0 <= k - 4 <= 2 * (B - 1):
                        b = (k - 4) // 2
                        act.wait_ge(s_xop, 2 * b + 2)
                        if b == 0:
                            act.wait_ge(s_xptp, 1)
                        copy(ctxt[:, :, b * S:(b + 1) * S], bank[2][:, 0:N].rearrange("p (h s) -> p h s", h=XP)).then_inc(s_xo, 1)
                    for t in tile(k, ACT_SQX):
                        square_x(t)
                    for t in tile(k, ACT_XT):
                        take_x(t)
                    for t in tile(k, ACT_TAKE_H):
                        take_h(t)
                    for t in tile(k, ACT_GATE0):
                        gate(2 * t)
                    for t in tile(k, ACT_GATE1):
                        square_h(2 * t)
                        gate(2 * t + 1)
                    for t in tile(k, ACT_SQH):
                        square_h(2 * t + 1)

        @block.vector
        def _(v):
            steps = [0]

            def link(ins):
                steps[0] += 1
                ins.then_inc(s_dve, 1)
                v.wait_ge(s_dve, steps[0])

            def turned_prob(g):
                v.wait_ge(s_ptp, g + 1)
                if g >= 2:
                    v.wait_ge(s_av, g - 1)
                nc.vector.tensor_copy(probt[:, g % 2, :, :].rearrange("p h k -> p (h k)"), bank[g % 2][:, :]).then_inc(s_pt, 1)

            def row_stats(n, t, r):
                link(nc.vector.bn_stats(stats[:, :], r))
                link(nc.vector.bn_aggr(mv[:, n, t, :], stats[:, :]))
                nc.vector.tensor_scalar(veps[:, n, t:t + 1], mv[:, n, t, 1:2], LN_EPS, None, ALU.add).then_inc(s_var[n], 1)

            def normal(n, t, r, dst, done):
                v.wait_ge(s_rstd[n], t + 1)
                nc.vector.tensor_scalar(dst, r, mv[:, n, t, 0:1], rstd[:, n, t:t + 1], ALU.subtract, ALU.mult).then_inc(done, 1)

            v.wait_ge(s_zero, 3)
            for c in range(EC):
                v.wait_ge(s_xtp, c + 1)
                nc.vector.tensor_copy(xt[:, c, :, 0:S], bank[c][:, 0:N].rearrange("p (b s) -> p b s", b=B)).then_inc(s_xt, 1)
            for c in range(2):
                v.wait_ge(s_qk, 3 + c)
                for h in range(HH):
                    last = nc.vector.tensor_scalar(kblk[:, c, :, h, :], kt[:, c, :, 0:S], cst[:, HMASK + h:HMASK + h + 1], None, ALU.mult)
                last.then_inc(s_kblk, 1)

            def soft(g):
                v.wait_ge(s_sc, g + 1)
                s = bank[6 + g % 2][:, 0:HH * S].rearrange("p (h s) -> p h s", h=HH)
                link(nc.vector.tensor_reduce(smax[:, g % 2, :], s, AXX, ALU.max))
                if g >= 2:
                    v.wait_ge(s_exp, g - 1)
                nc.vector.tensor_tensor(srel[:, g % 2, :, :], s, smax[:, g % 2, :].unsqueeze(2).broadcast_to([P, HH, S]), ALU.subtract).then_inc(s_sub, 1)

            def normalise(t):
                v.wait_ge(s_av, 2 * t + 2)
                o = bank[2][:, 0:HH * VW].rearrange("p (h w) -> p h w", h=HH)
                link(nc.vector.reciprocal(orec[:, :, :], o[:, :, 2 * HD:VW]))
                if t >= 2:
                    v.wait_ge(s_atp, t - 1)
                nc.vector.tensor_tensor(attn[:, t % 2, :, :].rearrange("p (h q) d -> p h q d", q=2), o[:, :, 0:2 * HD].rearrange("p h (q d) -> p h q d", q=2),
                                        orec[:, :, :].unsqueeze(3).broadcast_to([P, HH, 2, HD]), ALU.mult).then_inc(s_attn, 1)

            def attn_turned(t):
                v.wait_ge(s_atp, t + 1)
                nc.vector.tensor_copy(attnt[:, :, t * R:(t + 1) * R].rearrange("p c (a s) -> p c a s", a=2),
                                      bank[3][:, 0:E].rearrange("p (c a s) -> p c a s", c=EC, a=2)[:, :, :, 0:S]).then_inc(s_at, 1)

            def add_norm1(t):
                v.wait_ge(s_y, t + 1)
                nc.vector.tensor_tensor(res[:, t % 2, :], bank[3][0:R, E:2 * E], xn[:, t, :], ALU.add).then_inc(s_res, 1)
                v.wait_ge(s_res, t + 1)
                row_stats(0, t, res[:, t % 2, :])
                normal(0, t, res[:, t % 2, :], x1[:, t, :], s_ln)

            soft(0)
            for g in range(NG):
                if g + 1 < NG:
                    soft(g + 1)
                turned_prob(g)
                if g >= 2 and g % 2 == 0:
                    normalise(g // 2 - 1)
                    attn_turned(g // 2 - 1)
                if g >= 3 and g % 2 == 1:
                    add_norm1((g - 3) // 2)
                if g == 2:
                    v.wait_ge(s_seg, 48)
                    link(nc.vector.tensor_scalar(segc[:, :], segr[:, :], -(WIN - 1) / 2.0, None, ALU.add))
                    link(nc.vector.tensor_tensor(segc[:, :], segc[:, :], segc[:, :], ALU.mult))
                    link(nc.vector.tensor_reduce(segm[:, :], segc[:, :], AXX, ALU.max))
                    nc.vector.tensor_scalar(flag[:, :], segm[:, :], (WIN / 2.0) ** 2 - WIN / 4.0, None, ALU.is_gt).then_inc(s_flag, 1)
            normalise(RT - 1)
            attn_turned(RT - 1)
            add_norm1(RT - 1)

            v.wait_ge(s_ue, 26)
            link(nc.vector.tensor_scalar(wmean[:, :], wtot[:, :], 1.0 / (F * E), None, ALU.mult))
            link(nc.vector.tensor_scalar(weps[:, :], wmean[:, :], RMS_EPS, None, ALU.add))
            nc.vector.reciprocal(winv[:, :], weps[:, :]).then_inc(s_winv, 1)
            link(nc.vector.tensor_scalar(wone[:, 0, :], wmean[:, :], -1.0, 1.0, ALU.mult, ALU.add))
            link(nc.vector.reciprocal(wone[:, 0, :], wone[:, 0, :]))
            link(nc.vector.tensor_scalar(wone[:, 1, :], wmean[:, :], 1.0, None, ALU.add))
            nc.vector.tensor_tensor(wone[:, 1, :], wone[:, 1, :], wone[:, 0, :], ALU.mult).then_inc(s_wln, 1)

            v.wait_ge(s_x1tp, 1)
            nc.vector.tensor_copy(x1t[:, 1, :], bank[1][:, 0:N]).then_inc(s_x1t, 1)

            qcos = cst[:, C_QC:C_QC + S].unsqueeze(1).broadcast_to([P, B, S])
            qsin = cst[:, C_QS:C_QS + S].unsqueeze(1).broadcast_to([P, B, S])
            for p in range(XP):
                v.wait_ge(s_bp, p + 1)
                if p >= 2:
                    v.wait_ge(s_qf, p - 1)
                for q in range(2):
                    rows = slice(q * XR, (q + 1) * XR)
                    last = nc.vector.tensor_tensor(t2[XR:P, p % 2, :, q, :],
                                                   bank[p % 2][rows, 0:N].rearrange("p (b s) -> p b s", b=B), qsin[rows, :, :], ALU.mult)
                last.then_inc(s_bt, 1)
                for h in (2 * p, 2 * p + 1):
                    v.wait_ge(s_ap, h + 1)
                    nc.vector.tensor_tensor(qf[:, p, :, h % 2, :],
                                            bank[(2, 3, 6, 7)[h % 4]][:, 0:N].rearrange("p (b s) -> p b s", b=B), qcos, ALU.mult).then_inc(s_at2, 1)
                for u in FFN_UNITS[p]:
                    j, k = (u - 26) // 4, (u - 26) % 4
                    v.wait_ge(s_ue, u + 1)
                    nc.vector.tensor_scalar(wt[j][:, :, :].rearrange("p a b -> p (a b)")[:, k * 512:(k + 1) * 512], wtanh[:, u % 2, :],
                                            MAGIC, MAGIC, ALU.add, ALU.subtract).then_inc(s_wrnd, 1)

            def add2(t):
                v.wait_ge(s_xy, t + 1)
                nc.vector.tensor_tensor(res[:, t % 2, :], bank[7][0:R, 0:E], x1[:, t, :], ALU.add).then_inc(s_xres, 1)
                v.wait_ge(s_xres, t + 1)
                row_stats(1, t, res[:, t % 2, :])

            def norm2(t):
                normal(1, t, res[:, t % 2, :], x2[:, t, :], s_ln)

            def scale_x(t):
                f = fs[:, t, :]
                if t == 0:
                    v.wait_ge(s_g, 48)
                v.wait_ge(s_ln, RT + t + 1)
                link(nc.vector.tensor_tensor(xg[:, :, :], x2[:, t, :].unsqueeze(1).broadcast_to([R, 2, E]), g12[:, :, :], ALU.mult))
                nc.vector.tensor_reduce(f[:, 2:4], xg[:, :, :], AXX, ALU.max, apply_absolute_value=True).then_inc(s_xg, 1)

            def quant_x(t):
                f = fs[:, t, :]
                if t == 0:
                    v.wait_ge(s_watan, 1)
                    link(nc.vector.tensor_scalar(watan[:, :], wone[:, 0, :], 0.5, None, ALU.mult))
                v.wait_ge(s_xg, t + 1)
                v.wait_ge(s_rr, t + 1)
                link(nc.vector.tensor_scalar(f[:, 4:6], f[:, 2:4], f[:, 1:2], 1e-4, ALU.mult, ALU.max))
                link(nc.vector.reciprocal(f[:, 6:8], f[:, 4:6]))
                link(nc.vector.tensor_scalar(f[:, 8:10], f[:, 6:8], f[:, 1:2], 127.0, ALU.mult, ALU.mult))
                for g in range(2):
                    last = nc.vector.tensor_scalar(xg[:, g, :], xg[:, g, :], f[:, 8 + g:9 + g], MAGIC, ALU.mult, ALU.add)
                link(last)
                if t >= 2:
                    v.wait_ge(s_xqp, t - 1)
                nc.vector.tensor_scalar(xq[:, t % 2, :, :], xg[:, :, :], MAGIC, None, ALU.subtract).then_inc(s_xq, 1)
                v.wait_ge(s_xq, t + 1)
                link(nc.vector.scalar_tensor_tensor(f[:, 10:12], f[:, 4:6], 1.0 / 127.0, watan[0:R, 0:2], ALU.mult, ALU.mult))
                nc.vector.tensor_scalar(f[:, 14:15], f[:, 10:11], 0.5, None, ALU.mult).then_inc(s_f, 1)
                link(nc.vector.scalar_tensor_tensor(f[:, 15:16], f[:, 10:11], 0.5, f[:, 11:12], ALU.mult, ALU.mult))

            def hidden(k):
                t, hf = k // 2, k % 2
                v.wait_ge(s_th, k + 1)
                if t >= 2:
                    v.wait_ge(s_hg, 2 * (t - 1))
                    v.wait_ge(s_hsq, 2 * (t - 1))
                link(nc.vector.scalar_tensor_tensor(th[:, k % 2, :], th[:, k % 2, :], 1.0, bank[1][0:R, :], ALU.add, ALU.mult))
                nc.vector.tensor_tensor(hraw[:, t % 2, hf * 512:(hf + 1) * 512], th[:, k % 2, :], bank[3][0:R, :], ALU.mult).then_inc(s_h, 1)

            def max_h(t):
                f = fs[:, t, :]
                v.wait_ge(s_hsq, 2 * t + 2)
                link(nc.vector.tensor_tensor(f[:, 19:20], f[:, 16:17], f[:, 17:18], ALU.add))
                link(nc.vector.tensor_tensor(f[:, 20:21], f[:, 15:16], f[:, 15:16], ALU.mult))
                link(nc.vector.scalar_tensor_tensor(f[:, 19:20], f[:, 19:20], 1.0 / F, f[:, 20:21], ALU.mult, ALU.mult))
                nc.vector.tensor_scalar(f[:, 21:22], f[:, 19:20], RMS_EPS, None, ALU.add).then_inc(s_ms, 1)
                v.wait_ge(s_hg, 2 * t + 2)
                link(nc.vector.tensor_reduce(f[:, 18:19], hg[:, t % 2, :], AXX, ALU.max, apply_absolute_value=True))

            def quant_h(t):
                f = fs[:, t, :]
                v.wait_ge(s_rr3, t + 1)
                link(nc.vector.tensor_tensor(f[:, 23:24], f[:, 22:23], f[:, 15:16], ALU.mult))
                link(nc.vector.tensor_scalar(f[:, 24:25], f[:, 18:19], f[:, 23:24], 1e-4, ALU.mult, ALU.max))
                link(nc.vector.reciprocal(f[:, 25:26], f[:, 24:25]))
                link(nc.vector.tensor_scalar(f[:, 26:27], f[:, 25:26], f[:, 23:24], 127.0, ALU.mult, ALU.mult))
                link(nc.vector.scalar_tensor_tensor(f[:, 27:28], f[:, 24:25], 1.0 / 127.0, watan[0:R, 2:3], ALU.mult, ALU.mult))
                link(nc.vector.tensor_scalar(hg[:, t % 2, :], hg[:, t % 2, :], f[:, 26:27], MAGIC, ALU.mult, ALU.add))
                if t >= 2:
                    v.wait_ge(s_hqp, 2 * (t - 1))
                nc.vector.tensor_scalar(hq[:, t % 2, :], hg[:, t % 2, :], MAGIC, None, ALU.subtract).then_inc(s_hq, 1)

            def add3(t):
                v.wait_ge(s_y3, t + 1)
                nc.vector.scalar_tensor_tensor(r3[:, t % 2, :], bank[7][0:R, E:2 * E], fs[:, t, 27:28], x2[:, t, :], ALU.mult, ALU.add).then_inc(s_r3, 1)
                v.wait_ge(s_r3, t + 1)
                row_stats(2, t, r3[:, t % 2, :])

            def norm3(t):
                if t >= 2:
                    v.wait_ge(s_out[t % 2], 16 * (t // 2))
                normal(2, t, r3[:, t % 2, :], yout[:, t % 2, :], s_yo)

            outside_before = steps[0]
            outside = v.value_load(flag[0:1, 0:1])
            with v.If(outside > 0):
                v.wait_ge(g_io, 16)
                v.wait_ge(s_qf, XP)
                v.wait_ge(s_segf, 1)
                v.wait_ge(s_krope, 1)
                v.wait_ge(s_ue, UNITS)
                nc.vector.memset(g_acc_b, 0.0).then_inc(g_sp, 1)
                with v.Fori(0, B) as b:
                    nc.vector.tensor_copy(g_qb, big[:, :].rearrange("p (h n) -> p h n", h=XP)[:, :, bass.ds(b * R, R)]).then_inc(g_q, 1)
                    nc.vector.tensor_scalar(g_msk, g_iota, segf[:, bass.ds(b, 1)], None, ALU.subtract).then_inc(g_mask, 1)
                    v.wait_ge(g_mask, 3 * b + 1)
                    nc.vector.tensor_tensor(g_msk, g_msk, g_msk, ALU.mult).then_inc(g_mask, 1)
                    v.wait_ge(g_mask, 3 * b + 2)
                    nc.vector.tensor_scalar(g_msk, g_msk, LOOKBACK ** 2 / 4.0, NEG, ALU.is_gt, ALU.mult).then_inc(g_mask, 1)
                    with v.Fori(0, NKT) as t:
                        it = b * NKT + t
                        v.wait_ge(g_kp, it + 1)
                        v.wait_ge(g_tab, 32 * it + 32)
                        nc.vector.tensor_tensor(g_key, bank[1][:, 0:KT], g_cos, ALU.mult).then_inc(g_k1, 1)
                        nc.vector.tensor_tensor(g_key2, bank[1][:, P:P + KT], g_sin, ALU.mult).then_inc(g_k2, 1)
                        nc.vector.tensor_copy(g_v[:, bass.ds(t, 1), :], bank[1][0:KT, 2 * P:2 * P + XC].unsqueeze(1))
                        v.wait_ge(g_k1, it + 1)
                        v.wait_ge(g_k2, it + 1)
                        nc.vector.tensor_tensor(g_key, g_key, g_key2, ALU.add).then_inc(g_k, 1)
                        v.wait_ge(g_s, it + 1)
                        v.wait_ge(g_mask, 3 * b + 3)
                        for q in range(2):
                            last = nc.vector.tensor_tensor(g_sc[:, 4 * q:4 * q + 4, bass.ds(t * KT, KT)], bank[2 + q][0:R, 0:4 * KT].rearrange("p (h k) -> p h k", h=4),
                                                    g_msk[:, bass.ds(t * KT, KT)].unsqueeze(1).broadcast_to([R, 4, KT]), ALU.add)
                        last.then_inc(g_sp, 1)
                    v.wait_ge(g_sp, NKT * b + NKT + 1)
                    nc.vector.tensor_reduce(g_mx, g_sc, AXX, ALU.max, negate=True).then_inc(g_max, 1)
                    v.wait_ge(g_exp, b + 1)
                    nc.vector.reciprocal(g_rc, g_sm).then_inc(g_rec, 1)
                    v.wait_ge(g_rec, b + 1)
                    nc.vector.tensor_tensor(g_sc, g_sc, g_rc.unsqueeze(2).broadcast_to([R, XP, LK]), ALU.mult).then_inc(g_norm, 1)
                    v.wait_ge(g_norm, b + 1)
                    nc.vector.memset(g_acc_b, 0.0).then_inc(g_acc, 1)
                    with v.Fori(0, NKT) as t:
                        it = b * NKT + t
                        nc.vector.tensor_copy(g_vk, g_v[:, bass.ds(t, 1), :].rearrange("p a c -> p (a c)"))
                        nc.vector.tensor_copy(g_pk_b, g_sc[:, :, bass.ds(t * KT, KT)]).then_inc(g_pk, 1)
                        v.wait_ge(g_op, it + 1)
                        v.wait_ge(g_acc, it + b + 1)
                        nc.vector.tensor_tensor(g_acc_b, g_acc_b, bank[6][:, 0:N].rearrange("p (h s) -> p h s", h=XP), ALU.add).then_inc(g_acc, 1)
                    v.wait_ge(g_acc, (NKT + 1) * b + NKT + 1)
                    nc.vector.tensor_copy(ctxt[:, :, bass.ds(b * S, S)], g_acc_b).then_inc(s_xo, 1)
                for t in range(RT):
                    add2(t)
                    norm2(t)
                    scale_x(t)
                    quant_x(t)
                    hidden(2 * t)
                    hidden(2 * t + 1)
                    max_h(t)
                    quant_h(t)
                    add3(t)
                    norm3(t)
            steps[0] = outside_before
            with v.Else():
                def xmaxima(k):
                    v.wait_ge(s_xs, k + 1)
                    if k >= 3:
                        v.wait_ge(s_xexp, k - 2)
                    nc.vector.tensor_reduce(xmax[:, k % 3, :], bank[4 + k % 2][0:R, :].rearrange("p (h k) -> p h k", h=4), AXX, ALU.max, negate=True).then_inc(s_xmax, 1)

                def xrecip(k):
                    v.wait_ge(s_xexp, k + 1)
                    if k >= 3:
                        v.wait_ge(s_xnorm, k - 2)
                    nc.vector.reciprocal(xrec[:, k % 3, :], xsum[:, k % 3, :]).then_inc(s_xrec, 1)

                def xturned(k):
                    v.wait_ge(s_xptp, k + 1)
                    if k >= 2:
                        v.wait_ge(s_xop, k - 1)
                    nc.vector.tensor_copy(xpt[:, k % 2, :, :].rearrange("p h k -> p (h k)"), bank[0][:, 0:4 * R]).then_inc(s_xpt, 1)

                for k in range(STEPS):
                    if k < KS:
                        xmaxima(k)
                    if 0 <= k - 2 < KS:
                        xturned(k - 2)
                    if 0 <= k - 1 < KS:
                        xrecip(k - 1)
                    for t in tile(k, DVE_NORM3):
                        norm3(t)
                    for t in tile(k, DVE_ADD3):
                        add3(t)
                    for t in tile(k, DVE_NORM2):
                        norm2(t)
                        scale_x(t)
                    for t in tile(k, DVE_ADD2):
                        add2(t)
                    for t in tile(k, DVE_QX):
                        quant_x(t)
                    for t in tile(k, DVE_H0):
                        hidden(2 * t)
                    for t in tile(k, DVE_H1):
                        hidden(2 * t + 1)
                    for t in tile(k, DVE_QH):
                        quant_h(t)
                    for t in tile(k, DVE_MH):
                        max_h(t)

        @block.gpsimd
        def _(g):
            g.memset(wk2[:, :, 0:XC], 0.0).then_inc(s_zero, 1)
            g.memset(vblk[:, :, :, :], 0.0).then_inc(s_pool, 1)
            g.wait_ge(s_pool, 1)
            g.memset(vblk[0:SP, :, :, 2 * HD:2 * HD + 1], 1.0).then_inc(s_pool, 1)
            g.memset(vblk[SP:P, :, :, 2 * HD + 1:VW], 1.0).then_inc(s_pool, 1)
            g.wait_ge(s_pool, 3)
            g.memset(prob[:, :, :, S:SP], 0.0).then_inc(s_zero, 1)
            g.memset(xt[:, :, :, :], 0.0).then_inc(s_zero, 1)
            g.memset(mhalf[:, :], -0.5).then_inc(s_pool, 1)
            g.memset(ones[:, :], 1.0).then_inc(s_ones, 1)
            g.wait_ge(s_cst, 16)
            g.tensor_copy(identb[:, :], ident).then_inc(s_idb, 1)
            g.tensor_copy(causal[:, :], cst[0:SP, C_CB:C_CB + S]).then_inc(s_idb, 1)
            g.tensor_copy(identd[:, 0:S], cst[0:S, 0:S]).then_inc(s_idb, 1)
            g.tensor_copy(identd[:, S:R], cst[0:S, 0:S]).then_inc(s_idb, 1)
            g.wait_ge(s_wqr, 16)
            g.tensor_copy(wqa[:, :, XC:P], wqr_n[:, :, :]).then_inc(s_qr, 1)
            g.tensor_copy(wqs[:, :, 0:XR // 2], wqr_n[:, :, XR // 2:XR])
            g.tensor_copy(wqs[:, :, XR // 2:XR], wqr_n[:, :, 0:XR // 2]).then_inc(s_qr, 1)
            g.wait_ge(s_seg, 48)
            g.tensor_copy(segf[:, :], segi[:, :]).then_inc(s_segf, 1)
            g.wait_ge(s_segf, 1)
            g.tensor_tensor(dist[:, :, :], cst[0:S, C_IO:C_IO + WIN].unsqueeze(1).broadcast_to([S, B, WIN]),
                            segf[0:S, :].unsqueeze(2).broadcast_to([S, B, WIN]), ALU.subtract).then_inc(s_pool, 1)
            g.wait_ge(s_pool, 5)
            g.tensor_tensor(dist[:, :, :], dist[:, :, :], dist[:, :, :], ALU.mult).then_inc(s_pool, 1)
            g.wait_ge(s_pool, 6)
            g.tensor_scalar(xmask[:, :, :], dist[:, :, :], LOOKBACK ** 2 / 4.0, NEG, ALU.is_gt, ALU.mult).then_inc(s_mask, 1)

            def root(n, t):
                g.wait_ge(s_var[n], t + 1)
                g.tensor_tensor(rstd[:, n, t:t + 1], veps[:, n, t:t + 1], mhalf[:, :], ALU.pow).then_inc(s_rstd[n], 1)

            root(0, 0)
            root(0, 1)
            g.wait_ge(s_ue, 20)
            kc = cst[:, C_KC:C_KC + WIN].unsqueeze(1).broadcast_to([P, B, WIN])
            ks = cst[:, C_KS:C_KS + WIN].unsqueeze(1).broadcast_to([P, B, WIN])
            g.tensor_tensor(ka[:, :, :], ka[:, :, :], kc, ALU.mult).then_inc(s_pool, 1)
            g.tensor_tensor(kb[:, :, :], kb[:, :, :], ks, ALU.mult).then_inc(s_pool, 1)
            g.wait_ge(s_pool, 8)
            g.tensor_tensor(ka[:, :, :], ka[:, :, :], kb[:, :, :], ALU.add).then_inc(s_krope, 1)
            root(0, 2)
            root(0, 3)
            g.wait_ge(s_rstd[0], RT)
            for p in range(XP):
                g.wait_ge(s_bt, p + 1)
                g.wait_ge(s_at2, 2 * p + 2)
                both = qf[XR:P, p, :, :, :].rearrange("p b q s -> p (b q s)")
                g.tensor_tensor(both, both, t2[XR:P, p % 2, :, :, :].rearrange("p b q s -> p (b q s)"), ALU.add).then_inc(s_qf, 1)

            g.wait_ge(s_qf, XP)
            def rms_x(t):
                f = fs[:, t, :]
                g.wait_ge(s_sq, t + 1)
                g.tensor_scalar(f[:, 12:13], f[:, 0:1], 1.0 / E, RMS_EPS, ALU.mult, ALU.add).then_inc(s_pool, 1)
                g.wait_ge(s_pool, 9 + t)
                g.tensor_tensor(f[:, 1:2], f[:, 12:13], mhalf[:, :], ALU.pow).then_inc(s_rr, 1)

            def gain_h(k):
                t, cols = k // 2, slice((k % 2) * 512, (k % 2 + 1) * 512)
                g.wait_ge(s_h, k + 1)
                if t == 0:
                    g.wait_ge(s_g, 48)
                if t >= 2:
                    g.wait_ge(s_hq, t - 1)
                g.tensor_tensor(hg[:, t % 2, cols], hraw[:, t % 2, cols], g3b[:, cols], ALU.mult).then_inc(s_hg, 1)

            def root_h(t):
                g.wait_ge(s_ms, t + 1)
                g.tensor_tensor(fs[:, t, 22:23], fs[:, t, 21:22], mhalf[:, :], ALU.pow).then_inc(s_rr3, 1)

            g.wait_ge(s_flag, 1)
            outside = g.value_load(flag[0:1, 0:1])
            with g.If(outside > 0):
                for t in range(RT):
                    root(1, t)
                    rms_x(t)
                    gain_h(2 * t)
                    gain_h(2 * t + 1)
                    root_h(t)
                    root(2, t)
            with g.Else():
                for k in range(STEPS):
                    if 0 <= k - 1 < KS:
                        g.wait_ge(s_xrec, k)
                        g.tensor_tensor(xprob[:, (k - 1) % 3, :, :], xprob[:, (k - 1) % 3, :, :], xrec[:, (k - 1) % 3, :].unsqueeze(2).broadcast_to([R, 4, WIN]), ALU.mult).then_inc(s_xnorm, 1)
                    for t in tile(k, DVE_ADD3):
                        root(2, t)
                    for t in tile(k, DVE_ADD2):
                        root(1, t)
                    for t in tile(k, DVE_NORM2):
                        rms_x(t)
                    for t in tile(k, DVE_H0):
                        gain_h(2 * t)
                    for t in tile(k, DVE_H1):
                        gain_h(2 * t + 1)
                    for t in tile(k, DVE_MH):
                        root_h(t)


KS = 2 * B
PE_OUT, DVE_ADD2, DVE_NORM2, ACT_SQX, DVE_QX = 7, 8, 9, 9, 10
PE_TURN_X, ACT_XT, PE_UP0, ACT_GATE0, DVE_H0 = 11, 11, 12, 12, 13
PE_UP1, ACT_GATE1, DVE_H1, ACT_SQH, DVE_MH = 14, 14, 15, 15, 16
DVE_QH, PE_TURN_H, ACT_TAKE_H, PE_DOWN, DVE_ADD3, DVE_NORM3 = 17, 17, 17, 18, 18, 19
STEPS = DVE_NORM3 + 4 * (RT - 1) + 1
FFN_UNITS = [(26, 27), (28, 29), (30, 31), (32, 33), (34, 35), (36, 37), (), ()]


def tile(k, first):
    t, off = divmod(k - first, 4)
    return [t] if off == 0 and 0 <= t < RT else []


def started(k, first):
    return min(RT, max(0, (k - 1 - first) // 4 + 1))


UNITS = 38
SPREAD = [0, 4, 8, 12, 16, 19, 22, 25, 25]


def kernel(x, ctx_2048, itok_BxS_0_1023, L0_attn_Wqkv, L0_attn_Wproj, L0_xattn_W_kvc, L0_xattn_W_dq, L0_xattn_W_uq,
           L0_xattn_W_qr, L0_xattn_W_uk, L0_xattn_W_kr, L0_xattn_W_uv, L0_xattn_W_o, L0_ffn_w1, L0_ffn_g1, L0_ffn_w2,
           L0_ffn_g2, L0_ffn_w3, L0_ffn_g3):
    import concourse.bacc as bacc
    from concourse.bass_utils import run_bass_kernel_spmd

    nc = bacc.Bacc("TRN2", target_bir_lowering=False, num_devices=1)
    c, kc, ks, io = constants()
    named = {
        "x": np.ascontiguousarray(x).reshape(N, E), "ctx_kv": ctx_2048, "seg": itok_BxS_0_1023, "wqkv": L0_attn_Wqkv,
        "wproj": L0_attn_Wproj, "w_kvc": L0_xattn_W_kvc, "w_dq": L0_xattn_W_dq, "w_uq": L0_xattn_W_uq,
        "w_qr": L0_xattn_W_qr, "w_uk": L0_xattn_W_uk, "w_kr": L0_xattn_W_kr, "w_uv": L0_xattn_W_uv, "w_o": L0_xattn_W_o,
        "w1": L0_ffn_w1, "g1": L0_ffn_g1, "w2": L0_ffn_w2, "g2": L0_ffn_g2, "w3": L0_ffn_w3, "g3": L0_ffn_g3,
        "const": c, "kcos": kc, "ksin": ks, "kiota": io,
    }
    arrays, args = {}, []
    for name, a in named.items():
        a = np.ascontiguousarray(a)
        arrays[f"in_{name}"] = a
        args.append(nc.dram_tensor(f"in_{name}", a.shape, mybir.dt.from_np(a.dtype), kind="ExternalInput").ap())
    args.append(nc.dram_tensor("out_y", (N, E), F32, kind="ExternalOutput").ap())
    decoder(nc, *args)
    r = run_bass_kernel_spmd(nc, [arrays], core_ids=[0])
    return r.results[0]["out_y"].reshape(B, S, E)
```

```python
from contextlib import ExitStack

import numpy as np

import concourse.bass as bass
from concourse import mybir

ALU = mybir.AluOpType
ACT = mybir.ActivationFunctionType
AXX = mybir.AxisListType.X
F32 = mybir.dt.float32
BF16 = mybir.dt.bfloat16
I32 = mybir.dt.int32

P = 128
B, S, E = 8, 56, 256
N = B * S
EC = E // P
SP = 64
RT, R = 4, 2 * S
NH, HD = 16, 16
HH = NH // 2
NG = RT * 2
VW = 2 * HD + 2
XH, XD, XC, XQ, XR = 16, 128, 64, 96, 64
XP = XH // 2
BH, HN = B // 2, N // 2
QI = 12
LK, LOOKBACK = 1500, 8
WIN = 128
KT, NKT = 125, 12
F = 1024
NEG = -1e30
MAGIC = 12582912.0
LN_EPS, RMS_EPS = 1e-5, 1e-8

C_ID, C_QC, C_QS, C_KC, C_KS, C_IO, C_CB = 0, 128, 184, 240, 368, 496, 624
C_END = C_CB + S
HMASK = C_END
C_ALL = HMASK + HH


def constants():
    half = XR // 2
    inv = (1.0 / np.float32(10000.0) ** (np.arange(half, dtype=np.float32) / np.float32(half))).astype(np.float32)
    ang = np.arange(LK, dtype=np.float32)[:, None] * inv
    cos, sin = np.cos(ang).T, np.sin(ang).T
    kc = np.concatenate([np.ones((XC, LK)), cos, cos]).astype(np.float32)
    ks = np.concatenate([np.zeros((XC, LK)), -sin, sin]).astype(np.float32)
    scale = np.float32(1.0 / np.sqrt(XD + XR))
    c = np.zeros((P, C_ALL), np.float32)
    c[:, C_ID:C_ID + P] = np.eye(P)
    c[:, C_QC:C_QC + S] = kc[:, :S] * scale
    c[:, C_QS:C_QS + S] = np.concatenate([ks[XC:, :S], ks[XC:, :S]]) * scale
    c[:, C_KC:C_KC + WIN] = kc[:, :WIN]
    c[:, C_KS:C_KS + WIN] = ks[:, :WIN]
    c[:, C_IO:C_IO + WIN] = np.arange(WIN) + LOOKBACK / 2
    c[:S, C_CB:C_CB + S] = np.triu(np.full((S, S), NEG), 1)
    c[:, HMASK:HMASK + HH] = np.arange(P)[:, None] // HD == np.arange(HH)[None, :]
    io = np.broadcast_to(np.arange(LK, dtype=np.float32) + LOOKBACK / 2, (R, LK)).copy()
    return c, kc, ks, io


def decoder(nc, x, ctx_kv, seg, wqkv, wproj, w_kvc, w_dq, w_uq, w_qr, w_uk, w_kr, w_uv, w_o,
            w1, g1, w2, g2, w3, g3, const, kcos, ksin, kiota, out):
    with ExitStack() as stack:
        def sb(name, shape, dt=F32):
            return stack.enter_context(nc.sbuf_tensor(name, shape, dt))

        def sem(name):
            return stack.enter_context(nc.semaphore(name))

        bank = [stack.enter_context(nc.psum_tensor(f"bank{i}", [P, 512], F32)) for i in range(8)]

        cst = sb("cst", [P, C_ALL])
        ident = cst[:, C_ID:C_ID + P]
        identb = sb("identb", [P, P], BF16)
        identd = sb("identd", [S, R], BF16)
        causal = sb("causal", [SP, S], BF16)
        ones = sb("ones", [P, P])
        xn = sb("xn", [R, RT, E])
        def carve(block, sizes):
            at, pieces = 0, {}
            for name, cols in sizes:
                pieces[name] = block[:, at:at + cols]
                at += cols
            return pieces

        lower = sb("lower", [P, 13696])
        A = carve(lower, [("wqkv_n", 6 * E), ("wproj_n", EC * E), ("xt", EC * B * SP), ("wqkv_t", EC * 3 * E), ("kt", EC * B * SP),
                          ("wproj_t", EC * E), ("qt", EC * B * SP), ("vblk", B * HH * VW), ("srel", 2 * HH * S), ("prob", 2 * HH * SP),
                          ("probt", HH * P), ("attn", 2 * E), ("attnt", EC * N)])
        wqkv_n = A["wqkv_n"].rearrange("p (o e) -> p o e", e=E)
        wproj_n = A["wproj_n"].rearrange("p (o e) -> p o e", e=E)
        xt = A["xt"].rearrange("p (c b s) -> p c b s", c=EC, b=B)
        wqkv_t = A["wqkv_t"].rearrange("p (c o) -> p c o", c=EC)
        wproj_t = A["wproj_t"].rearrange("p (c o) -> p c o", c=EC)
        qt = A["qt"].rearrange("p (c b s) -> p c b s", c=EC, b=B)
        kt = A["kt"].rearrange("p (c b s) -> p c b s", c=EC, b=B)
        vblk = A["vblk"].rearrange("p (b h w) -> p b h w", b=B, h=HH)
        srel = A["srel"].rearrange("p (a h s) -> p a h s", a=2, h=HH)
        prob = A["prob"].rearrange("p (a h s) -> p a h s", a=2, h=HH)
        probt = A["probt"].rearrange("p (a h s) -> p a h s", a=2, h=HH // 2)
        attn = A["attn"].rearrange("p (a h d) -> p a h d", a=2, h=NH)
        attnt = A["attnt"].rearrange("p (c n) -> p c n", c=EC)
        C = carve(lower, [("wt", 8 * E), ("x1t", EC * N), ("qct", N), ("t2", 4 * N), ("xprob", 3 * 4 * WIN), ("xpt", 2 * 4 * R), ("ctxt", XP * N)])
        x1t = C["x1t"].rearrange("p (f c n) -> p f c n", f=2, c=EC)
        qct = C["qct"][0:XQ, :]
        t2 = C["t2"].rearrange("p (a h b q s) -> p a h b q s", a=2, h=2, b=BH, q=2)
        xprob = C["xprob"][0:R, :].rearrange("p (a h k) -> p a h k", a=3, h=4)
        xpt = C["xpt"].rearrange("p (a h s) -> p a h s", a=2, h=4)
        ctxt = C["ctxt"].rearrange("p (h n) -> p h n", h=XP)
        big = sb("big", [P, 2 * B * HH * S])
        kblk = big[:, :].rearrange("p (t c b h s) -> p t c b h s", t=RT, c=2, b=2, h=HH)
        qf = big[:, :].rearrange("p (f h b q s) -> p f h b q s", f=2, h=XP, b=BH, q=2)
        smax = sb("smax", [P, 2, HH])
        orec = sb("orec", [P, HH, 2])
        res = sb("res", [R, 2, E])
        r3 = sb("r3", [R, 2, E])
        identq = r3[0:SP, 0, 0:SP].bitcast(BF16)
        stats = sb("stats", [R, 6])
        mv = sb("mv", [R, 3, RT, 2])
        veps = sb("veps", [R, 3, RT])
        rstd = sb("rstd", [R, 3, RT])
        mhalf = sb("mhalf", [R, 1])
        x1 = sb("x1", [R, RT, E])
        x2 = xn
        stage = sb("stage", [P, XP * LK])
        wo_n = stage[:, 0:4096].rearrange("p (h e) -> p h e", h=XH)
        ukuv_n = stage[:, 4096:6144]
        uq_n = stage[0:XQ, 6144:8192]
        ukuv_t = stage[:, 8192:10240].rearrange("p (h k) -> p h k", h=XH)
        uq_t = stage[:, 10240:11776].rearrange("p (h k) -> p h k", h=XH)
        kv_n = sb("kv_n", [P, B, E])
        wn = [ukuv_n.rearrange("p (o e) -> p o e", e=E), stage[:, 6144:8192].rearrange("p (o e) -> p o e", e=E),
              kv_n[:, :, :].rearrange("p b e -> p (b e)").rearrange("p (o e) -> p o e", o=2)]
        wdq_n = sb("wdq_n", [P, EC, XQ])
        wqa = sb("wqa", [XQ, XH, P])
        wqs = sb("wqs", [XQ, XH, XR])
        wk1 = sb("wk1", [P, EC, P])
        wk2 = sb("wk2", [P, EC, P])
        wkr = sb("wkr", [XC, 2, XR])
        wkvct = sb("wkvct", [XC, E])
        wvo_b = sb("wvo", [P, XP * E])
        wvo = wvo_b[:, :].rearrange("p (h e) -> p h e", h=XP)
        segr = wvo_b[0:1, 0:N].bitcast(I32)
        segc = wvo_b[0:1, N:2 * N]
        kv_t = sb("kv_t", [P, EC, B, WIN])
        ka = sb("ka", [P, B, WIN])
        kb_b = sb("kb", [P, B * WIN])
        kb = kb_b[:, :].rearrange("p (b k) -> p b k", b=B)
        wqr_n = kb_b[0:XQ, :].rearrange("p (h r) -> p h r", h=XH)
        wrnd = kb_b[:, :].bitcast(BF16).rearrange("p (a n) -> p a n", a=2)
        vx = sb("vx", [P, B, XC])
        segi = sb("segi", [R, B], I32)
        segf = sb("segf", [R, B])
        segm = sb("segm", [1, 1])
        flag = sb("flag", [1, 1], I32)
        g3_b = sb("g3_b", [R, F])
        g3b = g3_b[:, :]
        dist = g3_b[0:S, :].rearrange("p (b k) -> p b k", b=B)
        xmask = sb("xmask", [S, B, WIN], BF16)
        xmax = sb("xmax", [R, 3, 4])
        xsum = sb("xsum", [R, 3, 4])
        xrec = sb("xrec", [R, 3, 4])
        wt_b = C["wt"].bitcast(BF16)
        wt3 = sb("w3_t", [P, 8, E], BF16)
        wt = [wt_b[:, 0:2 * F].rearrange("p (c f) -> p c f", c=EC), wt_b[:, 2 * F:4 * F].rearrange("p (c f) -> p c f", c=EC), wt3[:, :, :]]
        wsum = sb("wsum", [P, 2, 3])
        wtot = sb("wtot", [P, 3])
        wmean = sb("wmean", [P, 3])
        weps = sb("weps", [P, 3])
        winv = sb("winv", [P, 3])
        wone = sb("wone", [P, 2, 3])
        watan = sb("watan", [P, 3])
        junk_w = wt3[:, :, :].rearrange("p k e -> p (k e)")[:, 0:F]
        g12 = sb("g12", [R, 2, E])
        D = carve(stage, [("junk", F), ("th", F), ("hg", 4 * 513), ("hraw", 2 * F),
                          ("xg", 2 * E), ("xq", 2 * E), ("xqt", 4 * R), ("hq", F), ("hqt", 4 * R), ("yout", 2 * E)])
        junk = D["junk"][0:R, :]
        th = D["th"][0:R, :].rearrange("p (a n) -> p a n", a=2)
        hg = D["hg"][0:R, :].rearrange("p (a h n) -> p a h n", a=2, h=2)
        hraw = D["hraw"][0:R, :].rearrange("p (a n) -> p a n", a=2)
        xg = D["xg"][0:R, :].rearrange("p (g e) -> p g e", g=2)
        xq = D["xq"][0:R, :].bitcast(BF16).rearrange("p (a g e) -> p a g e", a=2, g=2)
        xqt = D["xqt"].bitcast(BF16).rearrange("p (a g c s) -> p a g c s", a=2, g=2, c=EC)
        hq = D["hq"][0:R, :].bitcast(BF16).rearrange("p (a f) -> p a f", a=2)
        hqt = D["hqt"].bitcast(BF16).rearrange("p (k s) -> p k s", k=8)
        yout = D["yout"][0:R, :].rearrange("p (a e) -> p a e", a=2)
        fs = sb("fs", [R, RT, 28])

        s_cst, s_x, s_wqkv, s_wproj = sem("s_cst"), sem("s_x"), sem("s_wqkv"), sem("s_wproj")
        s_uq, s_ukuv, s_wqr, s_wo, s_wdq, s_wkv = (sem(n) for n in ("s_uq", "s_ukuv", "s_wqr", "s_wo", "s_wdq", "s_wkv"))
        s_kv, s_seg, s_w, s_g = sem("s_kv"), sem("s_seg"), [sem(f"s_w{i}") for i in range(3)], sem("s_g")
        s_idb, s_zero, s_ones, s_segf, s_mask, s_qr = (sem(n) for n in ("s_idb", "s_zero", "s_ones", "s_segf", "s_mask", "s_qr"))
        s_xtp, s_xt, s_wtp, s_wt, s_qkp, s_qk, s_kblk = (sem(n) for n in ("s_xtp", "s_xt", "s_wtp", "s_wt", "s_qkp", "s_qk", "s_kblk"))
        s_vp, s_v, s_sc, s_sub, s_exp, s_ptp, s_pt = (sem(n) for n in ("s_vp", "s_v", "s_sc", "s_sub", "s_exp", "s_ptp", "s_pt"))
        s_av, s_attn, s_atp, s_at, s_y, s_res, s_ln = (sem(n) for n in ("s_av", "s_attn", "s_atp", "s_at", "s_y", "s_res", "s_ln"))
        s_var, s_rstd = ([sem(f"{n}{i}") for i in range(3)] for n in ("s_var", "s_rstd"))
        s_up, s_ue = sem("s_up"), sem("s_ue")
        s_wabs, s_winv, s_wtanh, s_wrnd, s_watan, s_wln = (sem(n) for n in ("s_wabs", "s_winv", "s_wtanh", "s_wrnd", "s_watan", "s_wln"))
        s_krope = sem("s_krope")
        s_x1tp, s_x1t, s_qcp, s_qc = (sem(n) for n in ("s_x1tp", "s_x1t", "s_qcp", "s_qc"))
        s_qp, s_qi, s_qf = (sem(n) for n in ("s_qp", "s_qi", "s_qf"))
        s_flag = sem("s_flag")
        s_xs, s_xmax, s_xexp, s_xrec, s_xnorm, s_xptp, s_xpt, s_xop, s_xo = (sem(n) for n in ("s_xs", "s_xmax", "s_xexp", "s_xrec", "s_xnorm", "s_xptp", "s_xpt", "s_xop", "s_xo"))
        s_xy, s_xres = sem("s_xy"), sem("s_xres")
        s_sq, s_rr, s_gx, s_xg, s_xq, s_xqp, s_xqt = (sem(n) for n in ("s_sq", "s_rr", "s_gx", "s_xg", "s_xq", "s_xqp", "s_xqt"))
        s_f, s_uv, s_th, s_h, s_hg, s_hsq, s_ms, s_rr3, s_hq, s_hqp, s_hqt, s_y3, s_r3, s_yo = (sem(n) for n in (
            "s_f", "s_uv", "s_th", "s_h", "s_hg", "s_hsq", "s_ms", "s_rr3", "s_hq", "s_hqp", "s_hqt", "s_y3", "s_r3", "s_yo"))
        s_out = [sem(f"s_out{i}") for i in range(2)]
        s_dve, s_pool = sem("s_dve"), sem("s_pool")
        g_q, g_kv, g_tab, g_ktp, g_kt, g_kp, g_k1, g_k2, g_k, g_sp, g_s, g_max, g_exp, g_rec, g_norm, g_pk, g_ptp, g_pt, g_op, g_acc, g_io, g_mask, g_out = (
            sem("g_" + n) for n in ("q", "kv", "tab", "ktp", "kt", "kp", "k1", "k2", "k", "sp", "s", "max", "exp", "rec",
                                    "norm", "pk", "ptp", "pt", "op", "acc", "io", "mask", "out"))

        g_sc = stage[0:R, 0:XP * LK].rearrange("p (h k) -> p h k", h=XP)
        g_qb = kv_t[:, 0, :, :].rearrange("p b k -> p (b k)")[:, 0:XH * S].rearrange("p (h r) -> p h r", h=XP)
        g_iota = C["t2"][0:R, 0:LK]
        g_msk = C["xprob"][0:R, 0:LK]
        g_kvn = kv_n[0:KT, 0, :]
        g_kvt = kv_n[:, 1, :].rearrange("p (c k) -> p c k", c=EC)[:, :, 0:KT]
        g_cos, g_sin = kv_n[:, 2, 0:KT], kv_n[:, 2, 128:128 + KT]
        g_key, g_key2 = kv_n[:, 3, 0:KT], kv_n[:, 3, 128:128 + KT]
        g_v = kv_n[0:KT, 4:7, :].rearrange("p a e -> p (a e)").rearrange("p (t c) -> p t c", c=XC)
        g_vk = kv_n[0:KT, 7, 0:XC]
        g_pk_b = kv_t[0:R, 1, :, :].rearrange("p b k -> p (b k)")[:, 0:XP * KT].rearrange("p (h k) -> p h k", h=XP)
        g_ptb = ka[0:KT, :, :].rearrange("p b k -> p (b k)")[:, 0:XP * R].rearrange("p (h k) -> p h k", h=XP)
        g_acc_b = kb[:, :, :].rearrange("p b k -> p (b k)")[:, 0:XP * S].rearrange("p (h k) -> p h k", h=XP)
        g_mx, g_sm, g_rc = fs[:, 0, 0:XP], fs[:, 1, 0:XP], fs[:, 2, 0:XP]

        block = stack.enter_context(nc.Block())

        @block.sync
        def _(sp):
            def load(dst, src, s, **kw):
                sp.dma_start(dst, src, **kw).then_inc(s, 16)

            load(xn[:, :, :], x.rearrange("(t p) e -> p t e", p=R), s_x)
            load(cst[:, :], const, s_cst)
            load(wqkv_n[:, :, :], wqkv.rearrange("(o p) e -> p o e", p=P), s_wqkv)
            load(wproj_n[:, :, :], wproj.rearrange("(o p) e -> p o e", p=P), s_wproj)
            load(uq_n, w_uq, s_uq)
            load(ukuv_n[0:XC, :], w_uk, s_ukuv)
            load(ukuv_n[XC:P, :], w_uv, s_ukuv)
            load(wqr_n[:, :, :], w_qr.rearrange("q (h r) -> q h r", h=XH), s_wqr)
            load(wk1[:, :, 0:XC], w_kvc.rearrange("(c p) k -> p c k", p=P), s_wkv)
            load(wkr[:, 0, :], w_kr, s_wkv)
            load(wkr[:, 1, 0:XR // 2], w_kr[:, XR // 2:XR], s_wkv)
            load(wkr[:, 1, XR // 2:XR], w_kr[:, 0:XR // 2], s_wkv)
            load(wdq_n[:, :, :], w_dq.rearrange("(c p) k -> p c k", p=P), s_wdq)
            load(segr[:, :], seg.rearrange("(o b) s -> o (b s)", o=1), s_seg)
            load(segi[0:S, :], seg.rearrange("b s -> s b"), s_seg, allow_slow_non_contiguous=True)
            load(segi[S:R, :], seg.rearrange("b s -> s b"), s_seg, allow_slow_non_contiguous=True)
            load(kv_n[:, :, :], ctx_kv[:, 0:WIN, :].rearrange("b k e -> k b e"), s_kv)
            load(wo_n, w_o.rearrange("(h d) e -> d h e", d=XD), s_wo)
            sp.wait_ge(s_ue, 8)
            load(wn[0][:, :, :], w1.rearrange("(o p) e -> p o e", p=P), s_w[0])
            load(wn[1][:, :, :], w2.rearrange("(o p) e -> p o e", p=P), s_w[1])
            sp.wait_ge(s_ue, 16)
            load(wn[2][:, :, :], w3.rearrange("(o p) e -> p o e", p=P), s_w[2])
            load(g12[:, 0, :], g1.rearrange("(o e) -> o e", o=1).broadcast_to([R, E]), s_g)
            load(g12[:, 1, :], g2.rearrange("(o e) -> o e", o=1).broadcast_to([R, E]), s_g)
            sp.wait_ge(s_mask, 1)
            load(g3b[:, :], g3.rearrange("(o e) -> o e", o=1).broadcast_to([R, F]), s_g)

            sp.wait_ge(s_flag, 1)
            outside = sp.value_load(flag[0:1, 0:1])
            with sp.If(outside > 0):
                sp.wait_ge(s_ue, UNITS)
                sp.wait_ge(s_qf, XP)
                sp.wait_ge(s_krope, 1)
                sp.dma_start(g_iota, kiota).then_inc(g_io, 16)
                with sp.Fori(0, B) as b:
                    with sp.Fori(0, NKT) as t:
                        it = b * NKT + t
                        sp.wait_ge(g_sp, it + 1)
                        sp.dma_start(g_kvn, ctx_kv[bass.ds(b, 1), bass.ds(t * KT, KT), :].rearrange("b k e -> (b k) e")).then_inc(g_kv, 16)
                        sp.dma_start(g_cos, kcos[:, bass.ds(t * KT, KT)]).then_inc(g_tab, 16)
                        sp.dma_start(g_sin, ksin[:, bass.ds(t * KT, KT)]).then_inc(g_tab, 16)
            for t in range(RT):
                sp.wait_ge(s_yo, t + 1)
                sp.dma_start(out[t * R:(t + 1) * R, :], yout[:, t % 2, :]).then_inc(s_out[t % 2], 16)
            for s in s_out:
                sp.wait_ge(s, 16 * RT // 2)

        @block.tensor
        def _(pe):
            mm = nc.tensor.matmul

            def turn(dst, src, eye):
                return nc.tensor.transpose(dst, src, eye)

            def turn4(dst, blocks, eye):
                for i, src in enumerate(blocks):
                    n = src.shape[0]
                    last = turn(dst[0:src.shape[1], i * n:(i + 1) * n], src, eye[0:n, 0:n])
                return last

            def turn8(dst, blocks):
                for i, src in enumerate(blocks):
                    last = turn(dst[:, i * P:(i + 1) * P], src, identb[:, :])
                return last

            def unit(u):
                o = bank[unit_bank(u)]
                if u < 2:
                    pe.wait_ge(s_v, 16)
                elif u == 23:
                    pe.wait_ge(s_sub, NG)
                elif u == 24:
                    pe.wait_ge(s_res, RT)
                elif u == 27:
                    pe.wait_ge(s_qi, 2 * QI)
                elif u != 25:
                    pe.wait_ge(s_ue, u - 1)
                if u < 4:
                    if u == 0:
                        pe.wait_ge(s_uq, 16)
                    last = turn4(o, [uq_n[:, (4 * u + i) * XD:(4 * u + i + 1) * XD] for i in range(4)], ident)
                elif u < 8:
                    if u == 4:
                        pe.wait_ge(s_ukuv, 32)
                    last = turn4(o, [ukuv_n[:, (4 * (u - 4) + i) * XD:(4 * (u - 4) + i + 1) * XD] for i in range(4)], ident)
                elif u < 10:
                    if u == 8:
                        pe.wait_ge(s_ue, 8)
                    for i in range(8):
                        h = 8 * (u - 8) + i
                        last = mm(o[0:XQ, i * XC:(i + 1) * XC], uq_t[:, h, :], ukuv_t[:, h, 0:XC], start=True, stop=True)
                elif u == 10:
                    pe.wait_ge(s_wkv, 64)
                    for c in range(EC):
                        last = turn(o[0:XC, c * P:(c + 1) * P], wk1[:, c, 0:XC], ident)
                elif u == 11:
                    pe.wait_ge(s_ue, 11)
                    for c in range(EC):
                        last = mm(o[:, c * P:(c + 1) * P], wkvct[:, c * P:(c + 1) * P],
                                  wkr[:, :, :].rearrange("k a r -> k (a r)"), start=True, stop=True)
                elif u < 16:
                    if u == 12:
                        pe.wait_ge(s_kv, 16)
                    last = turn4(o, [kv_n[:, i % B, (i // B) * P:(i // B + 1) * P] for i in range(4 * (u - 12), 4 * (u - 12) + 4)], ident)
                elif u < 18:
                    if u == 16:
                        pe.wait_ge(s_ue, 16)
                    h = u - 16
                    for c in range(EC):
                        last = mm(o[:, :], wk1[:, c, :], kv_t[:, c, 4 * h:4 * h + 4, :].rearrange("p b k -> p (b k)"), start=(c == 0), stop=(c == EC - 1))
                elif u == 18:
                    for b in range(B):
                        for c in range(EC):
                            last = mm(o[:, b * XC:(b + 1) * XC], kv_t[:, c, b, :], wk1[:, c, 0:XC], start=(c == 0), stop=(c == EC - 1))
                elif u < 23:
                    if u == 19:
                        pe.wait_ge(s_wo, 16)
                    for i in range(4):
                        h = 4 * (u - 19) + i
                        q, k = i % 2, i // 2
                        last = mm(o[q * XC:(q + 1) * XC, k * E:(k + 1) * E], ukuv_t[:, h, XC:P], wo_n[:, h, :], start=True, stop=True)
                elif u == 23:
                    pe.wait_ge(s_wabs, 6)
                    pe.wait_ge(s_ones, 1)
                    for a in range(2):
                        last = mm(o[:, 0:3], ones[:, :], wsum[:, a, :], start=(a == 0), stop=(a == 1))
                else:
                    v = u - 24
                    pe.wait_ge(s_wrnd, v + 1)
                    last = turn8(o[:, :].bitcast(BF16), [wrnd[:, v % 2, i * P:(i + 1) * P] for i in (range(8) if v >= 4 else [2 * (i % 4) + i // 4 for i in range(8)])])
                last.then_inc(s_up, 1)

            pe.wait_ge(s_cst, 16)
            pe.wait_ge(s_x, 16)
            for c in range(EC):
                for t in range(RT):
                    last = turn(bank[c][:, t * R:(t + 1) * R], xn[:, t, c * P:(c + 1) * P], ident[0:R, 0:R])
                last.then_inc(s_xtp, 1)
            pe.wait_ge(s_wqkv, 16)
            for k in range(3):
                turn4(bank[2 + k], [wqkv_n[:, i % 6, (i // 6) * P:(i // 6 + 1) * P] for i in range(4 * k, 4 * k + 4)], ident).then_inc(s_wtp, 1)
            pe.wait_ge(s_wproj, 16)
            turn4(bank[5], [wproj_n[:, i % 2, (i // 2) * P:(i // 2 + 1) * P] for i in range(4)], ident).then_inc(s_wtp, 1)
            pe.wait_ge(s_xt, 2)
            pe.wait_ge(s_wt, 3)
            for m in range(4):
                for c in range(EC):
                    last = mm(bank[(6, 7, 0, 1)[m]][:, :], wqkv_t[:, c, m * P:(m + 1) * P], xt[:, c, :, :].rearrange("p b s -> p (b s)"),
                              start=(c == 0), stop=(c == EC - 1))
                last.then_inc(s_qkp, 1)
            pe.wait_ge(s_wt, 4)
            for t in range(RT):
                for c in range(EC):
                    last = mm(bank[2 + t][:, 0:E], xt[:, c, 2 * t:2 * t + 2, :].rearrange("p b s -> p (b s)"), wqkv_t[:, c, 2 * E:3 * E], start=(c == 0), stop=(c == EC - 1))
                last.then_inc(s_vp, 1)

            def scores(g):
                t, hf = g // 2, g % 2
                o = bank[6 + g % 2]
                if g == 0:
                    pe.wait_ge(s_qk, 4)
                    pe.wait_ge(s_idb, 4)
                if g < 2:
                    pe.wait_ge(s_kblk, g + 1)
                else:
                    pe.wait_ge(s_sub, g - 1)
                mm(o[:, 0:HH * S], identq[:, :], causal[:, :].unsqueeze(1).broadcast_to([SP, HH, S]), start=True, stop=False)
                for a in range(2):
                    last = mm(o[a * SP:(a + 1) * SP, 0:HH * S], qt[:, hf, 2 * t + a, :], kblk[:, t, hf, a, :, :].rearrange("p h s -> p (h s)"), start=False, stop=True)
                last.then_inc(s_sc, 1)

            def prob_turn(g):
                pe.wait_ge(s_exp, g + 1)
                if g >= 2:
                    pe.wait_ge(s_pt, g - 1)
                turn4(bank[g % 2], [prob[:, g % 2, 2 * i:2 * i + 2, :].rearrange("p h s -> p (h s)") for i in range(4)], ident).then_inc(s_ptp, 1)

            def values(g):
                t, hf = g // 2, g % 2
                pe.wait_ge(s_pt, g + 1)
                if g == 0:
                    pe.wait_ge(s_v, 16)
                if hf == 0 and t >= 1:
                    pe.wait_ge(s_attn, t)
                for i in range(4):
                    for a in range(2):
                        last = mm(bank[2][a * SP:(a + 1) * SP, (4 * hf + i) * VW:(4 * hf + i + 1) * VW], probt[:, g % 2, i, a * SP:(a + 1) * SP],
                                  vblk[:, 2 * t + a, 4 * hf + i, :], start=True, stop=True)
                last.then_inc(s_av, 1)

            def attn_turn(t):
                pe.wait_ge(s_attn, t + 1)
                if t >= 1:
                    pe.wait_ge(s_res, t)
                for c in range(EC):
                    last = turn(bank[3][:, c * P:(c + 1) * P], attn[:, t % 2, c * HH:(c + 1) * HH, :].rearrange("p h d -> p (h d)"), ident)
                last.then_inc(s_atp, 1)

            def project(t):
                pe.wait_ge(s_at, t + 1)
                if t >= 1:
                    pe.wait_ge(s_res, t)
                for c in range(EC):
                    last = mm(bank[3][0:R, E:2 * E], attnt[:, c, t * R:(t + 1) * R], wproj_t[:, c, :], start=(c == 0), stop=(c == EC - 1))
                last.then_inc(s_y, 1)

            def latent(f, x_bank, q_bank):
                for t in (2 * f, 2 * f + 1):
                    pe.wait_ge(s_ln, t + 1)
                    for c in range(EC):
                        last = turn(x_bank[:, c * HN + (t - 2 * f) * R:c * HN + (t - 2 * f + 1) * R], x1[:, t, c * P:(c + 1) * P], ident[0:R, 0:R])
                last.then_inc(s_x1tp, 1)
                pe.wait_ge(s_x1t, f + 1)
                pe.wait_ge(s_wdq, 16)
                for c in range(EC):
                    last = mm(q_bank[0:XQ, 0:HN], wdq_n[:, c, :], x1t[:, f, c, :], start=(c == 0), stop=(c == EC - 1))
                last.then_inc(s_qcp, 1)

            def query(i):
                f, pp, kind = i // QI, i % QI // 3, i % 3
                if i % QI == 0:
                    pe.wait_ge(s_qc, f + 1)
                    pe.wait_ge(s_qr, 2)
                if i == QI:
                    pe.wait_ge(s_ue, 27)
                if i % QI >= 2:
                    pe.wait_ge(s_qi, i - 1)
                o = bank[query_bank(i)]
                for j in range(2):
                    if kind == 0:
                        w = wqs[:, 4 * pp + 2 * j:4 * pp + 2 * j + 2, :].rearrange("q h r -> q (h r)")
                    else:
                        w = wqa[:, 4 * pp + 2 * (kind - 1) + j, :]
                    last = mm(o[:, j * HN:(j + 1) * HN], w, qct[:, f * HN:(f + 1) * HN], start=True, stop=True)
                last.then_inc(s_qp, 1)

            scores(0)
            for g in range(NG):
                if g + 1 < NG:
                    scores(g + 1)
                mid = max(SPREAD[g], SPREAD[g + 1] - 1)
                for u in range(SPREAD[g], mid):
                    unit(u)
                prob_turn(g)
                for u in range(mid, SPREAD[g + 1]):
                    unit(u)
                if g >= 1:
                    values(g - 1)
                if g >= 4 and g % 2 == 0:
                    project((g - 4) // 2)
                if g >= 3 and g % 2 == 1:
                    attn_turn((g - 3) // 2)
            unit(23)
            values(NG - 1)
            pe.wait_ge(s_ue, 23)
            latent(0, bank[4], bank[5])
            project(RT - 2)
            for i in range(QI):
                query(i)
                if i == 1:
                    attn_turn(RT - 1)
                if i == 3:
                    project(RT - 1)
                for h in FFN_HALVES.get(i, ()):
                    unit(24 + h)
            latent(1, bank[0], bank[1])

            def context_out(t):
                pe.wait_ge(s_xo, 2 * t + 2)
                if t >= 1:
                    pe.wait_ge(s_xres, t)
                for p in range(XP):
                    last = mm(bank[7][0:R, 0:E], ctxt[:, p, t * R:(t + 1) * R], wvo[:, p, :], start=(p == 0), stop=(p == XP - 1))
                last.then_inc(s_xy, 1)

            def turn_x(t):
                pe.wait_ge(s_xq, t + 1)
                if t == 0:
                    pe.wait_ge(s_ue, UNITS)
                else:
                    pe.wait_ge(s_xqt, t)
                ob = bank[6][:, :].bitcast(BF16)
                for g in range(2):
                    for c in range(EC):
                        i = g * EC + c
                        last = turn(ob[:, i * R:(i + 1) * R], xq[:, t % 2, g, c * P:(c + 1) * P], identb[0:R, 0:R])
                last.then_inc(s_xqp, 1)

            def up(t, hf):
                k = 2 * t + hf
                if hf == 0:
                    pe.wait_ge(s_xqt, t + 1)
                if hf == 0 and k >= 2:
                    pe.wait_ge(s_h, max(2, k - 1))
                elif hf == 1 and k != 3:
                    pe.wait_ge(s_h, max(1, k - 1))
                for g in range(2):
                    for c in range(EC):
                        last = mm(bank[up_banks(k)[g]][0:R, :], xqt[:, t % 2, g, c, :], wt[g][:, c, hf * 512:(hf + 1) * 512], start=(c == 0), stop=(c == EC - 1))
                last.then_inc(s_uv, 1)

            def turn_h(t):
                pe.wait_ge(s_hq, 2 * t + 1)
                if t >= 1:
                    pe.wait_ge(s_hqt, t)
                ob = bank[2][:, :].bitcast(BF16)
                for k in range(8):
                    if k == 4:
                        pe.wait_ge(s_hq, 2 * t + 2)
                    last = turn(ob[:, k * R:(k + 1) * R], hq[:, t % 2, k * P:(k + 1) * P], identb[0:R, 0:R])
                last.then_inc(s_hqp, 1)

            def down(t):
                pe.wait_ge(s_hqt, t + 1)
                if t >= 1:
                    pe.wait_ge(s_r3, t)
                for k in range(8):
                    last = mm(bank[0][0:R, 0:E], hqt[:, k, :], wt[2][:, k, :], start=(k == 0), stop=(k == 7))
                last.then_inc(s_y3, 1)

            pe.wait_ge(s_flag, 1)
            outside = pe.value_load(flag[0:1, 0:1])
            with pe.If(outside > 0):
                for i in range(QI, 2 * QI):
                    query(i)
                for u in range(27, UNITS):
                    unit(u)
                pe.wait_ge(s_ue, UNITS)
                with pe.Fori(0, B) as b:
                    with pe.Fori(0, NKT) as t:
                        it = b * NKT + t
                        pe.wait_ge(g_kv, 16 * it + 16)
                        for c in range(EC):
                            last = turn(bank[0][:, c * P:c * P + KT], g_kvn[:, c * P:(c + 1) * P], ident[0:KT, 0:KT])
                        last.then_inc(g_ktp, 1)
                        pe.wait_ge(g_kt, it + 1)
                        for k, w in enumerate((wk1, wk2)):
                            for c in range(EC):
                                mm(bank[1][:, k * P:k * P + KT], w[:, c, :], g_kvt[:, c, :], start=(c == 0), stop=(c == EC - 1))
                        for c in range(EC):
                            last = mm(bank[1][0:KT, 2 * P:2 * P + XC], g_kvt[:, c, :], wk1[:, c, 0:XC], start=(c == 0), stop=(c == EC - 1))
                        last.then_inc(g_kp, 1)
                        pe.wait_ge(g_k, it + 1)
                        pe.wait_ge(g_q, b + 1)
                        for p in range(XP):
                            last = mm(bank[2 + p // 4][0:R, (p % 4) * KT:(p % 4 + 1) * KT], g_qb[:, p, :],
                                      g_key, start=True, stop=True)
                        last.then_inc(g_s, 1)
                    with pe.Fori(0, NKT) as t:
                        it = b * NKT + t
                        pe.wait_ge(g_pk, it + 1)
                        for p in range(XP):
                            last = turn(bank[4 + p // 4][0:KT, (p % 4) * R:(p % 4 + 1) * R], g_pk_b[:, p, :], ident[0:R, 0:R])
                        last.then_inc(g_ptp, 1)
                        pe.wait_ge(g_pt, it + 1)
                        for a in range(2):
                            last = mm(bank[6][a * XC:(a + 1) * XC, 0:XP * S], g_vk, g_ptb[:, :, a * S:(a + 1) * S], start=True, stop=True)
                        last.then_inc(g_op, 1)
                for t in range(RT):
                    context_out(t)
                    turn_x(t)
                    up(t, 0)
                    up(t, 1)
                    turn_h(t)
                    down(t)
            with pe.Else():
                def xscores(k):
                    b, hf = k // 2, k % 2
                    o = bank[4 + k % 2]
                    if k == 0:
                        pe.wait_ge(s_mask, 1)
                        pe.wait_ge(s_idb, 6)
                        pe.wait_ge(s_krope, 1)
                        pe.wait_ge(s_qi, QI)
                        pe.wait_ge(s_ue, 27)
                    if k % B == 0:
                        pe.wait_ge(s_qf, (k // B + 1) * XP // 2)
                    if k >= 2:
                        pe.wait_ge(s_xexp, k - 1)
                    mm(o[0:R, :], identd[:, :], xmask[:, b, :].unsqueeze(1).broadcast_to([S, 4, WIN]), start=True, stop=False)
                    for i in range(4):
                        last = mm(o[0:R, i * WIN:(i + 1) * WIN], qf[:, b // BH, 4 * hf + i, b % BH, :, :].rearrange("p q s -> p (q s)"), ka[:, b, :], start=False, stop=(i == 3))
                    last.then_inc(s_xs, 1)

                def xturn(k):
                    pe.wait_ge(s_xnorm, k + 1)
                    if k >= 1:
                        pe.wait_ge(s_xpt, k)
                    for i in range(4):
                        last = turn(bank[0][:, i * R:(i + 1) * R], xprob[:, k % 3, i, :], ident[0:R, 0:R])
                    last.then_inc(s_xptp, 1)

                def xvalues(k):
                    b, hf = k // 2, k % 2
                    pe.wait_ge(s_xpt, k + 1)
                    if hf == 0 and b >= 1:
                        pe.wait_ge(s_xo, b)
                    for a in range(2):
                        last = mm(bank[2][a * XC:(a + 1) * XC, hf * 4 * S:(hf + 1) * 4 * S], vx[:, b, :], xpt[:, k % 2, :, a * S:(a + 1) * S], start=True, stop=True)
                    last.then_inc(s_xop, 1)

                for k in range(STEPS):
                    if k < KS:
                        xscores(k)
                    if 0 <= k - 2 < KS:
                        xturn(k - 2)
                    for i in late_queries(k):
                        query(i)
                    for u in late_units(k):
                        unit(u)
                    if 0 <= k - 3 < KS:
                        xvalues(k - 3)
                    for t in tile(k, PE_OUT):
                        context_out(t)
                    for t in tile(k, PE_DOWN):
                        if t == 0:
                            pe.wait_ge(s_xpt, KS)
                        down(t)
                    for t in tile(k, PE_TURN_H):
                        if t == 0:
                            pe.wait_ge(s_xo, B)
                        turn_h(t)
                    for t in tile(k, PE_TURN_X):
                        turn_x(t)
                    for t in tile(k, PE_UP0):
                        up(t, 0)
                    for t in tile(k, PE_UP1):
                        if t == 1:
                            pe.wait_ge(s_xexp, KS)
                        up(t, 1)

        @block.scalar
        def _(act):
            def copy(dst, src, scale=1.0):
                return nc.scalar.activation(dst, src, ACT.Copy, scale=scale)

            def unit(u):
                o = bank[unit_bank(u)]
                act.wait_ge(s_up, u + 1)
                if u < 4:
                    last = copy(uq_t[:, 4 * u:4 * u + 4, :].rearrange("p h k -> p (h k)"), o[:, 0:4 * XQ])
                elif u < 8:
                    last = copy(ukuv_t[:, 4 * (u - 4):4 * (u - 4) + 4, :].rearrange("p h k -> p (h k)"), o[:, :])
                elif u < 10:
                    last = copy(wqa[:, 8 * (u - 8):8 * (u - 8) + 8, 0:XC], o[0:XQ, :].rearrange("p (h k) -> p h k", h=8))
                elif u == 10:
                    last = copy(wkvct[:, :], o[0:XC, 0:E])
                elif u == 11:
                    ob = o[:, 0:E].rearrange("p (c k) -> p c k", c=EC)
                    copy(wk1[:, :, XC:P], ob[:, :, 0:XR])
                    last = copy(wk2[:, :, XC:P], ob[:, :, XR:2 * XR])
                elif u < 16:
                    last = copy(kv_t[:, :, :, :].rearrange("p c b k -> p (c b k)")[:, 512 * (u - 12):512 * (u - 11)], o[:, :])
                elif u < 18:
                    if u == 16:
                        act.wait_ge(s_qr, 2)
                    h = 4 * (u - 16)
                    copy(ka[:, h:h + 4, :].rearrange("p b k -> p (b k)"), o[:, :])
                    copy(kb[XC:XC + XR // 2, h:h + 4, :].rearrange("p b k -> p (b k)"), o[XC + XR // 2:P, :])
                    last = copy(kb[XC + XR // 2:P, h:h + 4, :].rearrange("p b k -> p (b k)"), o[XC:XC + XR // 2, :])
                elif u == 18:
                    last = copy(vx[:, :, :].rearrange("p b k -> p (b k)"), o[:, :])
                elif u < 23:
                    act.wait_ge(s_flag, 1)
                    last = copy(wvo[:, 2 * (u - 19):2 * (u - 19) + 2, :].rearrange("p h e -> p (h e)"), o[:, :])
                elif u == 23:
                    last = copy(wtot[:, :], o[:, 0:3])
                else:
                    j, h = (u - 24) // 2, (u - 24) % 2
                    ob = o[:, :].bitcast(BF16)
                    if j < 2:
                        last = copy(wt[j][:, :, h * 512:(h + 1) * 512], ob.rearrange("p (c f) -> p c f", c=EC))
                    else:
                        last = copy(wt[2][:, :, h * P:(h + 1) * P], ob.rearrange("p (k e) -> p k e", k=8))
                last.then_inc(s_ue, 1)

            def sum_w(v):
                if v % 2 == 0:
                    act.wait_ge(s_w[v // 2], 16)
                if v:
                    act.wait_ge(s_wabs, v)
                nc.scalar.activation(junk_w, wn[v // 2][:, :, :].rearrange("p a b -> p (a b)")[:, v % 2 * F:(v % 2 + 1) * F], ACT.Abs,
                                     accum_out=wsum[:, v % 2, v // 2:v // 2 + 1]).then_inc(s_wabs, 1)

            def tanh_w(v):
                if v == 0:
                    act.wait_ge(s_winv, 1)
                half = wn[v // 2][:, :, :].rearrange("p a b -> p (a b)")[:, v % 2 * F:(v % 2 + 1) * F]
                nc.scalar.activation(half, half, ACT.Tanh, scale=winv[:, v // 2:v // 2 + 1]).then_inc(s_wtanh, 1)

            for k in range(3):
                act.wait_ge(s_wtp, k + 1)
                copy(wqkv_t[:, :, :].rearrange("p c o -> p (c o)")[:, 512 * k:512 * (k + 1)], bank[2 + k][:, :]).then_inc(s_wt, 1)
            act.wait_ge(s_wtp, 4)
            copy(wproj_t[:, :, :].rearrange("p c o -> p (c o)"), bank[5][:, :]).then_inc(s_wt, 1)
            for m in range(4):
                act.wait_ge(s_qkp, m + 1)
                d = (qt, kt)[m // 2][:, m % 2, :, :].rearrange("p b s -> p (b s)")
                copy(d, bank[(6, 7, 0, 1)[m]][:, :], HD ** -0.5 if m < 2 else 1.0).then_inc(s_qk, 1)
            act.wait_ge(s_zero, 2)
            for t in range(RT):
                act.wait_ge(s_vp, t + 1)
                for a in range(2):
                    src = bank[2 + t][a * SP:a * SP + S, 0:E].rearrange("p (h q d) -> p q h d", h=HH, q=2)
                    for q in range(2):
                        copy(vblk[q * SP:q * SP + S, 2 * t + a, :, q * HD:(q + 1) * HD], src[:, q, :, :]).then_inc(s_v, 1)

            def take_latent(f, x_bank, q_bank):
                act.wait_ge(s_x1tp, f + 1)
                copy(x1t[:, f, :, :].rearrange("p c n -> p (c n)"), x_bank[:, 0:2 * HN]).then_inc(s_x1t, 1)
                act.wait_ge(s_qcp, f + 1)
                copy(qct[:, f * HN:(f + 1) * HN], q_bank[0:XQ, 0:HN]).then_inc(s_qc, 1)

            for g in range(NG):
                act.wait_ge(s_sub, g + 1)
                if g >= 2:
                    act.wait_ge(s_ptp, g - 1)
                nc.scalar.activation(prob[:, g % 2, :, 0:S], srel[:, g % 2, :, :], ACT.Exp).then_inc(s_exp, 1)
                for u in range(SPREAD[g], SPREAD[g + 1]):
                    unit(u)
                for v in range(SUMS[g], SUMS[g + 1]):
                    sum_w(v)
            unit(23)
            take_latent(0, bank[4], bank[5])
            for v in range(6):
                tanh_w(v)
            act.wait_ge(s_wln, 1)
            nc.scalar.activation(wone[:, 0, :], wone[:, 1, :], ACT.Ln).then_inc(s_watan, 1)
            nc.scalar.activation(segm[:, :], mhalf[0:1, :], ACT.Exp)
            for u in range(24, 27):
                unit(u)
            take_latent(1, bank[0], bank[1])
            def square_x(t):
                act.wait_ge(s_ln, RT + t + 1)
                if t >= 1:
                    act.wait_ge(s_sq, t)
                nc.scalar.activation(junk[:, 0:E], x2[:, t, :], ACT.Square, accum_out=fs[:, t, 0:1]).then_inc(s_sq, 1)

            def take_x(t):
                act.wait_ge(s_xqp, t + 1)
                if t >= 2:
                    act.wait_ge(s_uv, 2 * (t - 1))
                copy(xqt[:, t % 2, :, :, :].rearrange("p g c s -> p (g c s)"), bank[6][:, :].bitcast(BF16)[:, 0:4 * R]).then_inc(s_xqt, 1)

            def gate(k):
                act.wait_ge(s_uv, k + 1)
                act.wait_ge(s_f, k // 2 + 1)
                if k >= 2:
                    act.wait_ge(s_h, k - 1)
                nc.scalar.activation(th[:, k % 2, :], bank[up_banks(k)[0]][0:R, :], ACT.Tanh, scale=fs[:, k // 2, 14:15]).then_inc(s_th, 1)

            def square_h(k):
                t, hf = k // 2, k % 2
                act.wait_ge(s_h, k + 1)
                if k:
                    act.wait_ge(s_hsq, k)
                nc.scalar.activation(junk[:, 512:1024], hraw[:, t % 2, hf * 512:(hf + 1) * 512], ACT.Square, accum_out=fs[:, t, 16 + hf:17 + hf]).then_inc(s_hsq, 1)

            def take_h(t):
                act.wait_ge(s_hqp, t + 1)
                if t >= 1:
                    act.wait_ge(s_y3, t)
                copy(hqt[:, :, :].rearrange("p k s -> p (k s)"), bank[2][:, :].bitcast(BF16)[:, 0:8 * R]).then_inc(s_hqt, 1)

            act.wait_ge(s_flag, 1)
            outside = act.value_load(flag[0:1, 0:1])
            with act.If(outside > 0):
                for u in range(27, UNITS):
                    unit(u)
                with act.Fori(0, B) as b:
                    with act.Fori(0, NKT) as t:
                        it = b * NKT + t
                        act.wait_ge(g_ktp, it + 1)
                        copy(g_kvt, bank[0][:, 0:E].rearrange("p (c k) -> p c k", c=EC)[:, :, 0:KT]).then_inc(g_kt, 1)
                    act.wait_ge(g_max, b + 1)
                    for p in range(XP):
                        last = nc.scalar.activation(g_sc[:, p, :], g_sc[:, p, :], ACT.Exp, bias=g_mx[:, p:p + 1], accum_out=g_sm[:, p:p + 1])
                    last.then_inc(g_exp, 1)
                    with act.Fori(0, NKT) as t:
                        it = b * NKT + t
                        act.wait_ge(g_ptp, it + 1)
                        for q in range(2):
                            last = copy(g_ptb[:, 4 * q:4 * q + 4, :].rearrange("p h k -> p (h k)"), bank[4 + q][0:KT, 0:4 * R])
                        last.then_inc(g_pt, 1)
                for t in range(RT):
                    square_x(t)
                    take_x(t)
                    for k in (2 * t, 2 * t + 1):
                        gate(k)
                        square_h(k)
                    take_h(t)
            with act.Else():
                for k in range(STEPS):
                    if ACT_TURNED <= k - 2 < KS:
                        act.wait_ge(s_xptp, k - 1)
                        act.wait_ge(s_xop, k - 3)
                        copy(xpt[:, (k - 2) % 2, :, :].rearrange("p h k -> p (h k)"), bank[0][:, 0:4 * R]).then_inc(s_xpt, 1)
                    if k < KS:
                        act.wait_ge(s_xmax, k + 1)
                        if k >= 3:
                            act.wait_ge(s_xptp, k - 2)
                        for i in range(4):
                            last = nc.scalar.activation(xprob[:, k % 3, i, :], bank[4 + k % 2][0:R, i * WIN:(i + 1) * WIN], ACT.Exp,
                                                        bias=xmax[:, k % 3, i:i + 1], accum_out=xsum[:, k % 3, i:i + 1])
                        last.then_inc(s_xexp, 1)
                    for u in late_units(k):
                        unit(u)
                    if k % 2 == 0 and 0 <= k - 4 <= 2 * (B - 1):
                        b = (k - 4) // 2
                        act.wait_ge(s_xop, 2 * b + 2)
                        if b == 0:
                            act.wait_ge(s_xptp, 1)
                        copy(ctxt[:, :, b * S:(b + 1) * S], bank[2][:, 0:N].rearrange("p (h s) -> p h s", h=XP)).then_inc(s_xo, 1)
                    for t in tile(k, ACT_SQX):
                        square_x(t)
                    for t in tile(k, ACT_XT):
                        take_x(t)
                    for t in tile(k, ACT_TAKE_H):
                        take_h(t)
                    for t in tile(k, ACT_GATE0):
                        gate(2 * t)
                    for t in tile(k, ACT_GATE1):
                        gate(2 * t + 1)
                    for t in tile(k, ACT_SQ0):
                        square_h(2 * t)
                    for t in tile(k, ACT_SQ1):
                        square_h(2 * t + 1)

        @block.vector
        def _(v):
            steps = [0]

            def mark(ins):
                steps[0] += 1
                ins.then_inc(s_dve, 1)
                return steps[0]

            def after(n):
                v.wait_ge(s_dve, n)

            def link(ins):
                after(mark(ins))

            def turned_prob(g):
                v.wait_ge(s_ptp, g + 1)
                if g >= 2:
                    v.wait_ge(s_av, g - 1)
                nc.vector.tensor_copy(probt[:, g % 2, :, :].rearrange("p h k -> p (h k)"), bank[g % 2][:, :]).then_inc(s_pt, 1)

            def row_stats(n, t, r):
                link(nc.vector.bn_stats(stats[:, :], r))
                link(nc.vector.bn_aggr(mv[:, n, t, :], stats[:, :]))
                nc.vector.tensor_scalar(veps[:, n, t:t + 1], mv[:, n, t, 1:2], LN_EPS, None, ALU.add).then_inc(s_var[n], 1)

            def normal(n, t, r, dst, done):
                v.wait_ge(s_rstd[n], t + 1)
                nc.vector.tensor_scalar(dst, r, mv[:, n, t, 0:1], rstd[:, n, t:t + 1], ALU.subtract, ALU.mult).then_inc(done, 1)

            v.wait_ge(s_zero, 3)
            for c in range(EC):
                v.wait_ge(s_xtp, c + 1)
                nc.vector.tensor_copy(xt[:, c, :, 0:S], bank[c][:, 0:N].rearrange("p (b s) -> p b s", b=B)).then_inc(s_xt, 1)
            for c in range(2):
                v.wait_ge(s_qk, 3 + c)
                for h in range(HH):
                    last = nc.vector.tensor_scalar(kblk[:, :, c, :, h, :], kt[:, c, :, 0:S].rearrange("p (t b) s -> p t b s", t=RT), cst[:, HMASK + h:HMASK + h + 1], None, ALU.mult)
                last.then_inc(s_kblk, 1)

            def soft(g):
                v.wait_ge(s_sc, g + 1)
                s = bank[6 + g % 2][:, 0:HH * S].rearrange("p (h s) -> p h s", h=HH)
                link(nc.vector.tensor_reduce(smax[:, g % 2, :], s, AXX, ALU.max))
                if g >= 2:
                    v.wait_ge(s_exp, g - 1)
                nc.vector.tensor_tensor(srel[:, g % 2, :, :], s, smax[:, g % 2, :].unsqueeze(2).broadcast_to([P, HH, S]), ALU.subtract).then_inc(s_sub, 1)

            def normalise(t):
                v.wait_ge(s_av, 2 * t + 2)
                o = bank[2][:, 0:HH * VW].rearrange("p (h w) -> p h w", h=HH)
                link(nc.vector.reciprocal(orec[:, :, :], o[:, :, 2 * HD:VW]))
                if t >= 2:
                    v.wait_ge(s_atp, t - 1)
                nc.vector.tensor_tensor(attn[:, t % 2, :, :].rearrange("p (h q) d -> p h q d", q=2), o[:, :, 0:2 * HD].rearrange("p h (q d) -> p h q d", q=2),
                                        orec[:, :, :].unsqueeze(3).broadcast_to([P, HH, 2, HD]), ALU.mult).then_inc(s_attn, 1)

            def attn_turned(t):
                v.wait_ge(s_atp, t + 1)
                nc.vector.tensor_copy(attnt[:, :, t * R:(t + 1) * R].rearrange("p c (a s) -> p c a s", a=2),
                                      bank[3][:, 0:E].rearrange("p (c a s) -> p c a s", c=EC, a=2)[:, :, :, 0:S]).then_inc(s_at, 1)

            def add1(t):
                v.wait_ge(s_y, t + 1)
                nc.vector.tensor_tensor(res[:, t % 2, :], bank[3][0:R, E:2 * E], xn[:, t, :], ALU.add).then_inc(s_res, 1)
                v.wait_ge(s_res, t + 1)
                row_stats(0, t, res[:, t % 2, :])

            def norm1(t):
                normal(0, t, res[:, t % 2, :], x1[:, t, :], s_ln)

            qcos = cst[:, C_QC:C_QC + S].unsqueeze(1).unsqueeze(1).broadcast_to([P, 2, BH, S])
            qsin = cst[:, C_QS:C_QS + S].unsqueeze(1).unsqueeze(1).broadcast_to([P, 2, BH, S])

            def query(i):
                f, pp, kind = i // QI, i % QI // 3, i % 3
                v.wait_ge(s_qp, i + 1)
                o = bank[query_bank(i)][:, 0:2 * HN].rearrange("p (j b s) -> p j b s", j=2, b=BH)
                if kind == 0:
                    n = i // 3
                    if n >= 2:
                        v.wait_ge(s_qf, n - 1)
                    for q in range(2):
                        rows = slice(q * XR, (q + 1) * XR)
                        last = nc.vector.tensor_tensor(t2[XR:P, n % 2, :, :, q, :], o[rows, :, :, :], qsin[rows, :, :, :], ALU.mult)
                else:
                    last = nc.vector.tensor_tensor(qf[:, f, 2 * pp + kind - 1, :, :, :].rearrange("p b q s -> p q b s"), o, qcos, ALU.mult)
                last.then_inc(s_qi, 1)

            def round_w(h):
                if h == 0:
                    v.wait_ge(s_krope, 1)
                if h >= 2:
                    v.wait_ge(s_up, 24 + h - 1)
                v.wait_ge(s_wtanh, h + 1)
                nc.vector.tensor_scalar(wrnd[:, h % 2, :], wn[h // 2][:, :, :].rearrange("p a b -> p (a b)")[:, h % 2 * F:(h % 2 + 1) * F],
                                        MAGIC, MAGIC, ALU.add, ALU.subtract).then_inc(s_wrnd, 1)

            soft(0)
            for g in range(NG):
                if g + 1 < NG:
                    soft(g + 1)
                turned_prob(g)
                if g >= 5 and g % 2 == 1:
                    norm1((g - 5) // 2)
                if g >= 3 and g % 2 == 1:
                    normalise((g - 3) // 2)
                if g >= 4 and g % 2 == 0:
                    add1((g - 4) // 2)
                if g >= 3 and g % 2 == 1:
                    attn_turned((g - 3) // 2)
                if g == 2:
                    v.wait_ge(s_seg, 48)
                    link(nc.vector.tensor_scalar(segc[:, :], segr[:, :], -(WIN - 1) / 2.0, None, ALU.add))
                    link(nc.vector.tensor_tensor(segc[:, :], segc[:, :], segc[:, :], ALU.mult))
                    link(nc.vector.tensor_reduce(segm[:, :], segc[:, :], AXX, ALU.max))
                    nc.vector.tensor_scalar(flag[:, :], segm[:, :], (WIN / 2.0) ** 2 - WIN / 4.0, None, ALU.is_gt).then_inc(s_flag, 1)
            v.wait_ge(s_ue, 24)
            link(nc.vector.tensor_scalar(wmean[:, :], wtot[:, :], 1.0 / (F * E), None, ALU.mult))
            link(nc.vector.tensor_scalar(weps[:, :], wmean[:, :], RMS_EPS, None, ALU.add))
            nc.vector.reciprocal(winv[:, :], weps[:, :]).then_inc(s_winv, 1)
            link(nc.vector.tensor_scalar(wone[:, 0, :], wmean[:, :], -1.0, 1.0, ALU.mult, ALU.add))
            link(nc.vector.reciprocal(wone[:, 0, :], wone[:, 0, :]))
            link(nc.vector.tensor_scalar(wone[:, 1, :], wmean[:, :], 1.0, None, ALU.add))
            nc.vector.tensor_tensor(wone[:, 1, :], wone[:, 1, :], wone[:, 0, :], ALU.mult).then_inc(s_wln, 1)
            normalise(RT - 1)
            for i in range(QI):
                query(i)
                if i == 0:
                    add1(RT - 2)
                if i == 1:
                    attn_turned(RT - 1)
                if i == 2:
                    norm1(RT - 2)
                if i == 3:
                    add1(RT - 1)
                if i == 6:
                    norm1(RT - 1)
                for h in FFN_HALVES.get(i + 1, ()):
                    round_w(h)

            def add2(t):
                v.wait_ge(s_xy, t + 1)
                nc.vector.tensor_tensor(res[:, t % 2, :], bank[7][0:R, 0:E], x1[:, t, :], ALU.add).then_inc(s_xres, 1)
                v.wait_ge(s_xres, t + 1)
                row_stats(1, t, res[:, t % 2, :])

            def norm2(t):
                normal(1, t, res[:, t % 2, :], x2[:, t, :], s_ln)

            def scale_x(t):
                f = fs[:, t, :]
                v.wait_ge(s_gx, t + 1)
                nc.vector.tensor_reduce(f[:, 2:4], xg[:, :, :], AXX, ALU.max, apply_absolute_value=True).then_inc(s_xg, 1)

            def quant_x(t):
                f = fs[:, t, :]
                if t == 0:
                    v.wait_ge(s_watan, 1)
                    link(nc.vector.tensor_scalar(watan[:, :], wone[:, 0, :], 0.5, None, ALU.mult))
                v.wait_ge(s_xg, t + 1)
                v.wait_ge(s_rr, t + 1)
                link(nc.vector.tensor_scalar(f[:, 4:6], f[:, 2:4], f[:, 1:2], 1e-4, ALU.mult, ALU.max))
                inverse = mark(nc.vector.reciprocal(f[:, 6:8], f[:, 4:6]))
                worth = mark(nc.vector.scalar_tensor_tensor(f[:, 10:12], f[:, 4:6], 1.0 / 127.0, watan[0:R, 0:2], ALU.mult, ALU.mult))
                after(inverse)
                factor = mark(nc.vector.tensor_scalar(f[:, 8:10], f[:, 6:8], f[:, 1:2], 127.0, ALU.mult, ALU.mult))
                after(worth)
                nc.vector.tensor_scalar(f[:, 14:15], f[:, 10:11], 0.5, None, ALU.mult).then_inc(s_f, 1)
                after(factor)
                for g in range(2):
                    scaled = mark(nc.vector.tensor_scalar(xg[:, g, :], xg[:, g, :], f[:, 8 + g:9 + g], MAGIC, ALU.mult, ALU.add))
                mark(nc.vector.scalar_tensor_tensor(f[:, 15:16], f[:, 10:11], 0.5, f[:, 11:12], ALU.mult, ALU.mult))
                after(scaled)
                if t >= 2:
                    v.wait_ge(s_xqp, t - 1)
                nc.vector.tensor_scalar(xq[:, t % 2, :, :], xg[:, :, :], MAGIC, None, ALU.subtract).then_inc(s_xq, 1)

            def hidden(k):
                t, hf = k // 2, k % 2
                v.wait_ge(s_th, k + 1)
                if t >= 2:
                    v.wait_ge(s_hg, 2 * (t - 1))
                    v.wait_ge(s_hsq, 2 * (t - 1))
                u, w = (bank[i] for i in up_banks(k))
                link(nc.vector.scalar_tensor_tensor(th[:, k % 2, :], th[:, k % 2, :], 1.0, u[0:R, :], ALU.add, ALU.mult))
                nc.vector.tensor_tensor(hraw[:, t % 2, hf * 512:(hf + 1) * 512], th[:, k % 2, :], w[0:R, :], ALU.mult).then_inc(s_h, 1)

            def max_h(t):
                f = fs[:, t, :]
                v.wait_ge(s_hsq, 2 * t + 2)
                mark(nc.vector.tensor_tensor(f[:, 20:21], f[:, 15:16], f[:, 15:16], ALU.mult))
                link(nc.vector.tensor_tensor(f[:, 19:20], f[:, 16:17], f[:, 17:18], ALU.add))
                link(nc.vector.scalar_tensor_tensor(f[:, 19:20], f[:, 19:20], 1.0 / F, f[:, 20:21], ALU.mult, ALU.mult))
                nc.vector.tensor_scalar(f[:, 21:22], f[:, 19:20], RMS_EPS, None, ALU.add).then_inc(s_ms, 1)

            def largest(k):
                t, hf = k // 2, k % 2
                v.wait_ge(s_hg, k + 1)
                row = hg[:, t % 2, :, :].rearrange("p h n -> p (h n)")
                if hf:
                    link(nc.vector.tensor_reduce(fs[:, t, 18:19], row[:, 512:1025], AXX, ALU.max, apply_absolute_value=True))
                else:
                    link(nc.vector.tensor_reduce(row[:, 512:513], row[:, 0:512], AXX, ALU.max, apply_absolute_value=True))

            def quant_h(t):
                f = fs[:, t, :]
                v.wait_ge(s_rr3, t + 1)
                link(nc.vector.tensor_tensor(f[:, 23:24], f[:, 22:23], f[:, 15:16], ALU.mult))
                link(nc.vector.tensor_scalar(f[:, 24:25], f[:, 18:19], f[:, 23:24], 1e-4, ALU.mult, ALU.max))
                inverse = mark(nc.vector.reciprocal(f[:, 25:26], f[:, 24:25]))
                mark(nc.vector.scalar_tensor_tensor(f[:, 27:28], f[:, 24:25], 1.0 / 127.0, watan[0:R, 2:3], ALU.mult, ALU.mult))
                after(inverse)
                link(nc.vector.tensor_scalar(f[:, 26:27], f[:, 25:26], f[:, 23:24], 127.0, ALU.mult, ALU.mult))
                h = [hg[:, t % 2, a, 0:512] for a in range(2)]
                scaled = [mark(nc.vector.tensor_scalar(h[a], h[a], f[:, 26:27], MAGIC, ALU.mult, ALU.add)) for a in range(2)]
                if t >= 2:
                    v.wait_ge(s_hqp, t - 1)
                for a in range(2):
                    after(scaled[a])
                    nc.vector.tensor_scalar(hq[:, t % 2, a * 512:(a + 1) * 512], h[a], MAGIC, None, ALU.subtract).then_inc(s_hq, 1)

            def add3(t):
                v.wait_ge(s_y3, t + 1)
                nc.vector.scalar_tensor_tensor(r3[:, t % 2, :], bank[0][0:R, 0:E], fs[:, t, 27:28], x2[:, t, :], ALU.mult, ALU.add).then_inc(s_r3, 1)
                v.wait_ge(s_r3, t + 1)
                row_stats(2, t, r3[:, t % 2, :])

            def norm3(t):
                if t >= 2:
                    v.wait_ge(s_out[t % 2], 16 * (t // 2))
                normal(2, t, r3[:, t % 2, :], yout[:, t % 2, :], s_yo)

            outside_before = steps[0]
            outside = v.value_load(flag[0:1, 0:1])
            with v.If(outside > 0):
                for i in range(QI, 2 * QI):
                    query(i)
                for u in range(27, UNITS):
                    round_w(u - 24)
                v.wait_ge(g_io, 16)
                v.wait_ge(s_qf, XP)
                v.wait_ge(s_segf, 1)
                v.wait_ge(s_krope, 1)
                v.wait_ge(s_ue, UNITS)
                nc.vector.memset(g_acc_b, 0.0).then_inc(g_sp, 1)
                with v.Fori(0, 2) as f, v.Fori(0, BH) as c:
                    b = f * BH + c
                    nc.vector.tensor_copy(g_qb, big[:, :].rearrange("p (f h n) -> p f h n", f=2, h=XP)[:, bass.ds(f, 1), :, bass.ds(c * R, R)].rearrange("p f h n -> p (f h) n")).then_inc(g_q, 1)
                    nc.vector.tensor_scalar(g_msk, g_iota, segf[:, bass.ds(b, 1)], None, ALU.subtract).then_inc(g_mask, 1)
                    v.wait_ge(g_mask, 3 * b + 1)
                    nc.vector.tensor_tensor(g_msk, g_msk, g_msk, ALU.mult).then_inc(g_mask, 1)
                    v.wait_ge(g_mask, 3 * b + 2)
                    nc.vector.tensor_scalar(g_msk, g_msk, LOOKBACK ** 2 / 4.0, NEG, ALU.is_gt, ALU.mult).then_inc(g_mask, 1)
                    with v.Fori(0, NKT) as t:
                        it = b * NKT + t
                        v.wait_ge(g_kp, it + 1)
                        v.wait_ge(g_tab, 32 * it + 32)
                        nc.vector.tensor_tensor(g_key, bank[1][:, 0:KT], g_cos, ALU.mult).then_inc(g_k1, 1)
                        nc.vector.tensor_tensor(g_key2, bank[1][:, P:P + KT], g_sin, ALU.mult).then_inc(g_k2, 1)
                        nc.vector.tensor_copy(g_v[:, bass.ds(t, 1), :], bank[1][0:KT, 2 * P:2 * P + XC].unsqueeze(1))
                        v.wait_ge(g_k1, it + 1)
                        v.wait_ge(g_k2, it + 1)
                        nc.vector.tensor_tensor(g_key, g_key, g_key2, ALU.add).then_inc(g_k, 1)
                        v.wait_ge(g_s, it + 1)
                        v.wait_ge(g_mask, 3 * b + 3)
                        for q in range(2):
                            last = nc.vector.tensor_tensor(g_sc[:, 4 * q:4 * q + 4, bass.ds(t * KT, KT)], bank[2 + q][0:R, 0:4 * KT].rearrange("p (h k) -> p h k", h=4),
                                                    g_msk[:, bass.ds(t * KT, KT)].unsqueeze(1).broadcast_to([R, 4, KT]), ALU.add)
                        last.then_inc(g_sp, 1)
                    v.wait_ge(g_sp, NKT * b + NKT + 1)
                    nc.vector.tensor_reduce(g_mx, g_sc, AXX, ALU.max, negate=True).then_inc(g_max, 1)
                    v.wait_ge(g_exp, b + 1)
                    nc.vector.reciprocal(g_rc, g_sm).then_inc(g_rec, 1)
                    v.wait_ge(g_rec, b + 1)
                    nc.vector.tensor_tensor(g_sc, g_sc, g_rc.unsqueeze(2).broadcast_to([R, XP, LK]), ALU.mult).then_inc(g_norm, 1)
                    v.wait_ge(g_norm, b + 1)
                    nc.vector.memset(g_acc_b, 0.0).then_inc(g_acc, 1)
                    with v.Fori(0, NKT) as t:
                        it = b * NKT + t
                        nc.vector.tensor_copy(g_vk, g_v[:, bass.ds(t, 1), :].rearrange("p a c -> p (a c)"))
                        nc.vector.tensor_copy(g_pk_b, g_sc[:, :, bass.ds(t * KT, KT)]).then_inc(g_pk, 1)
                        v.wait_ge(g_op, it + 1)
                        v.wait_ge(g_acc, it + b + 1)
                        nc.vector.tensor_tensor(g_acc_b, g_acc_b, bank[6][:, 0:N].rearrange("p (h s) -> p h s", h=XP), ALU.add).then_inc(g_acc, 1)
                    v.wait_ge(g_acc, (NKT + 1) * b + NKT + 1)
                    nc.vector.tensor_copy(ctxt[:, :, bass.ds(b * S, S)], g_acc_b).then_inc(s_xo, 1)
                for t in range(RT):
                    add2(t)
                    norm2(t)
                    scale_x(t)
                    quant_x(t)
                    hidden(2 * t)
                    hidden(2 * t + 1)
                    max_h(t)
                    largest(2 * t)
                    largest(2 * t + 1)
                    quant_h(t)
                    add3(t)
                    norm3(t)
            steps[0] = outside_before
            with v.Else():
                def xmaxima(k):
                    v.wait_ge(s_xs, k + 1)
                    if k >= 3:
                        v.wait_ge(s_xexp, k - 2)
                    nc.vector.tensor_reduce(xmax[:, k % 3, :], bank[4 + k % 2][0:R, :].rearrange("p (h k) -> p h k", h=4), AXX, ALU.max, negate=True).then_inc(s_xmax, 1)

                def xrecip(k):
                    v.wait_ge(s_xexp, k + 1)
                    if k >= 3:
                        v.wait_ge(s_xnorm, k - 2)
                    nc.vector.reciprocal(xrec[:, k % 3, :], xsum[:, k % 3, :]).then_inc(s_xrec, 1)

                def xturned(k):
                    v.wait_ge(s_xptp, k + 1)
                    if k >= 2:
                        v.wait_ge(s_xop, k - 1)
                    nc.vector.tensor_copy(xpt[:, k % 2, :, :].rearrange("p h k -> p (h k)"), bank[0][:, 0:4 * R]).then_inc(s_xpt, 1)

                for k in range(STEPS):
                    if k < KS:
                        xmaxima(k)
                    if 0 <= k - 2 < ACT_TURNED:
                        xturned(k - 2)
                    if 0 <= k - 1 < KS:
                        xrecip(k - 1)
                    for i in late_queries(k):
                        query(i)
                    for u in late_units(k + 1):
                        round_w(u - 24)
                    for t in tile(k, DVE_NORM3):
                        norm3(t)
                    for t in tile(k, DVE_ADD3):
                        add3(t)
                    for t in tile(k, DVE_H0):
                        hidden(2 * t)
                    for t in tile(k, DVE_H1):
                        hidden(2 * t + 1)
                    for t in tile(k, DVE_L0):
                        largest(2 * t)
                    for t in tile(k, DVE_MH):
                        max_h(t)
                        largest(2 * t + 1)
                    for t in tile(k, DVE_NORM2):
                        norm2(t)
                    for t in tile(k, DVE_ADD2):
                        add2(t)
                    for t in tile(k, DVE_QX):
                        scale_x(t)
                        quant_x(t)
                    for t in tile(k, DVE_QH):
                        quant_h(t)

        @block.gpsimd
        def _(g):
            g.memset(wk2[:, :, 0:XC], 0.0).then_inc(s_zero, 1)
            g.memset(vblk[:, :, :, :], 0.0).then_inc(s_pool, 1)
            g.wait_ge(s_pool, 1)
            g.memset(vblk[0:SP, :, :, 2 * HD:2 * HD + 1], 1.0).then_inc(s_pool, 1)
            g.memset(vblk[SP:P, :, :, 2 * HD + 1:VW], 1.0).then_inc(s_pool, 1)
            g.wait_ge(s_pool, 3)
            g.memset(prob[:, :, :, S:SP], 0.0).then_inc(s_zero, 1)
            g.memset(xt[:, :, :, :], 0.0).then_inc(s_zero, 1)
            g.memset(mhalf[:, :], -0.5).then_inc(s_pool, 1)
            g.memset(ones[:, :], 1.0).then_inc(s_ones, 1)
            g.wait_ge(s_cst, 16)
            g.tensor_copy(identb[:, :], ident).then_inc(s_idb, 1)
            g.tensor_copy(causal[:, :], cst[0:SP, C_CB:C_CB + S]).then_inc(s_idb, 1)
            for a in range(2):
                g.tensor_copy(identq[:, a * SP:(a + 1) * SP], cst[0:SP, 0:SP]).then_inc(s_idb, 1)
            g.tensor_copy(identd[:, 0:S], cst[0:S, 0:S]).then_inc(s_idb, 1)
            g.tensor_copy(identd[:, S:R], cst[0:S, 0:S]).then_inc(s_idb, 1)
            g.wait_ge(s_wqr, 16)
            g.tensor_copy(wqa[:, :, XC:P], wqr_n[:, :, :]).then_inc(s_qr, 1)
            g.tensor_copy(wqs[:, :, 0:XR // 2], wqr_n[:, :, XR // 2:XR])
            g.tensor_copy(wqs[:, :, XR // 2:XR], wqr_n[:, :, 0:XR // 2]).then_inc(s_qr, 1)
            g.wait_ge(s_seg, 48)
            g.tensor_copy(segf[:, :], segi[:, :]).then_inc(s_segf, 1)
            g.wait_ge(s_segf, 1)
            g.tensor_tensor(dist[:, :, :], cst[0:S, C_IO:C_IO + WIN].unsqueeze(1).broadcast_to([S, B, WIN]),
                            segf[0:S, :].unsqueeze(2).broadcast_to([S, B, WIN]), ALU.subtract).then_inc(s_pool, 1)
            g.wait_ge(s_pool, 5)
            g.tensor_tensor(dist[:, :, :], dist[:, :, :], dist[:, :, :], ALU.mult).then_inc(s_pool, 1)
            g.wait_ge(s_pool, 6)
            g.tensor_scalar(xmask[:, :, :], dist[:, :, :], LOOKBACK ** 2 / 4.0, NEG, ALU.is_gt, ALU.mult).then_inc(s_mask, 1)

            def root(n, t):
                g.wait_ge(s_var[n], t + 1)
                g.tensor_tensor(rstd[:, n, t:t + 1], veps[:, n, t:t + 1], mhalf[:, :], ALU.pow).then_inc(s_rstd[n], 1)

            root(0, 0)
            g.wait_ge(s_rstd[0], 1)
            g.wait_ge(s_ue, 18)
            kc = cst[XC:P, C_KC:C_KC + WIN].unsqueeze(1).broadcast_to([XR, B, WIN])
            ks = cst[XC:P, C_KS:C_KS + WIN].unsqueeze(1).broadcast_to([XR, B, WIN])
            g.tensor_tensor(ka[XC:P, :, :], ka[XC:P, :, :], kc, ALU.mult).then_inc(s_pool, 1)
            g.tensor_tensor(kb[XC:P, :, :], kb[XC:P, :, :], ks, ALU.mult).then_inc(s_pool, 1)
            g.wait_ge(s_pool, 8)
            g.tensor_tensor(ka[XC:P, :, :], ka[XC:P, :, :], kb[XC:P, :, :], ALU.add).then_inc(s_krope, 1)
            g.wait_ge(s_krope, 1)
            root(0, 1)
            root(0, 2)
            g.wait_ge(s_rstd[0], RT - 1)
            def add_rope(n):
                g.wait_ge(s_qi, 3 * n + 3)
                rope = qf[XR:P, n // 4, 2 * (n % 4):2 * (n % 4) + 2, :, :, :].rearrange("p h b q s -> p (h b q s)")
                g.tensor_tensor(rope, rope, t2[XR:P, n % 2, :, :, :, :].rearrange("p h b q s -> p (h b q s)"), ALU.add).then_inc(s_qf, 1)

            add_rope(0)
            g.wait_ge(s_qf, 1)
            root(0, 3)
            g.wait_ge(s_rstd[0], RT)
            for n in range(1, QI // 3):
                add_rope(n)

            def gain_x(t):
                if t == 0:
                    g.wait_ge(s_g, 48)
                else:
                    g.wait_ge(s_xq, t)
                g.wait_ge(s_ln, RT + t + 1)
                g.tensor_tensor(xg[:, :, :], x2[:, t, :].unsqueeze(1).broadcast_to([R, 2, E]), g12[:, :, :], ALU.mult).then_inc(s_gx, 1)

            def rms_x(t):
                f = fs[:, t, :]
                g.wait_ge(s_sq, t + 1)
                g.tensor_scalar(f[:, 12:13], f[:, 0:1], 1.0 / E, RMS_EPS, ALU.mult, ALU.add).then_inc(s_pool, 1)
                g.wait_ge(s_pool, 9 + t)
                g.tensor_tensor(f[:, 1:2], f[:, 12:13], mhalf[:, :], ALU.pow).then_inc(s_rr, 1)

            def gain_h(k):
                t, cols = k // 2, slice((k % 2) * 512, (k % 2 + 1) * 512)
                g.wait_ge(s_h, k + 1)
                if t == 0:
                    g.wait_ge(s_g, 48)
                if t >= 2:
                    g.wait_ge(s_hq, 2 * (t - 1))
                g.tensor_tensor(hg[:, t % 2, k % 2, 0:512], hraw[:, t % 2, cols], g3b[:, cols], ALU.mult).then_inc(s_hg, 1)

            def root_h(t):
                g.wait_ge(s_ms, t + 1)
                g.tensor_tensor(fs[:, t, 22:23], fs[:, t, 21:22], mhalf[:, :], ALU.pow).then_inc(s_rr3, 1)

            g.wait_ge(s_flag, 1)
            outside = g.value_load(flag[0:1, 0:1])
            with g.If(outside > 0):
                for n in range(QI // 3, XP):
                    add_rope(n)
                g.wait_ge(s_qf, XP)
                for t in range(RT):
                    root(1, t)
                    gain_x(t)
                    rms_x(t)
                    gain_h(2 * t)
                    gain_h(2 * t + 1)
                    root_h(t)
                    root(2, t)
            with g.Else():
                for k in range(STEPS):
                    if 0 <= k - 1 < KS:
                        if k - 1 == 0:
                            g.wait_ge(s_qf, QI // 3)
                        elif done_ropes(k) > done_ropes(k - 1):
                            g.wait_ge(s_qf, done_ropes(k))
                        g.wait_ge(s_xrec, k)
                        g.tensor_tensor(xprob[:, (k - 1) % 3, :, :], xprob[:, (k - 1) % 3, :, :], xrec[:, (k - 1) % 3, :].unsqueeze(2).broadcast_to([R, 4, WIN]), ALU.mult).then_inc(s_xnorm, 1)
                    for n in range(done_ropes(k), done_ropes(k + 1)):
                        if k:
                            g.wait_ge(s_xnorm, k)
                        add_rope(n)
                    for t in tile(k, DVE_ADD3):
                        root(2, t)
                    for t in tile(k, DVE_H0):
                        gain_h(2 * t)
                    for t in tile(k, DVE_H1):
                        gain_h(2 * t + 1)
                    for t in tile(k, DVE_MH):
                        root_h(t)
                    for t in tile(k, DVE_ADD2):
                        root(1, t)
                    for t in tile(k, DVE_NORM2):
                        gain_x(t)
                        rms_x(t)


KS = 2 * B
PE_OUT = (8, 11, 15, 19)
DVE_ADD2 = (9, 12, 16, 19)
DVE_NORM2 = (10, 13, 17, 20)
ACT_SQX = (10, 13, 17, 20)
DVE_QX = (11, 14, 18, 21)
PE_TURN_X = (11, 15, 19, 22)
ACT_XT = (11, 15, 19, 22)
PE_UP0 = (12, 16, 20, 23)
ACT_GATE0 = (12, 16, 20, 22)
DVE_H0 = (13, 17, 21, 24)
PE_UP1 = (14, 16, 20, 23)
ACT_GATE1 = (14, 16, 20, 23)
DVE_H1 = (15, 17, 21, 24)
DVE_L0 = (15, 17, 21, 24)
ACT_SQ0 = (14, 17, 21, 24)
ACT_SQ1 = (15, 17, 21, 24)
DVE_MH = (16, 18, 22, 25)
DVE_QH = (17, 18, 22, 25)
PE_TURN_H = (18, 19, 22, 25)
ACT_TAKE_H = (18, 19, 22, 25)
PE_DOWN = (19, 20, 23, 26)
DVE_ADD3 = (19, 20, 23, 26)
DVE_NORM3 = (20, 21, 24, 27)
STEPS = DVE_NORM3[-1] + 1
ACT_TURNED = 6
FFN_HALVES = {6: (0,), 8: (1,), 10: (2,)}
QLATE = [0, 2, 4, 6, 8, 10, 12]
LATE_UNITS = 6


def unit_bank(u):
    return 4 + u % 2 if u < 23 else 6 if u == 23 else 2 + u % 2 if u < 27 else (1, 3)[u % 2]


def query_bank(i):
    return 4 + i % 2 if i < QI else (1, 3)[i % 2]


def late_queries(k):
    return range(QI + QLATE[min(k, len(QLATE) - 1)], QI + QLATE[min(k + 1, len(QLATE) - 1)])


def done_ropes(k):
    return (QI + QLATE[min(k, len(QLATE) - 1)]) // 3


def late_units(k):
    return [27 + k - LATE_UNITS] if 0 <= k - LATE_UNITS < UNITS - 27 else []


def tile(k, stage):
    return [t for t in range(RT) if stage[t] == k]


def up_banks(k):
    return (4, 5) if k % 2 and k > 1 else (1, 3)


UNITS = 30
SPREAD = [0, 4, 8, 12, 15, 17, 19, 21, 23]
SUMS = [0, 0, 0, 0, 2, 4, 5, 6, 6]


def kernel(x, ctx_2048, itok_BxS_0_1023, L0_attn_Wqkv, L0_attn_Wproj, L0_xattn_W_kvc, L0_xattn_W_dq, L0_xattn_W_uq,
           L0_xattn_W_qr, L0_xattn_W_uk, L0_xattn_W_kr, L0_xattn_W_uv, L0_xattn_W_o, L0_ffn_w1, L0_ffn_g1, L0_ffn_w2,
           L0_ffn_g2, L0_ffn_w3, L0_ffn_g3):
    import concourse.bacc as bacc
    from concourse.bass_utils import run_bass_kernel_spmd

    nc = bacc.Bacc("TRN2", target_bir_lowering=False, num_devices=1)
    c, kc, ks, io = constants()
    named = {
        "x": np.ascontiguousarray(x).reshape(N, E), "ctx_kv": ctx_2048, "seg": itok_BxS_0_1023, "wqkv": L0_attn_Wqkv,
        "wproj": L0_attn_Wproj, "w_kvc": L0_xattn_W_kvc, "w_dq": L0_xattn_W_dq, "w_uq": L0_xattn_W_uq,
        "w_qr": L0_xattn_W_qr, "w_uk": L0_xattn_W_uk, "w_kr": L0_xattn_W_kr, "w_uv": L0_xattn_W_uv, "w_o": L0_xattn_W_o,
        "w1": L0_ffn_w1, "g1": L0_ffn_g1, "w2": L0_ffn_w2, "g2": L0_ffn_g2, "w3": L0_ffn_w3, "g3": L0_ffn_g3,
        "const": c, "kcos": kc, "ksin": ks, "kiota": io,
    }
    arrays, args = {}, []
    for name, a in named.items():
        a = np.ascontiguousarray(a)
        arrays[f"in_{name}"] = a
        args.append(nc.dram_tensor(f"in_{name}", a.shape, mybir.dt.from_np(a.dtype), kind="ExternalInput").ap())
    args.append(nc.dram_tensor("out_y", (N, E), F32, kind="ExternalOutput").ap())
    decoder(nc, *args)
    r = run_bass_kernel_spmd(nc, [arrays], core_ids=[0])
    return r.results[0]["out_y"].reshape(B, S, E)
```
